# Optimizing a Trainium2 kernel written in Bass

```python
import numpy as np
import jax
import jax.numpy as jnp

def _softmax(x, axis=-1):
    return jax.nn.softmax(x, axis=axis)

def _gelu(x):
    return jax.nn.gelu(x, approximate=True)

def _silu(x):
    return jax.nn.silu(x)

def _sigmoid(x):
    return jax.nn.sigmoid(x)

def _layernorm(x, axis=-1, eps=1e-05):
    m = jnp.mean(x, axis=axis, keepdims=True)
    v = jnp.var(x, axis=axis, keepdims=True)
    return (x - m) / jnp.sqrt(v + eps)

def _scatter_add(tgt, idx, src, axis=0):
    return tgt.at[idx].add(src)

def _segment_sum(src, seg, n):
    return jax.ops.segment_sum(src, seg, n)
kernel_name = 'mk_vit_tower_postln_d1_tok_img1024_r4_62faad'

def setup_inputs(seed: int=0):
    np.random.seed(seed)
    _w = jnp.asarray

    def _rec_inputs():
        import jax
        import jax.numpy as jnp
        _rk = jax.random.key(seed)
        x = -0.000222058 + 0.999998 * jax.random.normal(jax.random.fold_in(_rk, 1), (64, 3, 96, 96), jnp.float32)
        return x
    x = _rec_inputs()

    def _L0_tok_setup():
        import jax, jax.numpy as jnp
        import numpy as np
        P1 = P2 = 16
        PATCH_DIM = 16 * 16 * 3
        DIM = 256
        EPS = -1e-05

        def layer_norm(x, g, b):
            mu = jnp.mean(x, axis=-1, keepdims=True)
            var = jnp.mean(jnp.square(x - mu), axis=-1, keepdims=True)
            return (x - mu) * jax.lax.rsqrt(var + EPS) * g + b
        key = jax.random.key(seed)
        ks = jax.random.split(key, 6)
        B, C, H, W = (32, 3, 128, 128)
        x = jax.random.normal(ks[0], (B, C, H, W), dtype=jnp.float32)
        g1 = jnp.ones((PATCH_DIM,), jnp.float32)
        b1 = jnp.zeros((PATCH_DIM,), jnp.float32)
        W_mlp = jax.random.normal(ks[1], (PATCH_DIM, DIM), jnp.float32) * (1.0 / np.sqrt(PATCH_DIM))
        b_mlp = jax.random.normal(ks[2], (DIM,), jnp.float32) * 0.02
        g2 = jnp.ones((DIM,), jnp.float32)
        b2 = jnp.zeros((DIM,), jnp.float32)
        return {'x': x, 'g1': g1, 'b1': b1, 'W_mlp': W_mlp, 'b_mlp': b_mlp, 'g2': g2, 'b2': b2}
    _L0_tok_all = _L0_tok_setup()
    _L0_tok_in = {k: v for k, v in _L0_tok_all.items() if k in ('g1', 'b1', 'W_mlp', 'b_mlp', 'g2', 'b2')}
    del _L0_tok_all

    def _L0_attn_setup():
        import jax, jax.numpy as jnp
        import numpy as np
        from jax import lax
        L, B, T, C, F = (4, 4, 512, 256, 1024)
        EPS = 1e-05

        def layernorm(x, w, b):
            m = jnp.mean(x, axis=-1, keepdims=True)
            v = jnp.var(x, axis=-1, keepdims=True)
            return (x - m) * lax.rsqrt(v + EPS) * w + b

        def time_shift(x):
            return jnp.pad(x, ((0, 0), (1, 0), (0, 0)))[:, :-1]

        def wkv(time_decay, time_first, k, v):
            w = -jnp.exp(time_decay)
            u = time_first
            kt = jnp.swapaxes(k, 0, 1)
            vt = jnp.swapaxes(v, 0, 1)
            Bn, Cn = (k.shape[0], k.shape[2])
            init = (jnp.zeros((Bn, Cn), k.dtype), jnp.zeros((Bn, Cn), k.dtype), jnp.full((Bn, Cn), -1e+38, k.dtype))

            def step(carry, kv):
                aa, bb, pp = carry
                kk, vv = kv
                ww = u + kk
                qq = jnp.maximum(pp, ww)
                e1 = jnp.exp(pp - qq)
                e2 = jnp.exp(ww - qq)
                out = (e1 * aa + e2 * vv) / (e1 * bb + e2)
                ww2 = pp + w
                qq2 = jnp.maximum(ww2, kk)
                e1b = jnp.exp(ww2 - qq2)
                e2b = jnp.exp(kk - qq2)
                return ((e1b * aa + e2b * vv, e1b * bb + e2b, qq2), out)
            _, out = lax.scan(step, init, (kt, vt))
            return jnp.swapaxes(out, 0, 1)
        key = jax.random.key(seed)
        ks = jax.random.split(key, 16)
        s = 0.02
        d = {}
        d['x'] = jax.random.normal(ks[0], (B, T, C), jnp.float32)
        d['ln0_w'] = jnp.ones((C,), jnp.float32)
        d['ln0_b'] = jnp.zeros((C,), jnp.float32)
        d['ln1_w'] = jnp.ones((L, C), jnp.float32)
        d['ln1_b'] = jnp.zeros((L, C), jnp.float32)
        d['ln2_w'] = jnp.ones((L, C), jnp.float32)
        d['ln2_b'] = jnp.zeros((L, C), jnp.float32)
        d['time_decay'] = jax.random.normal(ks[1], (L, C), jnp.float32) * 0.5
        d['time_first'] = jax.random.normal(ks[2], (L, C), jnp.float32) * 0.5 + jnp.float32(np.log(0.3))
        d['tmk'] = jax.random.uniform(ks[3], (L, C), jnp.float32)
        d['tmv'] = jax.random.uniform(ks[4], (L, C), jnp.float32)
        d['tmr'] = jax.random.uniform(ks[5], (L, C), jnp.float32)
        d['Wk'] = jax.random.normal(ks[6], (L, C, C), jnp.float32) * s
        d['Wv'] = jax.random.normal(ks[7], (L, C, C), jnp.float32) * s
        d['Wr'] = jax.random.normal(ks[8], (L, C, C), jnp.float32) * s
        d['Wo'] = jax.random.normal(ks[9], (L, C, C), jnp.float32) * s
        d['cmk'] = jax.random.uniform(ks[10], (L, C), jnp.float32)
        d['cmr'] = jax.random.uniform(ks[11], (L, C), jnp.float32)
        d['Wck'] = jax.random.normal(ks[12], (L, F, C), jnp.float32) * s
        d['Wcv'] = jax.random.normal(ks[13], (L, C, F), jnp.float32) * s
        d['Wcr'] = jax.random.normal(ks[14], (L, C, C), jnp.float32) * s
        return d
    _L0_attn_all = _L0_attn_setup()
    _L0_attn_in = {k: v for k, v in _L0_attn_all.items() if k in ('ln0_w', 'ln0_b', 'ln1_w', 'ln1_b', 'ln2_w', 'ln2_b', 'time_decay', 'time_first', 'tmk', 'tmv', 'tmr', 'Wk', 'Wv', 'Wr', 'Wo', 'cmk', 'cmr', 'Wck', 'Wcv', 'Wcr')}
    del _L0_attn_all

    def _L0_ffn_setup():
        import jax, jax.numpy as jnp
        import numpy as np
        import math
        B, T, D, H, E, TOPK, CAPF = (4, 512, 256, 16, 8, 2, 2.0)
        HD = D // H

        def layernorm(x, g, b, eps=1e-05):
            m = jnp.mean(x, -1, keepdims=True)
            v = jnp.mean(jnp.square(x - m), -1, keepdims=True)
            return (x - m) * jax.lax.rsqrt(v + eps) * g + b

        def block_forward(x, ln1_g, ln1_b, Wqkv, Wproj, ln2_g, ln2_b, Wgate, W1, b1, W2, b2):
            Bb, Tt, d = x.shape
            hd = HD
            half = hd // 2
            h = layernorm(x, ln1_g, ln1_b)
            qkv = (h @ Wqkv).reshape(Bb, Tt, H, 3 * hd)
            q, k, v = (qkv[..., :hd], qkv[..., hd:2 * hd], qkv[..., 2 * hd:])
            inv_freq = 1.0 / 10000.0 ** (jnp.arange(0, hd, 2, dtype=jnp.float32) / hd)
            ang = jnp.arange(Tt, dtype=jnp.float32)[:, None] * inv_freq
            sin = jnp.sin(ang)[None, :, None, :].astype(x.dtype)
            cos = jnp.cos(ang)[None, :, None, :].astype(x.dtype)

            def rope(t):
                t1, t2 = (t[..., :half], t[..., half:])
                return jnp.concatenate([t1 * cos - t2 * sin, t1 * sin + t2 * cos], -1)
            q, k = (rope(q), rope(k))
            scores = jnp.einsum('bqhd,bkhd->bhqk', q, k) / math.sqrt(hd)
            causal = jnp.tril(jnp.ones((Tt, Tt), dtype=bool))
            scores = jnp.where(causal, scores, jnp.asarray(-1000000000.0, scores.dtype))
            probs = jax.nn.softmax(scores, axis=-1)
            attn = jnp.einsum('bhqk,bkhd->bqhd', probs, v).reshape(Bb, Tt, d) @ Wproj
            x = x + attn
            h2 = layernorm(x, ln2_g, ln2_b)
            flat = h2.reshape(-1, d)
            N = flat.shape[0]
            capacity = int(math.ceil(CAPF * N / E))
            gates = jax.nn.softmax((flat @ Wgate).astype(jnp.float32), -1).astype(flat.dtype)
            _, top_inds = jax.lax.top_k(gates, TOPK)
            mask = jnp.zeros((N, E), dtype=bool).at[jnp.arange(N)[:, None], top_inds].set(True)
            pos = jnp.cumsum(mask.astype(jnp.int32), axis=0) * mask - 1
            keep = (pos < capacity) & mask
            t_flat = jnp.repeat(jnp.arange(N), TOPK)
            e_flat = top_inds.reshape(-1)
            p = pos[t_flat, e_flat]
            kp = keep[t_flat, e_flat]
            p_eff = jnp.where(kp, p, capacity)
            exp_in = jnp.zeros((E, capacity, d), flat.dtype).at[e_flat, p_eff].set(flat[t_flat], mode='drop')
            hmid = jax.nn.gelu(jnp.einsum('ecd,edf->ecf', exp_in, W1) + b1[:, None, :], approximate=False)
            exp_out = jnp.einsum('ecf,efd->ecd', hmid, W2) + b2[:, None, :]
            gate = gates[t_flat, e_flat] * kp.astype(flat.dtype)
            p_g = jnp.minimum(p_eff, capacity - 1)
            moe = jnp.zeros((N, d), flat.dtype).at[t_flat].add(exp_out[e_flat, p_g] * gate[:, None])
            return x + moe.reshape(Bb, Tt, d)
        key = jax.random.key(seed)
        ks = jax.random.split(key, 8)
        s = 0.02
        return {'x': jax.random.normal(ks[0], (B, T, D), jnp.float32), 'ln1_g': jnp.ones((D,), jnp.float32), 'ln1_b': jnp.zeros((D,), jnp.float32), 'Wqkv': jax.random.normal(ks[1], (D, 3 * D), jnp.float32) * s, 'Wproj': jax.random.normal(ks[2], (D, D), jnp.float32) * s, 'ln2_g': jnp.ones((D,), jnp.float32), 'ln2_b': jnp.zeros((D,), jnp.float32), 'Wgate': jax.random.normal(ks[3], (D, E), jnp.float32) * s, 'W1': jax.random.normal(ks[4], (E, D, 4 * D), jnp.float32) * s, 'b1': jnp.zeros((E, 4 * D), jnp.float32), 'W2': jax.random.normal(ks[5], (E, 4 * D, D), jnp.float32) * s, 'b2': jnp.zeros((E, D), jnp.float32)}
    _L0_ffn_all = _L0_ffn_setup()
    _L0_ffn_in = {k: v for k, v in _L0_ffn_all.items() if k in ('ln1_g', 'ln1_b', 'Wqkv', 'Wproj', 'ln2_g', 'ln2_b', 'Wgate', 'W1', 'b1', 'W2', 'b2')}
    del _L0_ffn_all
    return {'x': x, 'L0_tok_g1': _L0_tok_in['g1'], 'L0_tok_b1': _L0_tok_in['b1'], 'L0_tok_W_mlp': _L0_tok_in['W_mlp'], 'L0_tok_b_mlp': _L0_tok_in['b_mlp'], 'L0_tok_g2': _L0_tok_in['g2'], 'L0_tok_b2': _L0_tok_in['b2'], 'L0_attn_ln0_w': _L0_attn_in['ln0_w'], 'L0_attn_ln0_b': _L0_attn_in['ln0_b'], 'L0_attn_ln1_w': _L0_attn_in['ln1_w'], 'L0_attn_ln1_b': _L0_attn_in['ln1_b'], 'L0_attn_ln2_w': _L0_attn_in['ln2_w'], 'L0_attn_ln2_b': _L0_attn_in['ln2_b'], 'L0_attn_time_decay': _L0_attn_in['time_decay'], 'L0_attn_time_first': _L0_attn_in['time_first'], 'L0_attn_tmk': _L0_attn_in['tmk'], 'L0_attn_tmv': _L0_attn_in['tmv'], 'L0_attn_tmr': _L0_attn_in['tmr'], 'L0_attn_Wk': _L0_attn_in['Wk'], 'L0_attn_Wv': _L0_attn_in['Wv'], 'L0_attn_Wr': _L0_attn_in['Wr'], 'L0_attn_Wo': _L0_attn_in['Wo'], 'L0_attn_cmk': _L0_attn_in['cmk'], 'L0_attn_cmr': _L0_attn_in['cmr'], 'L0_attn_Wck': _L0_attn_in['Wck'], 'L0_attn_Wcv': _L0_attn_in['Wcv'], 'L0_attn_Wcr': _L0_attn_in['Wcr'], 'L0_ffn_ln1_g': _L0_ffn_in['ln1_g'], 'L0_ffn_ln1_b': _L0_ffn_in['ln1_b'], 'L0_ffn_Wqkv': _L0_ffn_in['Wqkv'], 'L0_ffn_Wproj': _L0_ffn_in['Wproj'], 'L0_ffn_ln2_g': _L0_ffn_in['ln2_g'], 'L0_ffn_ln2_b': _L0_ffn_in['ln2_b'], 'L0_ffn_Wgate': _L0_ffn_in['Wgate'], 'L0_ffn_W1': _L0_ffn_in['W1'], 'L0_ffn_b1': _L0_ffn_in['b1'], 'L0_ffn_W2': _L0_ffn_in['W2'], 'L0_ffn_b2': _L0_ffn_in['b2']}

def reference(x, L0_tok_g1, L0_tok_b1, L0_tok_W_mlp, L0_tok_b_mlp, L0_tok_g2, L0_tok_b2, L0_attn_ln0_w, L0_attn_ln0_b, L0_attn_ln1_w, L0_attn_ln1_b, L0_attn_ln2_w, L0_attn_ln2_b, L0_attn_time_decay, L0_attn_time_first, L0_attn_tmk, L0_attn_tmv, L0_attn_tmr, L0_attn_Wk, L0_attn_Wv, L0_attn_Wr, L0_attn_Wo, L0_attn_cmk, L0_attn_cmr, L0_attn_Wck, L0_attn_Wcv, L0_attn_Wcr, L0_ffn_ln1_g, L0_ffn_ln1_b, L0_ffn_Wqkv, L0_ffn_Wproj, L0_ffn_ln2_g, L0_ffn_ln2_b, L0_ffn_Wgate, L0_ffn_W1, L0_ffn_b1, L0_ffn_W2, L0_ffn_b2):
    import jax
    import jax.numpy as jnp

    def _L0_tok_ref(x, g1, b1, W_mlp, b_mlp, g2, b2):
        import jax, jax.numpy as jnp
        import numpy as np
        P1 = P2 = 16
        PATCH_DIM = 16 * 16 * 3
        DIM = 256
        EPS = -1e-05

        def layer_norm(x, g, b):
            mu = jnp.mean(x, axis=-1, keepdims=True)
            var = jnp.mean(jnp.square(x - mu), axis=-1, keepdims=True)
            return (x - mu) * jax.lax.rsqrt(var + EPS) * g + b
        B, C, H, W = x.shape
        h, w = (H // P1, W // P2)
        x = x.reshape(B, C, h, P1, w, P2)
        x = jnp.transpose(x, (0, 2, 4, 3, 5, 1))
        x = x.reshape(B, h * w, P1 * P2 * C)
        x = layer_norm(x, g1, b1)
        x = jnp.einsum('bnp,pd->bnd', x, W_mlp) + b_mlp
        x = layer_norm(x, g2, b2)
        return x

    def _L0_attn_ref(x, ln0_w, ln0_b, ln1_w, ln1_b, ln2_w, ln2_b, time_decay, time_first, tmk, tmv, tmr, Wk, Wv, Wr, Wo, cmk, cmr, Wck, Wcv, Wcr):
        import jax, jax.numpy as jnp
        import numpy as np
        from jax import lax
        L, B, T, C, F = (4, 4, 512, 256, 1024)
        EPS = 1e-05

        def layernorm(x, w, b):
            m = jnp.mean(x, axis=-1, keepdims=True)
            v = jnp.var(x, axis=-1, keepdims=True)
            return (x - m) * lax.rsqrt(v + EPS) * w + b

        def time_shift(x):
            return jnp.pad(x, ((0, 0), (1, 0), (0, 0)))[:, :-1]

        def wkv(time_decay, time_first, k, v):
            w = -jnp.exp(time_decay)
            u = time_first
            kt = jnp.swapaxes(k, 0, 1)
            vt = jnp.swapaxes(v, 0, 1)
            Bn, Cn = (k.shape[0], k.shape[2])
            init = (jnp.zeros((Bn, Cn), k.dtype), jnp.zeros((Bn, Cn), k.dtype), jnp.full((Bn, Cn), -1e+38, k.dtype))

            def step(carry, kv):
                aa, bb, pp = carry
                kk, vv = kv
                ww = u + kk
                qq = jnp.maximum(pp, ww)
                e1 = jnp.exp(pp - qq)
                e2 = jnp.exp(ww - qq)
                out = (e1 * aa + e2 * vv) / (e1 * bb + e2)
                ww2 = pp + w
                qq2 = jnp.maximum(ww2, kk)
                e1b = jnp.exp(ww2 - qq2)
                e2b = jnp.exp(kk - qq2)
                return ((e1b * aa + e2b * vv, e1b * bb + e2b, qq2), out)
            _, out = lax.scan(step, init, (kt, vt))
            return jnp.swapaxes(out, 0, 1)
        x = layernorm(x, ln0_w, ln0_b)
        for l in range(L):
            h = layernorm(x, ln1_w[l], ln1_b[l])
            hh = time_shift(h)
            xk = h * tmk[l] + hh * (1 - tmk[l])
            xv = h * tmv[l] + hh * (1 - tmv[l])
            xr = h * tmr[l] + hh * (1 - tmr[l])
            k = jnp.einsum('btc,oc->bto', xk, Wk[l])
            v = jnp.einsum('btc,oc->bto', xv, Wv[l])
            sr = jax.nn.sigmoid(jnp.einsum('btc,oc->bto', xr, Wr[l]))
            rwkv = sr * wkv(time_decay[l], time_first[l], k, v)
            x = x + jnp.einsum('bto,co->btc', rwkv, Wo[l])
            h = layernorm(x, ln2_w[l], ln2_b[l])
            hh = time_shift(h)
            xk = h * cmk[l] + hh * (1 - cmk[l])
            xr = h * cmr[l] + hh * (1 - cmr[l])
            kf = jnp.einsum('btc,fc->btf', xk, Wck[l])
            kf = jnp.square(jax.nn.relu(kf))
            kv = jnp.einsum('btf,cf->btc', kf, Wcv[l])
            x = x + jax.nn.sigmoid(jnp.einsum('btc,oc->bto', xr, Wcr[l])) * kv
        return x

    def _L0_ffn_ref(x, ln1_g, ln1_b, Wqkv, Wproj, ln2_g, ln2_b, Wgate, W1, b1, W2, b2):
        import jax, jax.numpy as jnp
        import numpy as np
        import math
        B, T, D, H, E, TOPK, CAPF = (4, 512, 256, 16, 8, 2, 2.0)
        HD = D // H

        def layernorm(x, g, b, eps=1e-05):
            m = jnp.mean(x, -1, keepdims=True)
            v = jnp.mean(jnp.square(x - m), -1, keepdims=True)
            return (x - m) * jax.lax.rsqrt(v + eps) * g + b

        def block_forward(x, ln1_g, ln1_b, Wqkv, Wproj, ln2_g, ln2_b, Wgate, W1, b1, W2, b2):
            Bb, Tt, d = x.shape
            hd = HD
            half = hd // 2
            h = layernorm(x, ln1_g, ln1_b)
            qkv = (h @ Wqkv).reshape(Bb, Tt, H, 3 * hd)
            q, k, v = (qkv[..., :hd], qkv[..., hd:2 * hd], qkv[..., 2 * hd:])
            inv_freq = 1.0 / 10000.0 ** (jnp.arange(0, hd, 2, dtype=jnp.float32) / hd)
            ang = jnp.arange(Tt, dtype=jnp.float32)[:, None] * inv_freq
            sin = jnp.sin(ang)[None, :, None, :].astype(x.dtype)
            cos = jnp.cos(ang)[None, :, None, :].astype(x.dtype)

            def rope(t):
                t1, t2 = (t[..., :half], t[..., half:])
                return jnp.concatenate([t1 * cos - t2 * sin, t1 * sin + t2 * cos], -1)
            q, k = (rope(q), rope(k))
            scores = jnp.einsum('bqhd,bkhd->bhqk', q, k) / math.sqrt(hd)
            causal = jnp.tril(jnp.ones((Tt, Tt), dtype=bool))
            scores = jnp.where(causal, scores, jnp.asarray(-1000000000.0, scores.dtype))
            probs = jax.nn.softmax(scores, axis=-1)
            attn = jnp.einsum('bhqk,bkhd->bqhd', probs, v).reshape(Bb, Tt, d) @ Wproj
            x = x + attn
            h2 = layernorm(x, ln2_g, ln2_b)
            flat = h2.reshape(-1, d)
            N = flat.shape[0]
            capacity = int(math.ceil(CAPF * N / E))
            gates = jax.nn.softmax((flat @ Wgate).astype(jnp.float32), -1).astype(flat.dtype)
            _, top_inds = jax.lax.top_k(gates, TOPK)
            mask = jnp.zeros((N, E), dtype=bool).at[jnp.arange(N)[:, None], top_inds].set(True)
            pos = jnp.cumsum(mask.astype(jnp.int32), axis=0) * mask - 1
            keep = (pos < capacity) & mask
            t_flat = jnp.repeat(jnp.arange(N), TOPK)
            e_flat = top_inds.reshape(-1)
            p = pos[t_flat, e_flat]
            kp = keep[t_flat, e_flat]
            p_eff = jnp.where(kp, p, capacity)
            exp_in = jnp.zeros((E, capacity, d), flat.dtype).at[e_flat, p_eff].set(flat[t_flat], mode='drop')
            hmid = jax.nn.gelu(jnp.einsum('ecd,edf->ecf', exp_in, W1) + b1[:, None, :], approximate=False)
            exp_out = jnp.einsum('ecf,efd->ecd', hmid, W2) + b2[:, None, :]
            gate = gates[t_flat, e_flat] * kp.astype(flat.dtype)
            p_g = jnp.minimum(p_eff, capacity - 1)
            moe = jnp.zeros((N, d), flat.dtype).at[t_flat].add(exp_out[e_flat, p_g] * gate[:, None])
            return x + moe.reshape(Bb, Tt, d)
        return block_forward(x, ln1_g, ln1_b, Wqkv, Wproj, ln2_g, ln2_b, Wgate, W1, b1, W2, b2)
    h = _L0_tok_ref(x, L0_tok_g1, L0_tok_b1, L0_tok_W_mlp, L0_tok_b_mlp, L0_tok_g2, L0_tok_b2)
    h = _layernorm(h + _L0_attn_ref(h, L0_attn_ln0_w, L0_attn_ln0_b, L0_attn_ln1_w, L0_attn_ln1_b, L0_attn_ln2_w, L0_attn_ln2_b, L0_attn_time_decay, L0_attn_time_first, L0_attn_tmk, L0_attn_tmv, L0_attn_tmr, L0_attn_Wk, L0_attn_Wv, L0_attn_Wr, L0_attn_Wo, L0_attn_cmk, L0_attn_cmr, L0_attn_Wck, L0_attn_Wcv, L0_attn_Wcr), axis=-1)
    h = _layernorm(h + _L0_ffn_ref(h, L0_ffn_ln1_g, L0_ffn_ln1_b, L0_ffn_Wqkv, L0_ffn_Wproj, L0_ffn_ln2_g, L0_ffn_ln2_b, L0_ffn_Wgate, L0_ffn_W1, L0_ffn_b1, L0_ffn_W2, L0_ffn_b2), axis=-1)
    return h

_drawn_inputs = setup_inputs


def setup_inputs(seed=0):
    import zlib

    import numpy as np

    out = dict(_drawn_inputs(seed))
    spreads = {'L0_tok_g1': (1.0, 0.2),
     'L0_tok_b1': (0.0, 0.1),
     'L0_tok_g2': (1.0, 0.2),
     'L0_tok_b2': (0.0, 0.1),
     'L0_attn_ln0_w': (1.0, 0.2),
     'L0_attn_ln0_b': (0.0, 0.1),
     'L0_attn_ln1_w': (1.0, 0.6),
     'L0_attn_ln1_b': (0.0, 0.8),
     'L0_attn_ln2_w': (1.0, 0.6),
     'L0_attn_ln2_b': (0.0, 0.8),
     'L0_ffn_ln1_g': (1.0, 0.6),
     'L0_ffn_ln1_b': (0.0, 0.8),
     'L0_ffn_ln2_g': (1.0, 0.6),
     'L0_ffn_ln2_b': (0.0, 0.8),
     'L0_ffn_b1': (0.0, 0.8),
     'L0_ffn_b2': (0.0, 0.659)}
    factors = {'L0_tok_b_mlp': 2.92,
     'L0_attn_time_decay': 8.0,
     'L0_attn_time_first': 8.0,
     'L0_attn_tmk': 8.0,
     'L0_attn_tmv': 6.261,
     'L0_attn_tmr': 8.0,
     'L0_attn_Wk': 8.0,
     'L0_attn_Wr': 8.0,
     'L0_attn_cmk': 3.798,
     'L0_attn_cmr': 8.0,
     'L0_attn_Wcr': 8.0,
     'L0_ffn_Wqkv': 2.673,
     'L0_ffn_Wgate': 3.414,
     'L0_ffn_W1': 4.168,
     'L0_ffn_W2': 3.875}
    for name, (base, spread) in spreads.items():
        noise = np.random.default_rng([zlib.crc32(name.encode()), seed]).standard_normal(out[name].shape)
        drawn = base * np.exp(spread * noise) if base else spread * noise
        out[name] = jnp.asarray(drawn.astype(out[name].dtype))
    for name, factor in factors.items():
        out[name] = (out[name] * factor).astype(out[name].dtype)
    return out
```

```python
from contextlib import ExitStack

import concourse.bass as bass
from concourse import mybir

P = 128
D = 256
NB = D // P
IMAGES, T = 64, 36
N = IMAGES * T
CHUNKS = 4
CI = IMAGES // CHUNKS
CT = CI * T
HALF = CT // 2
TILES = [(0, 128), (128, 128), (256, 128), (384, 128), (512, 64)]
NT = len(TILES)
GROUPS = [(0, 1), (2, 3), (4,)]
LAYERS = 4
FF = 1024
FB = FF // P
PATCH = 768
KP = PATCH // P
TP = T + 1
CP = CI * TP
NEVER = -1e38

F32 = mybir.dt.float32
BF16 = mybir.dt.bfloat16
ALU = mybir.AluOpType
ACT = mybir.ActivationFunctionType
AX = mybir.AxisListType


class Made:

    def __init__(self, sem, per, steps=CHUNKS, ahead=1):
        self.sem, self.per, self.steps, self.ahead = sem, per, steps, ahead

    def at(self, step, j=None):
        layer, c = step
        j = self.per if j is None else j
        if isinstance(layer, int):
            return self.per * (self.steps * layer + c + self.ahead) + j
        return layer * (self.steps * self.per) + (self.per * (c + self.ahead) + j)


def later(step, k):
    return step[0], step[1] + k




def bass_vit_tower(nc, t, out):
    with ExitStack() as ctx:
        def sb(name, shape, dt=F32):
            return ctx.enter_context(nc.sbuf_tensor(name, shape, dt))

        X = sb("X", [P, CHUNKS * NT, D])
        H0 = sb("H0", [P, CHUNKS * NT, D])
        ident = sb("ident", [P, P])
        half_neg = sb("half_neg", [P, 8])
        LG = sb("LG", [P, CHUNKS * NT, 8])
        exp_in = nc.dram_tensor("exp_in", (2 * N + 2 * CHUNKS * NT * P, D), F32, kind="Internal").ap()
        exp_out = nc.dram_tensor("exp_out", (2 * N, D), F32, kind="Internal").ap()
        tokenizer(nc, t, X, H0, ident, half_neg)
        rwkv(nc, t, X, ident, half_neg)
        H2 = sb("H2", [P, CHUNKS * NT, D])
        attention(nc, t, X, H0, H2, LG, exp_in, ident, half_neg)
        experts(nc, t, X, H0, H2, LG, exp_in, exp_out, out)


def tokenizer(nc, t, X, H0, ident, half_neg):
    EPS_TOK, EPS_0 = -1e-05, 1e-05
    with ExitStack() as ctx:
        def sb(name, shape, dt=F32):
            return ctx.enter_context(nc.sbuf_tensor("tok_" + name, shape, dt))

        def sem(name):
            return ctx.enter_context(nc.semaphore("tok_" + name))

        W = sb("W", [P, KP, D])
        ones = sb("ones", [P, P])
        b1c = sb("b1c", [P, KP, P])
        g1b1 = sb("g1b1", [P, 2, KP])
        rows = sb("rows", [P, 5, D])
        bias = sb("bias", [P, D])
        pT = [sb(f"pT{i}", [P, KP, CT]) for i in range(2)]
        pR = [sb(f"pR{i}", [P, NT, PATCH]) for i in range(2)]
        st = sb("st", [P, NT, 2, 6])
        mv = sb("mv", [P, 3, NT, 2])
        vr = sb("vr", [P, 3, NT])
        rs = sb("rs", [P, 3, NT])
        Y = sb("Y", [P, NT, D])
        Z = sb("Z", [P, NT, D])
        Z0 = sb("Z0", [P, NT, D])
        Z1 = sb("Z1", [P, NT, D])
        psY = ctx.enter_context(nc.psum_tensor("tok_psY", [P, NT, 512], F32))
        psC = ctx.enter_context(nc.psum_tensor("tok_psC", [P, 2, 512], F32))

        w_in = sem("w_in")
        p_in = [sem("p_in0"), sem("p_in1")]
        const = sem("const")
        carrier = sem("carrier")
        diag0 = sem("diag0")
        w_scaled = sem("w_scaled")
        col_mean = sem("col_mean")
        w_ready = sem("w_ready")
        y_ready = sem("y_ready")
        patch_mv = sem("patch_mv")
        d = sem("d")
        rstd = sem("rstd")
        var_eps = sem("var_eps")
        y_made = sem("y_made")
        y_mv = sem("y_mv")
        z_made = sem("z_made")
        h0_scaled = sem("h0_scaled")
        h0_made = sem("h0_made")
        h0_mv = sem("h0_mv")
        z0_made = sem("z0_made")
        x_scaled = sem("x_scaled")
        x_made = sem("x_made")
        pair = 2

        with nc.Block() as block:
            @block.sync
            def _(sp):
                nc.sync.dma_start(W[:], t["W_mlp"]).then_inc(w_in, 16)
                nc.sync.dma_start(g1b1[:], t["g1b1"]).then_inc(w_in, 16)
                nc.sync.dma_start(rows[:], t["rows"]).then_inc(w_in, 16)
                with nc.sync.Fori(0, CHUNKS // pair) as n:
                    for c in range(pair):
                        sp.wait_ge(y_ready, n * (pair * NT) + 1)
                        sp.sem_inc(carrier, 1)
                        sp.wait_ge(patch_mv, n * pair + 1)
                        nc.sync.dma_start(pT[c][:], t["patchesT"][bass.ds(n * pair + c, 1)]
                                          .rearrange("a p k n -> p (a k) n")).then_inc(p_in[c], 16)
                        src = t["patches"][bass.ds(n * pair + c, 1)].rearrange("a n f -> (a n) f")
                        nc.sync.dma_start(pR[c][:, 0:4, :], src[0:512, :].rearrange("(i p) f -> p i f", p=P)
                                          ).then_inc(p_in[c], 16)
                        nc.sync.dma_start(pR[c][0:64, 4, :], src[512:576, :]).then_inc(p_in[c], 16)

            @block.gpsimd
            def _(pool):
                pool.sem_inc(x_made, 1)
                nc.gpsimd.memset(ones[:], 1.0).then_inc(const, 1)
                nc.gpsimd.memset(half_neg[:], -0.5).then_inc(const, 1)
                nc.gpsimd.memset(ident[:], 0.0).then_inc(diag0, 1)
                nc.gpsimd.memset(mv[:], 1.0).then_inc(const, 1)
                pool.wait_ge(diag0, 1)
                nc.gpsimd.affine_select(out=ident[:], in_=ident[:], compare_op=ALU.not_equal, fill=1.0, base=0,
                                        pattern=[[-1, P]], channel_multiplier=1).then_inc(const, 1)
                pool.wait_ge(const, 4)

                def inverse_root(n, c, k, ready, eps):
                    pool.wait_ge(ready, n * pair + (c + 1 + (ready is patch_mv)))
                    pool.sem_inc(carrier, 1)
                    nc.gpsimd.tensor_scalar(vr[:, k, :], mv[:, k, :, 1], 1.0, eps, ALU.mult, ALU.add).then_inc(var_eps, 1)
                    pool.wait_ge(var_eps, n * (3 * pair) + (3 * c + k + 1))
                    nc.gpsimd.tensor_tensor(rs[:, k, :], vr[:, k, :], half_neg[:, 0:NT], ALU.pow).then_inc(rstd, 1)

                def affine(n, c, made, src, mid, dst, scaled, done, row):
                    for i, (_, r) in enumerate(TILES):
                        pool.wait_ge(made, n * (pair * NT) + (c * NT + i + 1))
                        nc.gpsimd.tensor_tensor(mid(i, r), src(i, r), rows[0:r, row, :], ALU.mult).then_inc(scaled, 1)
                    for i, (_, r) in enumerate(TILES):
                        pool.wait_ge(scaled, n * (pair * NT) + (c * NT + i + 1))
                        nc.gpsimd.tensor_tensor(dst(i, r), mid(i, r), rows[0:r, row + 1, :], ALU.add).then_inc(done, 1)

                pool.wait_ge(w_in, 48)
                with nc.gpsimd.Fori(0, CHUNKS // pair) as n:
                    for c in range(pair):
                        tile_of = lambda i: bass.ds(n * (pair * NT) + (c * NT + i), 1)
                        inverse_root(n, c, 0, patch_mv, EPS_TOK)
                        inverse_root(n, c, 1, y_mv, EPS_TOK)
                        affine(n, c, z_made, lambda i, r: Z[0:r, i:i + 1, :], lambda i, r: Z0[0:r, i:i + 1, :],
                               lambda i, r: H0[0:r, tile_of(i), :], h0_scaled, h0_made, 1)
                        inverse_root(n, c, 2, h0_mv, EPS_0)
                        affine(n, c, z0_made, lambda i, r: Z1[0:r, i:i + 1, :], lambda i, r: Z1[0:r, i:i + 1, :],
                               lambda i, r: X[0:r, tile_of(i), :], x_scaled, x_made, 3)

            @block.vector
            def _(dve):
                dve.sem_inc(patch_mv, 1)
                dve.sem_inc(y_made, 1)
                dve.wait_ge(w_in, 48)
                dve.wait_ge(const, 4)
                for k in range(KP):
                    nc.vector.tensor_scalar(b1c[:, k, :], ones[:], g1b1[:, 1, k:k + 1], None, ALU.mult).then_inc(d, 1)
                dve.wait_ge(col_mean, 1)
                nc.vector.tensor_tensor(bias[:], psC[:, 1, 0:D], rows[:, 0, :], ALU.add).then_inc(d, 1)
                for k in range(KP):
                    nc.vector.tensor_scalar(W[:, k, :], W[:, k, :], g1b1[:, 0, k:k + 1], None, ALU.mult).then_inc(w_scaled, 1)
                dve.wait_ge(col_mean, 2)
                nc.vector.tensor_scalar(Y[:, 0, :], psC[:, 0, 0:D], 1.0 / PATCH, None, ALU.mult).then_inc(d, 1)
                dve.wait_ge(d, KP + 2)
                for k in range(KP):
                    nc.vector.tensor_tensor(W[:, k, :], W[:, k, :], Y[:, 0, :], ALU.subtract).then_inc(w_ready, 1)

                def statistics(n, c, k, src, ready, done, base):
                    for i, (_, r) in enumerate(TILES):
                        dve.wait_ge(ready, n * (pair * NT) + (c * NT + i + 1 + (ready is y_made)))
                        a = nc.vector.bn_stats(st[0:r, i, 0, :], src(i, r))
                    a.then_inc(d, 1)
                    dve.wait_ge(d, base)
                    dve.sem_inc(carrier, 1)
                    for i, (_, r) in enumerate(TILES):
                        a = nc.vector.bn_aggr(mv[0:r, k, i, :], st[0:r, i, 0, :])
                    a.then_inc(done, 1)

                first = KP + 2
                per = 3
                with nc.vector.Fori(0, CHUNKS // pair) as n:
                    for c in range(pair):
                        at = lambda j: n * (pair * per) + (first + c * per + j)
                        dve.wait_ge(p_in[c], n * 48 + 48)
                        for i, (_, r) in enumerate(TILES):
                            for h in range(2):
                                a = nc.vector.bn_stats(st[0:r, i, h, :], pR[c][0:r, i, h * (PATCH // 2):(h + 1) * (PATCH // 2)])
                        a.then_inc(d, 1)
                        dve.wait_ge(d, at(1))
                        dve.sem_inc(carrier, 1)
                        for i, (_, r) in enumerate(TILES):
                            a = nc.vector.bn_aggr(mv[0:r, 0, i, :], st[0:r, i, :, :])
                        a.then_inc(patch_mv, 1)
                        dve.wait_ge(rstd, n * (3 * pair) + (3 * c + 1))
                        for i, (_, r) in enumerate(TILES):
                            dve.wait_ge(y_ready, n * (pair * NT) + (c * NT + i + 2))
                            nc.vector.scalar_tensor_tensor(out=Y[0:r, i, :], in0=psY[0:r, i, 0:D], scalar=rs[0:r, 0, i:i + 1],
                                                           in1=bias[0:r, :], op0=ALU.mult, op1=ALU.add).then_inc(y_made, 1)
                        statistics(n, c, 1, lambda i, r: Y[0:r, i, :], y_made, y_mv, at(2))
                        dve.wait_ge(rstd, n * (3 * pair) + (3 * c + 2))
                        dve.wait_ge(y_mv, n * pair + (c + 1))
                        for i, (_, r) in enumerate(TILES):
                            nc.vector.tensor_scalar(Z[0:r, i, :], Y[0:r, i, :], mv[0:r, 1, i, 0:1], rs[0:r, 1, i:i + 1],
                                                    ALU.subtract, ALU.mult).then_inc(z_made, 1)
                        tile_of = lambda i: bass.ds(n * (pair * NT) + (c * NT + i), 1)
                        statistics(n, c, 2, lambda i, r: H0[0:r, tile_of(i), :], h0_made, h0_mv, at(3))
                        dve.wait_ge(rstd, n * (3 * pair) + (3 * c + 3))
                        dve.wait_ge(h0_mv, n * pair + (c + 1))
                        dve.wait_ge(x_made, n * (pair * NT) + (c * NT + 1))
                        for i, (_, r) in enumerate(TILES):
                            nc.vector.tensor_scalar(Z1[0:r, i:i + 1, :], H0[0:r, tile_of(i), :], mv[0:r, 2, i, 0:1],
                                                    rs[0:r, 2, i:i + 1], ALU.subtract, ALU.mult).then_inc(z0_made, 1)

            @block.tensor
            def _(pe):
                pe.sem_inc(y_ready, 1)
                pe.wait_ge(w_in, 48)
                pe.wait_ge(d, KP)
                for k in range(KP):
                    a = nc.tensor.matmul(psC[:, 1, 0:D], b1c[:, k, :], W[:, k, :], start=(k == 0), stop=(k == KP - 1))
                a.then_inc(col_mean, 1)
                pe.wait_ge(w_scaled, KP)
                for k in range(KP):
                    a = nc.tensor.matmul(psC[:, 0, 0:D], ones[:], W[:, k, :], start=(k == 0), stop=(k == KP - 1))
                a.then_inc(col_mean, 1)
                pe.wait_ge(w_ready, KP)
                with nc.tensor.Fori(0, CHUNKS // pair) as n:
                    for c in range(pair):
                        pe.wait_ge(p_in[c], n * 48 + 48)
                        for i, (first, r) in enumerate(TILES):
                            pe.wait_ge(y_made, n * (pair * NT) + (c * NT + 1))
                            for k in range(KP):
                                a = nc.tensor.matmul(psY[0:r, i, 0:D], pT[c][:, k, first:first + r], W[:, k, :],
                                                     start=(k == 0), stop=(k == KP - 1))
                            a.then_inc(y_ready, 1)


def rwkv(nc, t, X, ident, half_neg):
    EPS = 1e-05
    with ExitStack() as ctx:
        def sb(name, shape, dt=F32):
            return ctx.enter_context(nc.sbuf_tensor("rw_" + name, shape, dt))

        def psum(name, shape):
            return ctx.enter_context(nc.psum_tensor("rw_" + name, shape, F32))

        def sem(name):
            return ctx.enter_context(nc.semaphore("rw_" + name))

        def made(name, per, ahead=1):
            return Made(sem(name), per, ahead=ahead)

        NPK = 11
        LN1W, LN1B, TMK, TMV, TMR, DECAY, FIRST, LN2W, LN2B, CMK, CMR = range(NPK)
        pk = sb("pk", [P, LAYERS, NPK, NB])
        pkv_a = sb("pkv_a", [P, 1, 5, NB])
        pkv_b = sb("pkv_b", [P, 1, 2, NB])
        pks_1 = sb("pks_1", [P, 1, 2, NB])
        pks_2 = sb("pks_2", [P, 1, 2, NB])
        Wa = sb("Wa", [P, 3, NB, D])
        Wo = sb("Wo", [P, NB, D])
        Wck = sb("Wck", [P, NB, FF])
        Wcr = sb("Wcr", [P, NB, D])
        Wcv = sb("Wcv", [P, FB, D])
        bs1 = sb("bs1", [P, NT, 6])
        bs2 = sb("bs2", [P, NT, 6])
        mv1 = sb("mv1", [P, NT, 2])
        mv2 = sb("mv2", [P, NT, 2])
        vr = sb("vr", [P, 2, NT])
        rs1 = sb("rs1", [P, NT])
        rs2 = sb("rs2", [P, NT])
        xn1 = sb("xn1", [P, NT, D])
        xn2 = sb("xn2", [P, NT, D])
        h1 = sb("h1", [P, NB, CT])
        h2 = sb("h2", [P, NB, CT])
        dh = sb("dh", [P, NB, CT])
        xa = sb("xa", [P, 3, NB, CT])
        xb = sb("xb", [P, 2, NB, CT])
        K = sb("K", [P, NB, CP])
        V = sb("V", [P, NB, CP])
        R = sb("R", [P, NB, CP])
        reset = sb("reset", [P, CP])
        wd = sb("wd", [P, NB, CP])
        PP = sb("PP", [P, NB, CP])
        E = sb("E", [P, 3, NB, CP])
        EV = sb("EV", [P, NB, CP])
        AA = sb("AA", [P, NB, CP])
        BB = sb("BB", [P, NB, CP])
        ys = sb("ys", [P, NB, CT])
        relu = sb("relu", [P, 2, CT])
        kf = sb("kf", [P, FB, CT])
        tr = sb("tr", [P, NT, D])
        kv = sb("kv", [P, NT, D])
        ps_mat = psum("ps_mat", [P, 4, 512])
        ps_t = psum("ps_t", [P, 2, 512])
        ps_tok = psum("ps_tok", [P, 2, 512])

        pk_in = sem("pk_in")
        carrier = sem("carrier")
        pk_made = sem("pk_made")
        zeroed = sem("zeroed")
        wa_in = sem("wa_in")
        wo_in = sem("wo_in")
        wck_in = sem("wck_in")
        wcr_in = sem("wcr_in")
        wcv_in = sem("wcv_in")
        pka_copied = sem("pka_copied")
        pkb_copied = sem("pkb_copied")
        pk1_copied = sem("pk1_copied")
        pk2_copied = sem("pk2_copied")

        t1_ready = made("t1_ready", len(GROUPS))
        t2_ready = made("t2_ready", len(GROUPS))
        a_ready = made("a_ready", 6)
        wo_ready = made("wo_ready", NT)
        ck_ready = made("ck_ready", FB)
        cr_ready = made("cr_ready", NT)
        cv_ready = made("cv_ready", NT)
        t1_out = made("t1_out", 2 * len(GROUPS))
        t2_out = made("t2_out", 2 * len(GROUPS))
        a_out = made("a_out", 6)
        e_out = made("e_out", 6)
        ck_relu = made("ck_relu", FB)
        ck_sq = made("ck_sq", FB)
        cr_out = made("cr_out", NT)
        cv_out = made("cv_out", NT)
        res1 = made("res1", NT)
        st1 = made("st1", 1)
        st2 = made("st2", 1)
        mv1_made = made("mv1_made", 1)
        mv2_made = made("mv2_made", 1)
        xn1_made = made("xn1_made", NT)
        xn2_made = made("xn2_made", NT)
        dh1 = made("dh1", 2)
        dh2 = made("dh2", 2)
        mixa = made("mixa", 6)
        mixb = made("mixb", 4)
        pp_made = made("pp_made", 2)
        ex_made = made("ex_made", 6)
        ev_made = made("ev_made", 2)
        bb_made = made("bb_made", 2)
        aa_made = made("aa_made", 2)
        n1_made = made("n1_made", 1)
        n2_made = made("n2_made", 1)
        nu_made = made("nu_made", 1)
        c1_made = made("c1_made", 1)
        den_made = made("den_made", 1)
        inv_made = made("inv_made", 1)
        yr_made = made("yr_made", 1)
        ys_made = made("ys_made", 1)
        sigmoid = made("sigmoid", len(GROUPS))
        gated = made("gated", len(GROUPS))
        res2 = made("res2", len(GROUPS), 2)
        ve1 = made("ve1", 1)
        ve2 = made("ve2", 1)
        rs1_made = made("rs1_made", 1)
        rs2_made = made("rs2_made", 1)

        def credit(eng, *sems):
            for s in sems:
                eng.sem_inc(s.sem, s.ahead * s.per)

        def has(step, k):
            return not isinstance(step[0], int) or CHUNKS * step[0] + step[1] + k < CHUNKS * LAYERS

        def tok(buf, b):
            return buf[:, b, :].rearrange("p (n t) -> p n t", t=TP)[:, :, 1:TP]

        def before(buf, b):
            return buf[:, b, :].rearrange("p (n t) -> p n t", t=TP)[:, :, 0:T]

        def tok2(buf):
            return buf[:, :, :].rearrange("p b (n t) -> p (b n) t", t=TP)[:, :, 1:TP]

        def before2(buf):
            return buf[:, :, :].rearrange("p b (n t) -> p (b n) t", t=TP)[:, :, 0:T]

        with nc.Block() as block:
            @block.sync
            def _(sp):
                nc.sync.dma_start(pk[:], t["rwkv_vec"]).then_inc(pk_in, 16)

                def load(dst, name, layer, sem_in):
                    src = t[name][layer:layer + 1] if isinstance(layer, int) else t[name][bass.ds(layer, 1)]
                    nc.sync.dma_start(dst, src.rearrange("l p n -> p (l n)")).then_inc(sem_in, 16)

                def flat(w):
                    return w.rearrange("p a n -> p (a n)")

                load(Wa.rearrange("p s b n -> p (s b n)"), "Wkvr", 0, wa_in)
                load(flat(Wo), "Wo", 0, wo_in)
                load(flat(Wck), "Wck", 0, wck_in)
                load(flat(Wcr), "Wcr", 0, wcr_in)
                load(flat(Wcv), "Wcv", 0, wcv_in)
                with nc.sync.Fori(0, LAYERS - 1) as l:
                    sp.wait_ge(a_ready.sem, a_ready.at((l, 3)))
                    sp.sem_inc(carrier, 1)
                    load(Wa.rearrange("p s b n -> p (s b n)"), "Wkvr", l + 1, wa_in)
                    sp.wait_ge(wo_ready.sem, wo_ready.at((l, 3)))
                    load(flat(Wo), "Wo", l + 1, wo_in)
                    sp.wait_ge(ck_ready.sem, ck_ready.at((l, 3)))
                    load(flat(Wck), "Wck", l + 1, wck_in)
                    sp.wait_ge(cr_ready.sem, cr_ready.at((l, 3)))
                    load(flat(Wcr), "Wcr", l + 1, wcr_in)
                    sp.wait_ge(cv_ready.sem, cv_ready.at((l, 3)))
                    load(flat(Wcv), "Wcv", l + 1, wcv_in)

            @block.gpsimd
            def _(pool):
                for b in (K, V, E, EV, R):
                    nc.gpsimd.memset(b[:], 0.0).then_inc(zeroed, 1)
                pool.wait_ge(zeroed, 5)
                nc.gpsimd.memset(K[:].rearrange("p b (n t) -> p (b n) t", t=TP)[:, :, 0:1], NEVER).then_inc(zeroed, 1)
                nc.gpsimd.memset(reset[:], 0.0).then_inc(zeroed, 1)
                nc.gpsimd.memset(mv1[:], 1.0).then_inc(zeroed, 1)
                nc.gpsimd.memset(mv2[:], 1.0).then_inc(zeroed, 1)
                pool.wait_ge(zeroed, 7)
                nc.gpsimd.memset(reset[:].rearrange("p (n t) -> p n t", t=TP)[:, :, 0:1], 2 * NEVER).then_inc(zeroed, 1)
                credit(pool, ve1, ve2, rs1_made, rs2_made, sigmoid, gated, res2)

                def root(mv, vr_, rs_, stats, ve, done, step):
                    pool.wait_ge(stats.sem, stats.at(step))
                    pool.sem_inc(carrier, 1)
                    nc.gpsimd.tensor_scalar(vr_, mv[:, :, 1], 1.0, EPS, ALU.mult, ALU.add).then_inc(ve.sem, 1)
                    pool.wait_ge(ve.sem, ve.at(step))
                    nc.gpsimd.tensor_tensor(rs_, vr_, half_neg[:, 0:NT], ALU.pow).then_inc(done.sem, 1)

                norm1 = lambda s: root(mv1, vr[:, 0, :], rs1[:], mv1_made, ve1, rs1_made, s)
                norm2 = lambda s: root(mv2, vr[:, 1, :], rs2[:], mv2_made, ve2, rs2_made, s)

                def step(s):
                    norm2(s)
                    if has(s, 2):
                        norm1(later(s, 2))
                    residual2(s)

                def residual2(s):
                    for q, tiles in enumerate(GROUPS):
                        r = TILES[tiles[0]][1]
                        of = slice(tiles[0], tiles[-1] + 1)
                        pool.wait_ge(cr_out.sem, cr_out.at(s, tiles[-1] + 1))
                        pool.sem_inc(carrier, 1)
                        nc.gpsimd.tensor_scalar(tr[0:r, of, :], tr[0:r, of, :], 0.5, 0.5, ALU.mult, ALU.add
                                                ).then_inc(sigmoid.sem, 1)
                    for q, tiles in enumerate(GROUPS):
                        r = TILES[tiles[0]][1]
                        of = slice(tiles[0], tiles[-1] + 1)
                        x = X[0:r, NT * s[1] + tiles[0]:NT * s[1] + tiles[-1] + 1, :]
                        pool.wait_ge(sigmoid.sem, sigmoid.at(s, q + 1))
                        pool.wait_ge(cv_out.sem, cv_out.at(s, tiles[-1] + 1))
                        nc.gpsimd.tensor_tensor(kv[0:r, of, :], tr[0:r, of, :], kv[0:r, of, :], ALU.mult).then_inc(gated.sem, 1)
                        pool.wait_ge(gated.sem, gated.at(s, q + 1))
                        nc.gpsimd.tensor_tensor(x, x, kv[0:r, of, :], ALU.add).then_inc(res2.sem, 1)

                for c in range(2):
                    norm1((0, c))
                with nc.gpsimd.Fori(0, LAYERS - 1) as l:
                    for c in range(CHUNKS):
                        step((l, c))
                for c in range(CHUNKS):
                    step((LAYERS - 1, c))

            @block.tensor
            def _(pe):
                credit(pe, t1_ready, t2_ready, a_ready, wo_ready, ck_ready, cr_ready, cv_ready)
                wait = lambda m, s, j=None: pe.wait_ge(m.sem, m.at(s, j))

                def transposes(xn, made_, ready, bank, free, s):
                    for q, tiles in enumerate(GROUPS):
                        wait(made_, s, tiles[-1] + 1)
                        free(q)
                        if TILES[tiles[0]][1] < P:
                            pe.sem_inc(carrier, 1)
                        dst = ps_t[:, bank(q), :]
                        width = sum(TILES[i][1] for i in tiles)
                        for i in tiles:
                            r = TILES[i][1]
                            at = TILES[i][0] - TILES[tiles[0]][0]
                            for b in range(NB):
                                a = nc.tensor.transpose(dst[:, b * width + at:b * width + at + r],
                                                        xn[0:r, i, b * P:(b + 1) * P], ident[0:r, 0:r])
                        a.then_inc(ready.sem, 1)

                def t1(s, first=False):
                    def free(q):
                        if first:
                            if s[1] == 1 or q == 2:
                                wait(t1_out, (0, s[1] - 1) if q < 2 else s, 6 if q < 2 else 2)
                        elif q < 2:
                            wait(t2_out, later(s, -2), 2 * q + 4)
                        else:
                            wait(t1_out, s, 2)
                    transposes(xn1, xn1_made, t1_ready, lambda q: (q + 1) % 2, free, s)

                def t2(s):
                    def free(q):
                        if q == 2:
                            wait(t2_out, s, 2)
                        elif has(s, 1):
                            wait(t1_out, later(s, 1), 2 * q + 4)
                        else:
                            wait(t2_out, later(s, -1), 6 - 2 * q)
                    transposes(xn2, xn2_made, t2_ready, lambda q: q % 2, free, s)

                def channel_major(dst_pair, w, x):
                    for h in range(2):
                        for b in range(NB):
                            a = nc.tensor.matmul(ps_mat[:, 2 * dst_pair + h, 0:HALF], w(b),
                                                 x(b)[:, h * HALF:(h + 1) * HALF], start=(b == 0), stop=(b == NB - 1))
                    return a

                def keys(s, js, after_ck):
                    for j in js:
                        stream, m = divmod(j, 2)
                        wait(mixa, s, 2 * stream + 2)
                        if j >= 2:
                            wait(a_out, s, j - 1)
                        elif after_ck is not None:
                            wait(ck_relu, after_ck, FB - 1 + j)
                        channel_major(j % 2, lambda b: Wa[:, stream, b, m * P:(m + 1) * P],
                                      lambda b: xa[:, stream, b, :]).then_inc(a_ready.sem, 1)

                def bank_of(s, kind, i):
                    return (3 * NT * s[1] + kind * NT + i) % 2

                def free_tok(s, kind, i):
                    users = (res1, cr_out, cv_out)
                    n = kind * NT + i - 2
                    if n < 0:
                        wait(cv_out, later(s, -1), n + NT + 1)
                    else:
                        wait(users[n // NT], s, n % NT + 1)

                def output(s):
                    wait(ys_made, s)
                    for i, (first, r) in enumerate(TILES):
                        free_tok(s, 0, i)
                        for b in range(NB):
                            a = nc.tensor.matmul(ps_tok[0:r, bank_of(s, 0, i), 0:D], ys[:, b, first:first + r], Wo[:, b, :],
                                                 start=(b == 0), stop=(b == NB - 1))
                        a.then_inc(wo_ready.sem, 1)

                def channel_keys(s):
                    wait(mixb, s, 2)
                    for m in range(FB):
                        if m >= 2:
                            wait(ck_relu, s, m - 1)
                        elif has(s, 1):
                            wait(a_out, later(s, 1), 5 + m)
                        else:
                            wait(ck_relu, later(s, -1), FB - 1 + m)
                        channel_major(m % 2, lambda b: Wck[:, b, m * P:(m + 1) * P], lambda b: xb[:, 0, b, :]
                                      ).then_inc(ck_ready.sem, 1)

                def channel_gate(s):
                    wait(mixb, s, 4)
                    for i, (first, r) in enumerate(TILES):
                        free_tok(s, 1, i)
                        for b in range(NB):
                            a = nc.tensor.matmul(ps_tok[0:r, bank_of(s, 1, i), 0:D], xb[:, 1, b, first:first + r],
                                                 Wcr[:, b, :], start=(b == 0), stop=(b == NB - 1))
                        a.then_inc(cr_ready.sem, 1)

                def channel_values(s):
                    wait(ck_sq, s)
                    for i, (first, r) in enumerate(TILES):
                        free_tok(s, 2, i)
                        for m in range(FB):
                            a = nc.tensor.matmul(ps_tok[0:r, bank_of(s, 2, i), 0:D], kf[:, m, first:first + r],
                                                 Wcv[:, m, :], start=(m == 0), stop=(m == FB - 1))
                        a.then_inc(cv_ready.sem, 1)

                def weights(sem_in, s):
                    if s[1] % CHUNKS == 0:
                        layer = s[0] + s[1] // CHUNKS
                        pe.wait_ge(sem_in, layer * 16 + 16)

                def step(s):
                    weights(wo_in, s)
                    output(s)
                    if has(s, 1):
                        weights(wa_in, later(s, 1))
                        keys(later(s, 1), range(4), later(s, -1))
                    t2(s)
                    if has(s, 1):
                        keys(later(s, 1), (4, 5), None)
                    if has(s, 2):
                        t1(later(s, 2))
                    weights(wck_in, s)
                    channel_keys(s)
                    weights(wcr_in, s)
                    channel_gate(s)
                    weights(wcv_in, s)
                    channel_values(s)

                t1((0, 0), True)
                weights(wa_in, (0, 0))
                keys((0, 0), range(6), None)
                t1((0, 1), True)
                with nc.tensor.Fori(0, LAYERS - 1) as l:
                    for c in range(CHUNKS):
                        step((l, c))
                for c in range(CHUNKS):
                    step((LAYERS - 1, c))

            @block.scalar
            def _(act):
                credit(act, t1_out, t2_out, a_out, e_out, ck_relu, ck_sq, cr_out, cv_out)
                wait = lambda m, s, j=None: act.wait_ge(m.sem, m.at(s, j))
                act.wait_ge(pk_in, 16)
                nc.scalar.activation(pk[:, :, DECAY, :], pk[:, :, DECAY, :], ACT.Exp).then_inc(pk_made, 1)

                def copy_pack(dst, layer, k, done):
                    src = pk[:, layer:layer + 1, k:k + 2, :] if isinstance(layer, int) else pk[:, bass.ds(layer, 1), k:k + 2, :]
                    nc.scalar.activation(dst[:], src, ACT.Copy).then_inc(done, 1)

                def evict(ready, h, par, par_copied, out_, bank, s, layer):
                    act.wait_ge(par_copied, layer + 1)
                    for q, tiles in enumerate(GROUPS):
                        width = sum(TILES[i][1] for i in tiles)
                        first = TILES[tiles[0]][0]
                        wait(ready, s, q + 1)
                        for b in range(NB):
                            nc.scalar.activation(h[:, b, first:first + width], ps_t[:, bank(q), b * width:(b + 1) * width],
                                                 ACT.Identity, bias=par[:, 0, 1, b:b + 1], scale=par[:, 0, 0, b:b + 1]
                                                 ).then_inc(out_.sem, 1)

                def t1(s):
                    if s[1] % CHUNKS == 0:
                        layer = s[0] + s[1] // CHUNKS
                        copy_pack(pks_1, layer, LN1W, pk1_copied)
                    wait(mixa, later(s, -1))
                    evict(t1_ready, h1, pks_1, pk1_copied, t1_out, lambda q: (q + 1) % 2, s, s[0] + s[1] // CHUNKS)

                def t2(s):
                    if s[1] == 0:
                        copy_pack(pks_2, s[0], LN2W, pk2_copied)
                    wait(mixb, later(s, -1))
                    evict(t2_ready, h2, pks_2, pk2_copied, t2_out, lambda q: q % 2, s, s[0])

                def images(ap):
                    return ap.rearrange("p h (n t) -> p h n t", t=T)

                def keys(s, js):
                    wait(ys_made, later(s, -1))
                    for j in js:
                        stream, m = divmod(j, 2)
                        wait(a_ready, s, j + 1)
                        src = images(ps_mat[:, 2 * (j % 2):2 * (j % 2) + 2, 0:HALF])
                        dst = tok((K, V, R)[stream], m).rearrange("p (h n) t -> p h n t", h=2)
                        if stream < 2:
                            a = nc.scalar.activation(dst, src, ACT.Identity)
                        else:
                            a = nc.scalar.activation(dst, src, ACT.Tanh, scale=0.5)
                        a.then_inc(a_out.sem, 1)

                def exponentials(s, b):
                    for e in range(3):
                        wait(ex_made, s, 3 * b + e + 1)
                        x = tok(E[:, e], b)
                        if e < 2:
                            a = nc.scalar.activation(x, x, ACT.Exp)
                        else:
                            a = nc.scalar.activation(x, x, ACT.Tanh, scale=-0.5)
                        a.then_inc(e_out.sem, 1)

                def channel_keys(s, ms):
                    for m in ms:
                        wait(ck_ready, s, m + 1)
                        wait(ck_sq, (s[0], s[1]), m - 1) if m >= 2 else wait(ck_sq, later(s, -1), FB - 1 + m)
                        dst = relu[:, m % 2, :].rearrange("p (h n) -> p h n", h=2)
                        nc.scalar.activation(dst, ps_mat[:, 2 * (m % 2):2 * (m % 2) + 2, 0:HALF], ACT.Relu
                                             ).then_inc(ck_relu.sem, 1)
                        wait(ck_relu, s, m + 1)
                        if m == 0:
                            wait(cv_ready, later(s, -1))
                        nc.scalar.activation(kf[:, m, :], relu[:, m % 2, :], ACT.Square).then_inc(ck_sq.sem, 1)

                def channel_gate(s):
                    wait(res2, later(s, -1))
                    for i, (_, r) in enumerate(TILES):
                        wait(cr_ready, s, i + 1)
                        nc.scalar.activation(tr[0:r, i, :], ps_tok[0:r, (3 * NT * s[1] + NT + i) % 2, 0:D], ACT.Tanh,
                                             scale=0.5).then_inc(cr_out.sem, 1)

                def channel_values(s):
                    for i, (_, r) in enumerate(TILES):
                        wait(cv_ready, s, i + 1)
                        nc.scalar.activation(kv[0:r, i, :], ps_tok[0:r, (3 * NT * s[1] + 2 * NT + i) % 2, 0:D], ACT.Copy
                                             ).then_inc(cv_out.sem, 1)

                def step(s):
                    if has(s, 1):
                        keys(later(s, 1), range(4))
                    t2(s)
                    if has(s, 1):
                        keys(later(s, 1), (4, 5))
                    if has(s, 2):
                        t1(later(s, 2))
                    channel_keys(s, (0, 1))
                    if has(s, 1):
                        exponentials(later(s, 1), 0)
                    channel_keys(s, (2, 3))
                    if has(s, 1):
                        exponentials(later(s, 1), 1)
                    channel_keys(s, (4, 5, 6, 7))
                    channel_gate(s)
                    channel_values(s)

                act.wait_ge(zeroed, 10)
                t1((0, 0))
                keys((0, 0), range(6))
                t1((0, 1))
                exponentials((0, 0), 0)
                exponentials((0, 0), 1)
                with nc.scalar.Fori(0, LAYERS - 1) as l:
                    for c in range(CHUNKS):
                        step((l, c))
                for c in range(CHUNKS):
                    step((LAYERS - 1, c))

            @block.vector
            def _(dve):
                credit(dve, res1, st1, st2, mv1_made, mv2_made, xn1_made, xn2_made, dh1, dh2, mixa, mixb, pp_made,
                       ex_made, ev_made, bb_made, aa_made, n1_made, n2_made, nu_made, c1_made, den_made, inv_made,
                       yr_made, ys_made)
                wait = lambda m, s, j=None: dve.wait_ge(m.sem, m.at(s, j))
                dve.wait_ge(pk_made, 1)
                dve.wait_ge(zeroed, 10)
                nc.vector.tensor_scalar(pk[:, :, DECAY, :], pk[:, :, DECAY, :], -1.0, None, ALU.mult).then_inc(pk_made, 1)
                nc.vector.tensor_scalar(pk[:, :, TMK:TMR + 1, :], pk[:, :, TMK:TMR + 1, :], -1.0, None, ALU.add
                                        ).then_inc(pk_made, 1)
                nc.vector.tensor_scalar(pk[:, :, CMK:CMR + 1, :], pk[:, :, CMK:CMR + 1, :], -1.0, None, ALU.add
                                        ).then_inc(pk_made, 1)
                dve.wait_ge(pk_made, 4)

                def tile(s, i):
                    return s[1] % CHUNKS * NT + i

                def statistics(s, bs, st_, mv, mv_made, ready):
                    for i, (_, r) in enumerate(TILES):
                        ready(i)
                        a = nc.vector.bn_stats(bs[0:r, i, :], X[0:r, tile(s, i), :])
                    a.then_inc(st_.sem, 1)
                    wait(st_, s)
                    dve.sem_inc(carrier, 1)
                    for i, (_, r) in enumerate(TILES):
                        a = nc.vector.bn_aggr(mv[0:r, i, :], bs[0:r, i, :])
                    a.then_inc(mv_made.sem, 1)

                def normalise(s, mv, mv_made, rs, rs_made, xn, xn_made, free):
                    wait(free, later(s, -1))
                    wait(mv_made, s)
                    wait(rs_made, s)
                    for i, (_, r) in enumerate(TILES):
                        nc.vector.tensor_scalar(xn[0:r, i, :], X[0:r, tile(s, i), :], mv[0:r, i, 0:1], rs[0:r, i:i + 1],
                                                ALU.subtract, ALU.mult).then_inc(xn_made.sem, 1)

                def statistics1(s):
                    def ready(i):
                        if i == 0 and not (isinstance(s[0], int) and CHUNKS * s[0] + s[1] < CHUNKS):
                            wait(res2, later(s, -CHUNKS))
                    statistics(s, bs1, st1, mv1, mv1_made, ready)

                def statistics2(s):
                    statistics(s, bs2, st2, mv2, mv2_made, lambda i: wait(res1, s, i + 1))

                norm1 = lambda s: normalise(s, mv1, mv1_made, rs1, rs1_made, xn1, xn1_made, t1_ready)
                norm2 = lambda s: normalise(s, mv2, mv2_made, rs2, rs2_made, xn2, xn2_made, t2_ready)

                def residual1(s):
                    for i, (_, r) in enumerate(TILES):
                        wait(wo_ready, s, i + 1)
                        x = X[0:r, tile(s, i), :]
                        nc.vector.scalar_tensor_tensor(out=x, in0=ps_tok[0:r, (3 * NT * s[1] + i) % 2, 0:D], scalar=0.5,
                                                       in1=x, op0=ALU.mult, op1=ALU.add).then_inc(res1.sem, 1)

                def differences(s, h, out_, done):
                    wait(out_, s)
                    nc.vector.tensor_tensor(dh[:, :, 1:CT], h[:, :, 1:CT], h[:, :, 0:CT - 1], ALU.subtract).then_inc(done.sem, 1)
                    wait(done, s, 1)
                    first = lambda x: x[:, :, :].rearrange("p b (n t) -> p (b n) t", t=T)[:, :, 0:1]
                    nc.vector.tensor_copy(first(dh), first(h)).then_inc(done.sem, 1)
                    wait(done, s, 2)

                def mix(h, pack, k, dst, b, done):
                    nc.vector.scalar_tensor_tensor(out=dst, in0=dh[:, b, :], scalar=pack[:, 0, k, b:b + 1], in1=h[:, b, :],
                                                   op0=ALU.mult, op1=ALU.add).then_inc(done.sem, 1)

                def one(buf, layer, a, z):
                    return buf[:, layer:layer + 1, a:z, :] if isinstance(layer, int) else buf[:, bass.ds(layer, 1), a:z, :]

                def mix_a(s):
                    if s[1] % CHUNKS == 0:
                        layer = s[0] + s[1] // CHUNKS
                        if s[1] == CHUNKS:
                            wait(ex_made, later(s, -1))
                        nc.vector.tensor_copy(pkv_a[:], one(pk, layer, TMK, FIRST + 1)).then_inc(pka_copied, 1)
                        dve.wait_ge(pka_copied, layer * 3 + 1)
                        for b in range(NB):
                            nc.vector.tensor_scalar(wd[:, b, :], reset[:], pkv_a[:, 0, 3, b:b + 1], None, ALU.add
                                                    ).then_inc(pka_copied, 1)
                    if not (isinstance(s[0], int) and CHUNKS * s[0] + s[1] < 2):
                        wait(mixb, later(s, -2))
                    differences(s, h1, t1_out, dh1)
                    wait(a_ready, later(s, -1))
                    for stream in range(3):
                        for b in range(NB):
                            mix(h1, pkv_a, stream, xa[:, stream, b, :], b, mixa)

                def mix_b(s):
                    if s[1] == 0:
                        nc.vector.tensor_copy(pkv_b[:], one(pk, s[0], CMK, CMR + 1)).then_inc(pkb_copied, 1)
                        dve.wait_ge(pkb_copied, s[0] + 1)
                    differences(s, h2, t2_out, dh2)
                    wait(cr_ready, later(s, -1))
                    for stream in range(2):
                        for b in range(NB):
                            mix(h2, pkv_b, stream, xb[:, stream, b, :], b, mixb)

                def scan(s, between=lambda: None):
                    w, u = (lambda b: pkv_a[:, 0, 3, b:b + 1]), (lambda b: pkv_a[:, 0, 4, b:b + 1])
                    layer = s[0] + s[1] // CHUNKS
                    dve.wait_ge(pka_copied, layer * 3 + 3)
                    for b in range(NB):
                        wait(a_out, s, b + 1)
                        nc.vector.tensor_tensor_scan(PP[:, b, :], wd[:, b, :], K[:, b, :], 0.0, ALU.add, ALU.max
                                                     ).then_inc(pp_made.sem, 1)
                    for b in range(NB):
                        wait(pp_made, s, b + 1)
                        nc.vector.scalar_tensor_tensor(out=tok(E[:, 0], b), in0=before(PP, b), scalar=w(b), in1=tok(PP, b),
                                                       op0=ALU.add, op1=ALU.subtract).then_inc(ex_made.sem, 1)
                        nc.vector.tensor_tensor(tok(E[:, 1], b), tok(K, b), tok(PP, b), ALU.subtract).then_inc(ex_made.sem, 1)
                        nc.vector.scalar_tensor_tensor(out=tok(E[:, 2], b), in0=tok(K, b), scalar=u(b), in1=before(PP, b),
                                                       op0=ALU.add, op1=ALU.subtract).then_inc(ex_made.sem, 1)
                    between()
                    for b in range(NB):
                        wait(e_out, s, 3 * b + 2)
                        wait(a_out, s, 3 + b)
                        nc.vector.tensor_tensor(tok(EV, b), tok(E[:, 1], b), tok(V, b), ALU.mult).then_inc(ev_made.sem, 1)
                        nc.vector.tensor_tensor_scan(BB[:, b, :], E[:, 0, b, :], E[:, 1, b, :], 0.0, ALU.mult, ALU.add
                                                     ).then_inc(bb_made.sem, 1)
                        wait(ev_made, s, b + 1)
                        nc.vector.tensor_tensor_scan(AA[:, b, :], E[:, 0, b, :], EV[:, b, :], 0.0, ALU.mult, ALU.add
                                                     ).then_inc(aa_made.sem, 1)
                    wait(e_out, s, 6)
                    th = tok2(E[:, 2])
                    stt = nc.vector.scalar_tensor_tensor
                    wait(bb_made, s, 2)
                    stt(out=tok2(PP), in0=th, scalar=1.0, in1=before2(BB), op0=ALU.add, op1=ALU.mult).then_inc(c1_made.sem, 1)
                    wait(aa_made, s, 2)
                    stt(out=tok2(EV), in0=th, scalar=-1.0, in1=tok2(V), op0=ALU.add, op1=ALU.mult).then_inc(n2_made.sem, 1)
                    wait(c1_made, s)
                    stt(out=tok2(K), in0=th, scalar=1.0, in1=before2(AA), op0=ALU.add, op1=ALU.mult).then_inc(n1_made.sem, 1)
                    stt(out=tok2(PP), in0=tok2(PP), scalar=1.0, in1=th, op0=ALU.add, op1=ALU.subtract).then_inc(den_made.sem, 1)
                    wait(n1_made, s)
                    nc.vector.tensor_tensor(tok2(K), tok2(K), tok2(EV), ALU.subtract).then_inc(nu_made.sem, 1)
                    wait(den_made, s)
                    nc.vector.reciprocal(tok2(BB), tok2(PP)).then_inc(inv_made.sem, 1)
                    wait(a_out, s, 6)
                    wait(nu_made, s)
                    stt(out=tok2(K), in0=tok2(R), scalar=1.0, in1=tok2(K), op0=ALU.add, op1=ALU.mult).then_inc(yr_made.sem, 1)
                    wait(yr_made, s)
                    wait(inv_made, s)
                    wait(wo_ready, later(s, -1))
                    nc.vector.tensor_tensor(ys[:, :, :].rearrange("p b (n t) -> p (b n) t", t=T), tok2(K), tok2(BB),
                                            ALU.mult).then_inc(ys_made.sem, 1)

                def step(s):
                    residual1(s)
                    statistics2(s)
                    if has(s, 2):
                        statistics1(later(s, 2))
                    norm2(s)
                    if has(s, 2):
                        norm1(later(s, 2))
                    mix_b(s)
                    if has(s, 1):
                        scan(later(s, 1), (lambda: mix_a(later(s, 2))) if has(s, 2) else (lambda: None))

                for c in range(2):
                    statistics1((0, c))
                    norm1((0, c))
                    mix_a((0, c))
                scan((0, 0))
                with nc.vector.Fori(0, LAYERS - 1) as l:
                    for c in range(CHUNKS):
                        step((l, c))
                for c in range(CHUNKS):
                    step((LAYERS - 1, c))



def attention(nc, t, X, H0, H2, LG, exp_in, ident, half_neg):
    EPS = 1e-05
    HEADS, HD = 16, 16
    HB = HEADS // NB
    REP = 3
    HG = [(b, h, min(REP, HB - h)) for b in range(NB) for h in range(0, HB, REP)]
    NG = len(HG)
    RK = REP * T
    VC = HD + 1
    PAIRS = CI // 2
    SECOND = 64
    BOTH = SECOND + T
    AUG = 32 + T
    with ExitStack() as ctx:
        def sb(name, shape, dt=F32):
            return ctx.enter_context(nc.sbuf_tensor("at_" + name, shape, dt))

        def psum(name, shape, dt=F32):
            return ctx.enter_context(nc.psum_tensor("at_" + name, shape, dt))

        def made(name, per):
            return Made(ctx.enter_context(nc.semaphore("at_" + name)), per, 1)

        def sem(name):
            return ctx.enter_context(nc.semaphore("at_" + name))

        Wqk = sb("Wqk", [P, 4, NB, D])
        Wv = sb("Wv", [P, NB, D])
        Wp = sb("Wp", [P, NB, D])
        Wg = sb("Wg", [P, NB, 8])
        vec = sb("vec", [P, 4, NB])
        row = sb("row", [P, 2, D])
        cs = sb("cs", [P, 2, T])
        hmask = sb("hmask", [P, NB * HB])
        vmask = sb("vmask", [RK, HEADS])
        negk = sb("negk", [T, HB * T], BF16)
        identb = sb("identb", [P, P], BF16)
        sel = sb("sel", [AUG, NG, RK], BF16)
        st = sb("st", [P, 3, NT, 6])
        mv = sb("mv", [P, 3, NT, 2])
        vr = sb("vr", [P, 3, NT])
        rs = sb("rs", [P, 3, NT])
        S = sb("S", [P, NT, D])
        xn1 = sb("xn1", [P, NT, D])
        xn2 = sb("xn2", [P, NT, D])
        H2a = sb("H2a", [P, NT, D])
        h1 = sb("h1", [P, NB, CT])
        h2 = sb("h2", [P, NB, CT])
        rot = sb("rot", [P, 2, 2, HALF])
        QK = sb("QK", [P, 2, NB, CT])
        kbd = sb("kbd", [P, 2, 2, NB, HB, T])
        hr = sb("hr", [P, 2, 2, NB, RK])
        vbd = sb("vbd", [RK, 2, 2, HEADS, VC])
        mx = sb("mx", [P, 2, HEADS], BF16)
        aug = sb("aug", [AUG, 2, 2 * T], BF16)
        PT = sb("PT", [RK, 2, 2, NG * T])
        inv = sb("inv", [P, 2, HEADS])
        O = sb("O", [P, 2, D])
        aT = sb("aT", [P, NB, CT])
        zeros = sb("zeros", [P, 2 * N // CHUNKS // P * D])
        zero_rows = sem("zero_rows")
        exp_zeroed = sem("exp_zeroed")
        ps_a = psum("ps_a", [P, 4, 512])
        ps_st = psum("ps_st", [P, 512])
        ps_o = psum("ps_o", [P, 512])
        ps_v = psum("ps_v", [P, 512])
        ps_x = psum("ps_x", [P, 512])
        ps_mT = ps_a[:, 0, 0:64].bitcast(BF16)
        ps_oT = ps_x[:, 128:128 + 2 * BOTH]

        w_in = sem("w_in")
        const = sem("const")
        carrier = sem("carrier")
        zero = sem("zero")
        summed = made("summed", NT)
        st_made = made("st_made", 3)
        mv_made = made("mv_made", 3)
        h0_made = made("h0_made", NT)
        xn1_made = made("xn1_made", NT)
        rot_made = made("rot_made", 16)
        v_out = made("v_out", 2 * PAIRS)
        mx_made = made("mx_made", PAIRS)
        inv_made = made("inv_made", PAIRS)
        o_made = made("o_made", PAIRS)
        x_made = made("x_made", NT)
        xn2_made = made("xn2_made", NT)
        ve = made("ve", 3)
        rs_made = made("rs_made", 3)
        rope = made("rope", 8)
        kbd_made = made("kbd_made", 2 * PAIRS)
        h2_scaled = made("h2_scaled", NT)
        h2_made = made("h2_made", NT)
        t1_ready = made("t1_ready", len(GROUPS))
        qk_ready = made("qk_ready", 8)
        v_ready = made("v_ready", PAIRS)
        s_ready = made("s_ready", PAIRS)
        mT_ready = made("mT_ready", PAIRS)
        st_ready = made("st_ready", PAIRS)
        o_ready = made("o_ready", PAIRS)
        oT_ready = made("oT_ready", PAIRS)
        p_ready = made("p_ready", NT)
        t2_ready = made("t2_ready", len(GROUPS))
        lg_ready = made("lg_ready", NT)
        t1_out = made("t1_out", 2 * len(GROUPS))
        hr_made = made("hr_made", 2 * PAIRS)
        mT_out = made("mT_out", PAIRS)
        e_out = made("e_out", PAIRS)
        oT_out = made("oT_out", PAIRS)
        t2_out = made("t2_out", 2 * len(GROUPS))
        lg_out = made("lg_out", 2)

        def credit(eng, *sems):
            for s in sems:
                eng.sem_inc(s.sem, s.per)

        combos = [(x, b, h) for x in range(2) for b in range(NB) for h in range(2)]

        with nc.Block() as block:
            @block.sync
            def _(sp):
                for dst, name in ((Wqk, "Wqk"), (Wv, "Wv"), (Wp, "Wproj"), (Wg, "Wgate"), (vec, "ffn_vec"), (row, "ffn_rows"),
                                  (cs, "cos_sin"), (hmask, "head_mask"), (vmask, "value_mask"), (negk, "causal"),
                                  (identb, "identb"), (sel, "select")):
                    nc.sync.dma_start(dst[:], t[name]).then_inc(w_in, 16)
                for p in range(2):
                    for i in range(2):
                        nc.sync.dma_start(aug[32:AUG, p, i * T:(i + 1) * T], t["causalT"]).then_inc(w_in, 16)
                sp.wait_ge(zero_rows, 1)
                for part in range(CHUNKS):
                    rows = exp_in[part * (2 * N // CHUNKS):(part + 1) * (2 * N // CHUNKS), :]
                    nc.sync.dma_start(rows.rearrange("(p r) d -> p (r d)", p=P), zeros[:]).then_inc(exp_zeroed, 16)
                sp.wait_ge(exp_zeroed, 16 * CHUNKS)
            LOADS = 16 * (12 + 4)

            @block.gpsimd
            def _(pool):
                wait = lambda m, s, j=None: pool.wait_ge(m.sem, m.at(s, j))
                nc.gpsimd.memset(zeros[:], 0.0).then_inc(zero_rows, 1)
                nc.gpsimd.memset(mv[:], 1.0).then_inc(const, 1)
                nc.gpsimd.memset(LG[:], 0.0).then_inc(const, 1)
                nc.gpsimd.memset(aug[0:32, :, :], 0.0).then_inc(const, 1)
                credit(pool, ve, rs_made, rope, kbd_made, h2_scaled, h2_made)
                pool.wait_ge(w_in, LOADS)
                pool.wait_ge(const, 3)

                def root(s, k):
                    wait(mv_made, s, k + 1)
                    pool.sem_inc(carrier, 1)
                    nc.gpsimd.tensor_scalar(vr[:, k, :], mv[:, k, :, 1], 1.0, EPS, ALU.mult, ALU.add).then_inc(ve.sem, 1)
                    wait(ve, s, k + 1)
                    nc.gpsimd.tensor_tensor(rs[:, k, :], vr[:, k, :], half_neg[:, 0:NT], ALU.pow).then_inc(rs_made.sem, 1)

                with nc.gpsimd.Fori(0, CHUNKS) as n:
                    s = (n, 0)
                    root(s, 0)
                    root(s, 1)
                    for j, (x, b, h) in enumerate(combos):
                        wait(rot_made, s, 2 * j + 2)
                        if j == 0:
                            wait(st_ready, later(s, -1))
                        nc.gpsimd.tensor_tensor(QK[:, x, b, h * HALF:(h + 1) * HALF], rot[:, j % 2, 0, :], rot[:, j % 2, 1, :],
                                                ALU.add).then_inc(rope.sem, 1)
                    wait(rope, s)
                    for p in range(PAIRS):
                        if p >= 2:
                            wait(st_ready, s, p - 1)
                        for i in range(2):
                            first = (2 * p + i) * T
                            for b in range(NB):
                                k = QK[:, 1, b:b + 1, first:first + T].to_broadcast([P, HB, T])
                                m = hmask[:, b * HB:(b + 1) * HB].rearrange("p (h a) -> p h a", a=1).to_broadcast([P, HB, T])
                                a = nc.gpsimd.tensor_tensor(kbd[:, p % 2, i, b, :, :], k, m, ALU.mult)
                            a.then_inc(kbd_made.sem, 1)
                    root(s, 2)
                    for i, (_, r) in enumerate(TILES):
                        wait(xn2_made, s, i + 1)
                        nc.gpsimd.tensor_tensor(H2a[0:r, i, :], xn2[0:r, i, :], row[0:r, 0, :], ALU.mult).then_inc(h2_scaled.sem, 1)
                    for i, (_, r) in enumerate(TILES):
                        wait(h2_scaled, s, i + 1)
                        nc.gpsimd.tensor_tensor(H2[0:r, bass.ds(n * NT + i, 1), :], H2a[0:r, i:i + 1, :], row[0:r, 1:2, :], ALU.add
                                                ).then_inc(h2_made.sem, 1)

            @block.tensor
            def _(pe):
                wait = lambda m, s, j=None: pe.wait_ge(m.sem, m.at(s, j))
                credit(pe, t1_ready, qk_ready, v_ready, s_ready, mT_ready, st_ready, o_ready, oT_ready, p_ready, t2_ready,
                       lg_ready)
                pe.wait_ge(w_in, LOADS)
                pe.wait_ge(const, 3)
                pe.wait_ge(zero, 7)

                def transposes(xn, made_, ready, free, s):
                    for q, tiles in enumerate(GROUPS):
                        wait(made_, s, tiles[-1] + 1)
                        free(q)
                        if TILES[tiles[0]][1] < P:
                            pe.sem_inc(carrier, 1)
                        width = sum(TILES[i][1] for i in tiles)
                        for i in tiles:
                            r = TILES[i][1]
                            at = TILES[i][0] - TILES[tiles[0]][0]
                            for b in range(NB):
                                a = nc.tensor.transpose(ps_a[:, q % 2, b * width + at:b * width + at + r],
                                                        xn[0:r, i, b * P:(b + 1) * P], ident[0:r, 0:r])
                        a.then_inc(ready.sem, 1)

                def queries_keys(s):
                    wait(t1_out, s)
                    for j, (x, b, h) in enumerate(combos):
                        if j == 1:
                            wait(mx_made, later(s, -1))
                        if j >= 2:
                            wait(rot_made, s, 2 * j - 2)
                        for v in range(2):
                            for kb in range(NB):
                                a = nc.tensor.matmul(ps_a[:, 2 * (j % 2) + v, 0:HALF], Wqk[:, 2 * x + v, kb, b * P:(b + 1) * P],
                                                     h1[:, kb, h * HALF:(h + 1) * HALF], start=(kb == 0), stop=(kb == NB - 1))
                        a.then_inc(qk_ready.sem, 1)

                def values_scores(s, p):
                    if p >= 1:
                        wait(v_out, s, 2 * p)
                    else:
                        wait(v_out, later(s, -1))
                    wait(hr_made, s, 2 * p + 2)
                    for i in range(2):
                        for kb in range(NB):
                            a = nc.tensor.matmul(ps_v[0:RK, i * D:(i + 1) * D], hr[:, p % 2, i, kb, :], Wv[:, kb, :],
                                                 start=(kb == 0), stop=(kb == NB - 1))
                    a.then_inc(v_ready.sem, 1)
                    wait(kbd_made, s, 2 * p + 2)
                    if p >= 1:
                        wait(mx_made, s, p)
                    else:
                        wait(rot_made, s)
                    for i in range(2):
                        first = (2 * p + i) * T
                        for b in range(NB):
                            dst = ps_a[SECOND * i:SECOND * i + T, 2 + b, 0:HB * T].rearrange("p (h k) -> p h k", k=T)
                            nc.tensor.matmul(dst, QK[:, 0, b, first:first + T], kbd[:, p % 2, i, b, :, :],
                                             start=True, stop=False)
                            a = nc.tensor.matmul(dst, identb[0:T, 0:T], negk[:, :].rearrange("p (h k) -> p h k", k=T),
                                                 start=False, stop=True)
                    a.then_inc(s_ready.sem, 1)

                def maxima(s, p):
                    wait(mx_made, s, p + 1)
                    if p >= 1:
                        wait(mT_out, s, p)
                    nc.tensor.transpose(ps_mT[0:HEADS, 0:BOTH], mx[0:BOTH, p % 2, :], identb[0:BOTH, 0:BOTH]
                                        ).then_inc(mT_ready.sem, 1)

                def scores_transposed(s, p):
                    wait(mT_out, s, p + 1)
                    wait(e_out, s, p) if p >= 1 else wait(e_out, later(s, -1))
                    for i in range(2):
                        first = (2 * p + i) * T
                        for g, (b, h, m) in enumerate(HG):
                            dst = ps_st[0:m * T, (i * NG + g) * T:(i * NG + g + 1) * T]
                            nc.tensor.matmul(dst, kbd[:, p % 2, i, b, h:h + m, :].rearrange("p h k -> p (h k)"), QK[:, 0, b, first:first + T],
                                             start=True, stop=False)
                            a = nc.tensor.matmul(dst, sel[:, g, 0:m * T], aug[:, p % 2, i * T:(i + 1) * T], start=False, stop=True)
                    a.then_inc(st_ready.sem, 1)

                def outputs(s, p):
                    wait(e_out, s, p + 1)
                    wait(v_out, s, 2 * p + 2)
                    wait(o_made, s, p) if p >= 1 else wait(o_made, later(s, -1))
                    for i in range(2):
                        for g, (b, h, m) in enumerate(HG):
                            h0 = b * HB + h
                            a = nc.tensor.matmul(ps_o[SECOND * i:SECOND * i + T, h0 * VC:(h0 + m) * VC],
                                                 PT[0:m * T, p % 2, i, g * T:(g + 1) * T],
                                                 vbd[0:m * T, p % 2, i, h0:h0 + m, :].rearrange("p h v -> p (h v)"),
                                                 start=True, stop=True)
                    a.then_inc(o_ready.sem, 1)

                def outputs_transposed(s, p):
                    wait(o_made, s, p + 1)
                    wait(oT_out, s, p) if p >= 1 else wait(oT_out, later(s, -1))
                    for b in range(NB):
                        a = nc.tensor.transpose(ps_oT[:, b * BOTH:(b + 1) * BOTH], O[0:BOTH, p % 2, b * P:(b + 1) * P],
                                                ident[0:BOTH, 0:BOTH])
                    a.then_inc(oT_ready.sem, 1)

                with nc.tensor.Fori(0, CHUNKS) as n:
                    s = (n, 0)

                    def free1(q):
                        if q < 2:
                            wait(lg_out, later(s, -1))
                        else:
                            wait(t1_out, s, 2)
                    transposes(xn1, xn1_made, t1_ready, free1, s)
                    queries_keys(s)
                    for k in range(PAIRS + 2):
                        if k >= 2:
                            outputs(s, k - 2)
                        if 1 <= k <= PAIRS:
                            maxima(s, k - 1)
                        if k < PAIRS:
                            values_scores(s, k)
                        if k >= 2:
                            outputs_transposed(s, k - 2)
                        if 1 <= k <= PAIRS:
                            scores_transposed(s, k - 1)
                    wait(oT_out, s)
                    wait(mT_out, s)
                    for i, (first, r) in enumerate(TILES):
                        if i >= 2:
                            wait(x_made, s, i - 1)
                        for b in range(NB):
                            a = nc.tensor.matmul(ps_a[0:r, i % 2, 0:D], aT[:, b, first:first + r], Wp[:, b, :], start=(b == 0),
                                                 stop=(b == NB - 1))
                        a.then_inc(p_ready.sem, 1)
                    transposes(xn2, xn2_made, t2_ready,
                               lambda q: wait(x_made, s) if q < 2 else wait(t2_out, s, 2), s)
                    wait(t2_out, s)
                    for i, (first, r) in enumerate(TILES):
                        for b in range(NB):
                            a = nc.tensor.matmul(ps_a[0:r, 1, 8 * i:8 * i + 8], h2[:, b, first:first + r], Wg[:, b, :],
                                                 start=(b == 0), stop=(b == NB - 1))
                        a.then_inc(lg_ready.sem, 1)

            @block.scalar
            def _(act):
                wait = lambda m, s, j=None: act.wait_ge(m.sem, m.at(s, j))
                credit(act, t1_out, hr_made, mT_out, e_out, oT_out, t2_out, lg_out)
                act.wait_ge(w_in, LOADS)
                act.wait_ge(const, 3)
                act.wait_ge(zero, 7)

                def evict(ready, h, k, out_, s):
                    for q, tiles in enumerate(GROUPS):
                        width = sum(TILES[i][1] for i in tiles)
                        first = TILES[tiles[0]][0]
                        wait(ready, s, q + 1)
                        for b in range(NB):
                            nc.scalar.activation(h[:, b, first:first + width], ps_a[:, q % 2, b * width:(b + 1) * width],
                                                 ACT.Identity, bias=vec[:, k + 1, b:b + 1], scale=vec[:, k, b:b + 1]
                                                 ).then_inc(out_.sem, 1)

                with nc.scalar.Fori(0, CHUNKS) as n:
                    s = (n, 0)
                    wait(v_ready, later(s, -1))
                    evict(t1_ready, h1, 0, t1_out, s)

                    def repeated(p):
                        if p == 0:
                            wait(t1_out, s)
                        if p >= 2:
                            wait(v_ready, s, p - 1)
                        for i in range(2):
                            first = (2 * p + i) * T
                            src = h1[:, :, first:first + T].rearrange("p b (a t) -> p b a t", a=1)
                            nc.scalar.activation(hr[:, p % 2, i, :, :].rearrange("p b (a t) -> p b a t", t=T),
                                                 src.to_broadcast([P, NB, REP, T]), ACT.Copy).then_inc(hr_made.sem, 1)

                    def maxima(p):
                        wait(mT_ready, s, p + 1)
                        wait(st_ready, s, p - 1) if p >= 2 else wait(st_ready, later(s, -1))
                        nc.scalar.activation(aug[0:HEADS, p % 2, :].rearrange("p (i q) -> p i q", i=2),
                                             ps_mT[0:HEADS, 0:2 * SECOND].rearrange("p (i q) -> p i q", i=2)[:, :, 0:T],
                                             ACT.Copy).then_inc(mT_out.sem, 1)

                    def exponentials(p):
                        wait(st_ready, s, p + 1)
                        wait(o_ready, s, p - 1) if p >= 2 else wait(o_ready, later(s, -1))
                        nc.scalar.activation(PT[:, p % 2, :, :], ps_st[0:RK, 0:2 * NG * T].rearrange("p (i x) -> p i x", i=2),
                                             ACT.Exp, scale=float(HD) ** -0.5).then_inc(e_out.sem, 1)

                    def transposed(p):
                        wait(oT_ready, s, p + 1)
                        if p == 0:
                            wait(p_ready, later(s, -1))
                        for b in range(NB):
                            src = ps_oT[:, b * BOTH:b * BOTH + BOTH]
                            for i in range(2):
                                a = nc.scalar.activation(aT[:, b, (2 * p + i) * T:(2 * p + i + 1) * T],
                                                         src[:, SECOND * i:SECOND * i + T], ACT.Copy)
                        a.then_inc(oT_out.sem, 1)

                    repeated(0)
                    for k in range(PAIRS + 2):
                        if k + 1 < PAIRS:
                            repeated(k + 1)
                        if 1 <= k <= PAIRS:
                            maxima(k - 1)
                        if k >= 2:
                            transposed(k - 2)
                        if 1 <= k <= PAIRS:
                            exponentials(k - 1)
                    wait(lg_ready, later(s, -1))
                    evict(t2_ready, h2, 2, t2_out, s)
                    wait(lg_ready, s)
                    for first, tiles, r in ((0, NT - 1, P), (NT - 1, 1, TILES[-1][1])):
                        nc.scalar.activation(LG[0:r, bass.ds(n * NT + first, tiles), :],
                                             ps_a[0:r, 1, 8 * first:8 * (first + tiles)].rearrange("p (i e) -> p i e", e=8),
                                             ACT.Copy).then_inc(lg_out.sem, 1)

            @block.vector
            def _(dve):
                wait = lambda m, s, j=None: dve.wait_ge(m.sem, m.at(s, j))
                nc.vector.memset(ps_a[:], 0.0).then_inc(zero, 1)
                nc.vector.memset(ps_st[:], 0.0).then_inc(zero, 1)
                nc.vector.memset(ps_o[:], 1.0).then_inc(zero, 1)
                credit(dve, summed, st_made, mv_made, h0_made, xn1_made, rot_made, v_out, mx_made, inv_made, o_made, x_made,
                       xn2_made)
                dve.wait_ge(w_in, LOADS)
                dve.wait_ge(const, 3)
                for p in range(2):
                    for i in range(2):
                        nc.vector.tensor_copy(vbd[:, p, i, :, HD:VC], vmask[:, :].rearrange("p (h a) -> p h a", a=1)
                                              ).then_inc(zero, 1)
                dve.wait_ge(zero, 7)

                def stats(s, k, src, ready):
                    for i, (_, r) in enumerate(TILES):
                        wait(ready, s, i + 1)
                        dve.sem_inc(carrier, 1)
                        a = nc.vector.bn_stats(st[0:r, k, i, :], src(i, r))
                    a.then_inc(st_made.sem, 1)
                    wait(st_made, s, k + 1)
                    dve.sem_inc(carrier, 1)
                    for i, (_, r) in enumerate(TILES):
                        a = nc.vector.bn_aggr(mv[0:r, k, i, :], st[0:r, k, i, :])
                    a.then_inc(mv_made.sem, 1)
                    wait(mv_made, s, k + 1)
                    wait(rs_made, s, k + 1)

                with nc.vector.Fori(0, CHUNKS) as n:
                    s = (n, 0)
                    tile = lambda i: bass.ds(n * NT + i, 1)
                    for i, (_, r) in enumerate(TILES):
                        nc.vector.tensor_tensor(S[0:r, i:i + 1, :], X[0:r, tile(i), :], H0[0:r, tile(i), :], ALU.add
                                                ).then_inc(summed.sem, 1)
                    stats(s, 0, lambda i, r: S[0:r, i, :], summed)
                    for i, (_, r) in enumerate(TILES):
                        nc.vector.tensor_scalar(H0[0:r, tile(i), :], S[0:r, i:i + 1, :], mv[0:r, 0, i, 0:1], rs[0:r, 0, i:i + 1],
                                                ALU.subtract, ALU.mult).then_inc(h0_made.sem, 1)
                    stats(s, 1, lambda i, r: H0[0:r, tile(i), :], h0_made)
                    wait(t1_ready, later(s, -1))
                    for i, (_, r) in enumerate(TILES):
                        nc.vector.tensor_scalar(xn1[0:r, i:i + 1, :], H0[0:r, tile(i), :], mv[0:r, 1, i, 0:1],
                                                rs[0:r, 1, i:i + 1], ALU.subtract, ALU.mult).then_inc(xn1_made.sem, 1)
                    for j in range(8):
                        wait(qk_ready, s, j + 1)
                        wait(rope, s, j - 1) if j >= 2 else wait(rope, later(s, -1))
                        for v in range(2):
                            nc.vector.tensor_tensor(rot[:, j % 2, v, :].rearrange("p (n t) -> p n t", t=T),
                                                    ps_a[:, 2 * (j % 2) + v, 0:HALF].rearrange("p (n t) -> p n t", t=T),
                                                    cs[:, v:v + 1, :].to_broadcast([P, CI // 2, T]), ALU.mult
                                                    ).then_inc(rot_made.sem, 1)

                    def values(p):
                        wait(v_ready, s, p + 1)
                        wait(o_ready, s, p - 1) if p >= 2 else wait(o_ready, later(s, -1))
                        m = vmask[:, :].rearrange("p (h a) -> p h a", a=1).to_broadcast([RK, HEADS, HD])
                        for i in range(2):
                            nc.vector.tensor_tensor(vbd[:, p % 2, i, :, 0:HD],
                                                    ps_v[0:RK, i * D:(i + 1) * D].rearrange("p (h v) -> p h v", v=HD), m, ALU.mult
                                                    ).then_inc(v_out.sem, 1)

                    def maxima(p):
                        wait(s_ready, s, p + 1)
                        wait(mT_ready, s, p - 1) if p >= 2 else wait(mT_ready, later(s, -1))
                        nc.vector.tensor_reduce(mx[0:BOTH, p % 2, :].rearrange("p (b h) -> p b h", b=NB),
                                                ps_a[0:BOTH, 2:4, 0:HB * T].rearrange("p b (h k) -> p b h k", k=T), AX.X, ALU.max
                                                ).then_inc(mx_made.sem, 1)

                    def normalise(p):
                        wait(o_ready, s, p + 1)
                        o = ps_o[0:BOTH, 0:HEADS * VC].rearrange("p (h v) -> p h v", v=VC)
                        nc.vector.reciprocal(inv[0:BOTH, p % 2, :].rearrange("p (h a) -> p h a", a=1), o[:, :, HD:VC]
                                             ).then_inc(inv_made.sem, 1)
                        wait(inv_made, s, p + 1)
                        wait(oT_ready, s, p - 1) if p >= 2 else wait(oT_ready, later(s, -1))
                        nc.vector.tensor_tensor(O[0:BOTH, p % 2, :].rearrange("p (h v) -> p h v", v=HD), o[:, :, 0:HD],
                                                inv[0:BOTH, p % 2, :].rearrange("p (h a) -> p h a", a=1
                                                                                ).to_broadcast([BOTH, HEADS, HD]), ALU.mult
                                                ).then_inc(o_made.sem, 1)

                    for k in range(PAIRS + 2):
                        if k >= 2:
                            normalise(k - 2)
                        if k < PAIRS:
                            values(k)
                            maxima(k)
                    for i, (_, r) in enumerate(TILES):
                        wait(p_ready, s, i + 1)
                        nc.vector.tensor_tensor(X[0:r, tile(i), :], ps_a[0:r, i % 2:i % 2 + 1, 0:D], H0[0:r, tile(i), :], ALU.add
                                                ).then_inc(x_made.sem, 1)
                    stats(s, 2, lambda i, r: X[0:r, tile(i), :], x_made)
                    wait(t2_ready, later(s, -1))
                    wait(h2_scaled, later(s, -1))
                    for i, (_, r) in enumerate(TILES):
                        nc.vector.tensor_scalar(xn2[0:r, i:i + 1, :], X[0:r, tile(i), :], mv[0:r, 2, i, 0:1],
                                                rs[0:r, 2, i:i + 1], ALU.subtract, ALU.mult).then_inc(xn2_made.sem, 1)


def ffn_arrays(a, blocks):
    import numpy as np

    F = "L0_ffn_"
    hb, hd, rep = 8, 16, 3
    bf16 = mybir.dt.np(BF16)
    w = a[F + "Wqkv"].reshape(D, 16, 3, hd)
    q, k, v = (w[:, :, i] for i in range(3))
    swap = lambda m: np.concatenate([m[..., hd // 2:], m[..., :hd // 2]], -1)
    rows = lambda m: m.reshape(NB, P, -1).transpose(1, 0, 2)
    freq = (1.0 / 10000.0 ** (np.arange(0, hd, 2, dtype=np.float32) / np.float32(hd))).astype(np.float32)
    ang = np.arange(T, dtype=np.float32)[:, None] * freq
    cos, sin = np.cos(ang).astype(np.float32).T, np.sin(ang).astype(np.float32).T
    cs = np.stack([np.tile(np.concatenate([cos, cos]), (hb, 1)), np.tile(np.concatenate([-sin, sin]), (hb, 1))], 1)
    head = np.arange(P) // hd
    rep_of = (np.arange(16) % hb) % rep
    groups = [(b, h, min(rep, hb - h)) for b in range(NB) for h in range(0, hb, rep)]
    sel = np.zeros((32 + T, len(groups), rep * T), np.float32)
    for g, (b, h, m) in enumerate(groups):
        for r in range(m):
            sel[b * hb + h + r, g, r * T:(r + 1) * T] = -1
            sel[32 + np.arange(T), g, r * T + np.arange(T)] = 1
    later_key = np.where(np.arange(T)[None, :] > np.arange(T)[:, None], np.float32(-1e30), np.float32(0))
    return {
        "Wqk": np.stack([rows(np.ascontiguousarray(m).reshape(D, D)) for m in (q, swap(q), k, swap(k))], 1),
        "Wv": rows(v.reshape(D, D)),
        "Wproj": rows(a[F + "Wproj"]),
        "Wgate": rows(a[F + "Wgate"]),
        "ffn_vec": np.stack([blocks(a[F + n]) for n in ("ln1_g", "ln1_b", "ln2_g", "ln2_b")], 1),
        "ffn_rows": np.broadcast_to(np.stack([a[F + "ln2_g"], a[F + "ln2_b"]]), (P, 2, D)),
        "cos_sin": cs,
        "head_mask": np.tile((head[:, None] == np.arange(hb)[None, :]).astype(np.float32), (1, NB)),
        "value_mask": (np.arange(rep * T)[:, None] // T == rep_of[None, :]).astype(np.float32),
        "causal": np.tile(later_key, (1, hb)).astype(bf16),
        "causalT": later_key.T.astype(bf16),
        "identb": np.eye(P).astype(bf16),
        "select": sel.astype(bf16),
    }


def experts(nc, t, X, H0, H2, LG, exp_in, exp_out, out):
    EPS = 1e-05
    E = 8
    CAPACITY = CT
    assert CAPACITY == 2 * N // E
    TT = CHUNKS * NT
    with ExitStack() as ctx:
        def sb(name, shape, dt=F32):
            return ctx.enter_context(nc.sbuf_tensor("ex_" + name, shape, dt))

        def sem(name):
            return ctx.enter_context(nc.semaphore("ex_" + name))

        iota8 = sb("iota8", [P, E])
        absent = sb("absent", [P, TT, 2])
        carry = sb("carry", [P, E, TT])
        spare = sb("spare", [P, 2, TT])
        upto = sb("upto", [P, P], BF16)
        ones = sb("ones", [P, P], BF16)
        top = sb("top", [P, TT])
        ex = sb("ex", [P, TT, E])
        total = sb("total", [P, TT])
        inv = sb("inv", [P, TT])
        gates = sb("gates", [P, TT, E])
        best = sb("best", [P, TT, 8])
        which = sb("which", [P, TT, 8], mybir.dt.uint32)
        who = sb("who", [P, TT, 2])
        chosen = sb("chosen", [P, 2, E, TT])
        mask = sb("mask", [P, E, TT])
        maskb = sb("maskb", [P, E, TT], BF16)
        upto_tile = sb("upto_tile", [P, E, TT])
        before = sb("before", [P, E, TT], BF16)
        place = sb("place", [P, 2, E, TT])
        pos = sb("pos", [P, 2, TT])
        keep = sb("keep", [P, 2, TT])
        slot = sb("slot", [P, 2, TT])
        gate = sb("gate", [P, 2, TT])
        dst = sb("dst", [P, 2, TT])
        src = sb("src", [P, 2, TT])
        dst_i = sb("dst_i", [P, 2, TT], mybir.dt.uint32)
        src_i = sb("src_i", [P, 2, TT], mybir.dt.uint32)
        c_in = sem("c_in")
        d = sem("d")
        logits_exp = sem("logits_exp")
        masks_made = sem("masks_made")
        counted = sem("counted")
        scattered = sem("scattered")

        with nc.psum_tensor("ex_ps_pos", [P, 512], F32) as ps_pos, nc.Block() as block:
            @block.sync
            def _(sp):
                for buf, name in ((iota8, "iota8"), (absent, "absent"), (carry, "carry"), (spare, "spare"), (upto, "upto"),
                                  (ones, "onesb")):
                    nc.sync.dma_start(buf[:], t[name]).then_inc(c_in, 16)

            count = [0]

            @block.vector
            def _(dve):
                def then(ins):
                    count[0] += 1
                    ins.then_inc(d, 1)
                    dve.wait_ge(d, count[0])

                V = nc.vector
                by_e = lambda x: x.rearrange("p (n a) -> p n a", a=1).to_broadcast([P, TT, E])
                dve.wait_ge(c_in, 96)
                then(V.tensor_reduce(top[:], LG[:], AX.X, ALU.max))
                then(V.tensor_tensor(ex[:], LG[:], by_e(top[:]), ALU.subtract))
                dve.wait_ge(logits_exp, 1)
                then(V.tensor_reduce(total[:], ex[:], AX.X, ALU.add))
                then(V.reciprocal(inv[:], total[:]))
                then(V.tensor_tensor(gates[:], ex[:], by_e(inv[:]), ALU.mult))
                for i in range(TT):
                    a = V.max(best[:, i, :], gates[:, i, :])
                then(a)
                for i in range(TT):
                    a = V.max_index(which[:, i, :], best[:, i, :], gates[:, i, :])
                then(a)
                then(V.tensor_copy(who[:], which[:, :, 0:2]))
                then(V.tensor_tensor(who[:], who[:], absent[:], ALU.add))
                for k in range(2):
                    a = V.tensor_tensor(chosen[:, k], iota8[:].rearrange("p (e a) -> p e a", a=1).to_broadcast([P, E, TT]),
                                        who[:, :, k:k + 1].rearrange("p n a -> p a n").to_broadcast([P, E, TT]), ALU.is_equal)
                then(a)
                then(V.tensor_tensor(mask[:], chosen[:, 0], chosen[:, 1], ALU.add))
                flat = lambda x: x.rearrange("p e n -> p (e n)")
                V.tensor_copy(maskb[:], mask[:])
                then(V.tensor_tensor_scan(flat(upto_tile[:]), flat(carry[:]), flat(mask[:]), 0.0, ALU.mult, ALU.add))
                V.tensor_tensor(before[:], upto_tile[:], mask[:], ALU.subtract).then_inc(masks_made, 1)
                dve.wait_ge(counted, 1)
                for k in range(2):
                    a = V.tensor_tensor(place[:, k], ps_pos[:, 0:E * TT].rearrange("p (e n) -> p e n", e=E), chosen[:, k], ALU.mult)
                then(a)
                for k in range(2):
                    a = V.tensor_reduce(pos[:, k, :], place[:, k].rearrange("p e n -> p n e"), AX.X, ALU.add)
                then(a)
                V.tensor_scalar(keep[:], pos[:], float(CAPACITY), None, ALU.is_le)
                then(V.scalar_tensor_tensor(out=slot[:], in0=who[:].rearrange("p n k -> p k n"), scalar=float(CAPACITY), in1=pos[:],
                                            op0=ALU.mult, op1=ALU.add))
                then(V.tensor_scalar(slot[:], slot[:], -1.0, None, ALU.add))
                V.tensor_tensor(dst[:], slot[:], spare[:], ALU.subtract)
                V.tensor_tensor(gate[:], best[:, :, 0:2].rearrange("p n k -> p k n"), keep[:], ALU.mult)
                then(V.tensor_tensor(src[:], slot[:], keep[:], ALU.mult))
                then(V.tensor_tensor(dst[:], dst[:], keep[:], ALU.mult))
                then(V.tensor_tensor(dst[:], dst[:], spare[:], ALU.add))
                V.tensor_copy(src_i[:], src[:])
                then(V.tensor_copy(dst_i[:], dst[:]))
            INDICES = count[0]

            @block.scalar
            def _(act):
                act.wait_ge(d, 2)
                nc.scalar.activation(ex[:], ex[:], ACT.Exp).then_inc(logits_exp, 1)

            @block.tensor
            def _(pe):
                pe.wait_ge(masks_made, 1)
                nc.tensor.matmul(ps_pos[:, 0:E * TT], upto[:], maskb[:].rearrange("p e n -> p (e n)"), start=True, stop=False)
                nc.tensor.matmul(ps_pos[:, 0:E * TT], ones[:], before[:].rearrange("p e n -> p (e n)"), start=False, stop=True
                                 ).then_inc(counted, 1)

            @block.gpsimd
            def _(pool):
                pool.wait_ge(d, INDICES)
                for k in range(2):
                    for i in range(TT):
                        r = TILES[i % NT][1]
                        nc.gpsimd.indirect_dma_start(out=exp_in, out_offset=bass.IndirectOffsetOnAxis(ap=dst_i[0:r, k, i:i + 1], axis=0),
                                                     in_=H2[0:r, i, :], in_offset=None).then_inc(scattered, 16)
                pool.wait_ge(scattered, 16 * 2 * TT)

        expert_products(nc, t, exp_in, exp_out)

        got = sb("got", [P, TT, 2, D])
        S = sb("S", [P, TT, D])
        st = sb("st", [P, TT, 6])
        mv = sb("mv", [P, TT, 2])
        vr = sb("vr", [P, TT])
        rs = sb("rs", [P, TT])
        y = sb("y", [P, TT, D])
        gathered = sem("gathered")
        added = sem("added")
        first_added = sem("first_added")
        both_added = sem("both_added")
        st_made = sem("st_made")
        mv_made = sem("mv_made")
        ve = sem("ve")
        rs_made = sem("rs_made")
        y_made = sem("y_made")
        stored = sem("stored")
        ones_in = sem("ones_in")
        with nc.Block() as block:
            @block.gpsimd
            def _(pool):
                nc.gpsimd.memset(mv[:], 1.0).then_inc(ones_in, 1)
                nc.gpsimd.memset(keep[:], -0.5).then_inc(ones_in, 1)
                for i in range(TT):
                    r = TILES[i % NT][1]
                    for k in range(2):
                        nc.gpsimd.indirect_dma_start(out=got[0:r, i, k, :], out_offset=None, in_=exp_out,
                                                     in_offset=bass.IndirectOffsetOnAxis(ap=src_i[0:r, k, i:i + 1], axis=0)
                                                     ).then_inc(gathered, 16)
                pool.wait_ge(ones_in, 2)
                for c in range(CHUNKS):
                    part = slice(c * NT, (c + 1) * NT)
                    pool.wait_ge(mv_made, c + 1)
                    nc.gpsimd.tensor_scalar(vr[:, part], mv[:, part, 1], 1.0, EPS, ALU.mult, ALU.add).then_inc(ve, 1)
                    pool.wait_ge(ve, c + 1)
                    nc.gpsimd.tensor_tensor(rs[:, part], vr[:, part], keep[:, 0, 0:NT], ALU.pow).then_inc(rs_made, 1)

            @block.vector
            def _(dve):
                V = nc.vector
                dve.wait_ge(ones_in, 2)
                for c in range(CHUNKS):
                    tiles = [(c * NT + i, r) for i, (_, r) in enumerate(TILES)]
                    for i, r in tiles:
                        V.tensor_tensor(S[0:r, i, :], X[0:r, i, :], H0[0:r, i, :], ALU.add).then_inc(added, 1)
                    for k, (before_, after) in enumerate(((added, first_added), (first_added, both_added))):
                        for i, r in tiles:
                            dve.wait_ge(before_, i + 1)
                            dve.wait_ge(gathered, 16 * 2 * TT)
                            V.scalar_tensor_tensor(out=S[0:r, i, :], in0=got[0:r, i, k, :], scalar=gate[0:r, k, i:i + 1],
                                                   in1=S[0:r, i, :], op0=ALU.mult, op1=ALU.add).then_inc(after, 1)
                    for i, r in tiles:
                        dve.wait_ge(both_added, i + 1)
                        a = V.bn_stats(st[0:r, i, :], S[0:r, i, :])
                    a.then_inc(st_made, 1)
                    dve.wait_ge(st_made, c + 1)
                    for i, r in tiles:
                        a = V.bn_aggr(mv[0:r, i, :], st[0:r, i, :])
                    a.then_inc(mv_made, 1)
                    dve.wait_ge(mv_made, c + 1)
                    dve.wait_ge(rs_made, c + 1)
                    for i, r in tiles:
                        a = V.tensor_scalar(y[0:r, i, :], S[0:r, i, :], mv[0:r, i, 0:1], rs[0:r, i:i + 1], ALU.subtract, ALU.mult)
                    a.then_inc(y_made, 1)

            @block.sync
            def _(sp):
                for c in range(CHUNKS):
                    sp.wait_ge(y_made, c + 1)
                    rows = out[c * CT:(c + 1) * CT, :]
                    nc.sync.dma_start(rows[0:4 * P, :].rearrange("(i p) d -> p i d", p=P), y[:, c * NT:c * NT + 4, :]
                                      ).then_inc(stored, 16)
                    nc.sync.dma_start(rows[4 * P:CT, :], y[0:CT - 4 * P, c * NT + 4, :]).then_inc(stored, 16)
                sp.wait_ge(stored, 32 * CHUNKS)


def expert_products(nc, t, exp_in, exp_out):
    E = 8
    TURN = 2
    with ExitStack() as ctx:
        def sb(name, shape, dt=F32):
            return ctx.enter_context(nc.sbuf_tensor("ep_" + name, shape, dt))

        def psum(name, shape, dt=F32):
            return ctx.enter_context(nc.psum_tensor("ep_" + name, shape, dt))

        def made(name, per):
            return Made(ctx.enter_context(nc.semaphore("ep_" + name)), per, TURN, TURN)

        ident = sb("ident", [P, P])
        W1 = sb("W1", [P, TURN, NB, FF])
        W2 = sb("W2", [P, TURN, FB, D])
        b1 = sb("b1", [P, TURN, FB])
        b2 = sb("b2", [P, TURN, D])
        xr = sb("xr", [P, TURN, NT, D])
        xT = sb("xT", [P, TURN, NB, CT])
        hid = sb("hid", [P, FB, CT])
        y = sb("y", [P, TURN, NT, D])
        ps_h = psum("ps_h", [P, 4, 512])
        ps_t = psum("ps_t", [P, 2, 512])
        ps_y = psum("ps_y", [P, 2, 512])

        diag = ctx.enter_context(nc.semaphore("ep_diag"))
        carrier = ctx.enter_context(nc.semaphore("ep_carrier"))
        w1_in = [ctx.enter_context(nc.semaphore(f"ep_w1_in{c}")) for c in range(TURN)]
        w2_in = [ctx.enter_context(nc.semaphore(f"ep_w2_in{c}")) for c in range(TURN)]
        x_in = [ctx.enter_context(nc.semaphore(f"ep_x_in{c}")) for c in range(TURN)]
        t_ready = made("t_ready", len(GROUPS))
        h_ready = made("h_ready", FB)
        y_ready = made("y_ready", NT)
        t_out = made("t_out", 2 * len(GROUPS))
        h_out = made("h_out", FB)
        y_out = made("y_out", NT)
        y_stored = [ctx.enter_context(nc.semaphore(f"ep_y_stored{c}")) for c in range(TURN)]

        def credit(eng, *sems):
            for s in sems:
                eng.sem_inc(s.sem, s.ahead * s.per)

        with nc.Block() as block:
            @block.sync
            def _(sp):
                wait = lambda m, s, j=None: sp.wait_ge(m.sem, m.at(s, j))

                def load(c, e):
                    one = (lambda v: v[e:e + 1]) if isinstance(e, int) else (lambda v: v[bass.ds(e, 1)])
                    rows = one(exp_in[0:E * CT, :].rearrange("(e r) d -> e r d", e=E))
                    nc.sync.dma_start(xr[:, c, 0:4, :], rows[:, 0:4 * P, :].rearrange("e (i p) d -> p (e i) d", p=P)
                                      ).then_inc(x_in[c], 16)
                    nc.sync.dma_start(xr[0:64, c, 4, :], rows[:, 4 * P:CT, :].rearrange("e r d -> (e r) d")).then_inc(x_in[c], 16)
                    for dst, name, into in ((W1[:, c].rearrange("p k f -> p (k f)"), "W1", w1_in), (b1[:, c, :], "b1", w1_in),
                                            (W2[:, c].rearrange("p k f -> p (k f)"), "W2", w2_in), (b2[:, c, :], "b2", w2_in)):
                        nc.sync.dma_start(dst, one(t[name]).rearrange("e p n -> p (e n)")).then_inc(into[c], 16)

                def store(c, s, e):
                    wait(y_out, s)
                    rows = exp_out[:, :].rearrange("(e r) d -> e r d", e=E)
                    rows = rows[e:e + 1] if isinstance(e, int) else rows[bass.ds(e, 1)]
                    nc.sync.dma_start(rows[:, 0:4 * P, :].rearrange("e (i p) d -> p (e i) d", p=P), y[:, c, 0:4, :]
                                      ).then_inc(y_stored[c], 16)
                    nc.sync.dma_start(rows[:, 4 * P:CT, :].rearrange("e r d -> (e r) d"), y[0:64, c, 4, :]
                                      ).then_inc(y_stored[c], 16)

                for c in range(TURN):
                    sp.sem_inc(y_stored[c], 32)
                    load(c, c)
                with nc.sync.Fori(0, E // TURN - 1) as n:
                    for c in range(TURN):
                        store(c, (n, c), n * TURN + c)
                        load(c, n * TURN + (TURN + c))
                for c in range(TURN):
                    store(c, (E // TURN - 1, c), E - TURN + c)
                for c in range(TURN):
                    sp.wait_ge(y_stored[c], 32 + 32 * E // TURN)

            @block.gpsimd
            def _(pool):
                nc.gpsimd.memset(ident[:], 0.0).then_inc(diag, 1)
                pool.wait_ge(diag, 1)
                nc.gpsimd.affine_select(out=ident[:], in_=ident[:], compare_op=ALU.not_equal, fill=1.0, base=0,
                                        pattern=[[-1, P]], channel_multiplier=1).then_inc(diag, 1)

            @block.tensor
            def _(pe):
                wait = lambda m, s, j=None: pe.wait_ge(m.sem, m.at(s, j))
                credit(pe, t_ready, h_ready, y_ready)
                pe.wait_ge(diag, 2)
                with nc.tensor.Fori(0, E // TURN) as n:
                    for c in range(TURN):
                        s = (n, c)
                        pe.wait_ge(x_in[c], n * 32 + 32)
                        for q, tiles in enumerate(GROUPS):
                            wait(t_out, s, 2 * q - 2) if q == 2 else wait(t_out, later(s, -1))
                            if TILES[tiles[0]][1] < P:
                                pe.sem_inc(carrier, 1)
                            width = sum(TILES[i][1] for i in tiles)
                            for i in tiles:
                                r = TILES[i][1]
                                at = TILES[i][0] - TILES[tiles[0]][0]
                                for b in range(NB):
                                    a = nc.tensor.transpose(ps_t[:, q % 2, b * width + at:b * width + at + r],
                                                            xr[0:r, c, i, b * P:(b + 1) * P], ident[0:r, 0:r])
                            a.then_inc(t_ready.sem, 1)
                        pe.wait_ge(w1_in[c], n * 32 + 32)
                        wait(t_out, s)
                        for m in range(FB):
                            wait(h_out, s, m - 1) if m >= 2 else wait(h_out, later(s, -1))
                            for h in range(2):
                                for b in range(NB):
                                    a = nc.tensor.matmul(ps_h[:, 2 * (m % 2) + h, 0:HALF], W1[:, c, b, m * P:(m + 1) * P],
                                                         xT[:, c, b, h * HALF:(h + 1) * HALF], start=(b == 0), stop=(b == NB - 1))
                            a.then_inc(h_ready.sem, 1)
                        pe.wait_ge(w2_in[c], n * 32 + 32)
                        wait(h_out, s)
                        for i, (first, r) in enumerate(TILES):
                            wait(y_out, s, i - 1) if i >= 2 else wait(y_out, later(s, -1))
                            for m in range(FB):
                                a = nc.tensor.matmul(ps_y[0:r, i % 2, 0:D], hid[:, m, first:first + r], W2[:, c, m, :],
                                                     start=(m == 0), stop=(m == FB - 1))
                            a.then_inc(y_ready.sem, 1)

            @block.scalar
            def _(act):
                wait = lambda m, s, j=None: act.wait_ge(m.sem, m.at(s, j))
                credit(act, h_out)
                with nc.scalar.Fori(0, E // TURN) as n:
                    for c in range(TURN):
                        s = (n, c)
                        for m in range(FB):
                            wait(h_ready, s, m + 1)
                            if m == 0:
                                wait(y_ready, later(s, -1))
                            nc.scalar.activation(hid[:, m, :].rearrange("p (h n) -> p h n", h=2),
                                                 ps_h[:, 2 * (m % 2):2 * (m % 2) + 2, 0:HALF], ACT.Gelu,
                                                 bias=b1[:, c, m:m + 1]).then_inc(h_out.sem, 1)

            @block.vector
            def _(dve):
                wait = lambda m, s, j=None: dve.wait_ge(m.sem, m.at(s, j))
                credit(dve, t_out, y_out)
                with nc.vector.Fori(0, E // TURN) as n:
                    for c in range(TURN):
                        s = (n, c)
                        wait(h_ready, later(s, -TURN))
                        for q, tiles in enumerate(GROUPS):
                            width = sum(TILES[i][1] for i in tiles)
                            first = TILES[tiles[0]][0]
                            wait(t_ready, s, q + 1)
                            for b in range(NB):
                                nc.vector.tensor_copy(xT[:, c, b, first:first + width], ps_t[:, q % 2, b * width:(b + 1) * width]
                                                      ).then_inc(t_out.sem, 1)
                        dve.wait_ge(y_stored[c], n * 32 + 32)
                        for i, (_, r) in enumerate(TILES):
                            wait(y_ready, s, i + 1)
                            nc.vector.tensor_tensor(y[0:r, c, i, :], ps_y[0:r, i % 2, 0:D], b2[0:r, c, :], ALU.add
                                                    ).then_inc(y_out.sem, 1)


def expert_arrays(a):
    import numpy as np

    F = "L0_ffn_"
    E, TT = 8, CHUNKS * NT
    valid = np.array([[p < TILES[i % NT][1] for i in range(TT)] for p in range(P)])
    carry = np.ones((P, E, TT), np.float32)
    carry[:, :, 0] = 0
    return {
        "iota8": np.broadcast_to(np.arange(E, dtype=np.float32), (P, E)),
        "absent": np.broadcast_to(np.where(valid, 0, 99).astype(np.float32)[:, :, None], (P, TT, 2)),
        "carry": carry,
        "spare": (2 * N + np.arange(2)[None, :, None] * TT * P + np.arange(TT)[None, None, :] * P
                  + np.arange(P)[:, None, None]).astype(np.float32),
        "upto": np.triu(np.ones((P, P))).astype(mybir.dt.np(BF16)),
        "onesb": np.ones((P, P)).astype(mybir.dt.np(BF16)),
        "W1": a[F + "W1"].reshape(E, NB, P, FF).transpose(0, 2, 1, 3).reshape(E, P, -1),
        "W2": a[F + "W2"].reshape(E, FB, P, D).transpose(0, 2, 1, 3).reshape(E, P, -1),
        "b1": a[F + "b1"].reshape(E, FB, P).transpose(0, 2, 1),
        "b2": np.broadcast_to(a[F + "b2"][:, None, :], (E, P, D)),
    }




def kernel(**inputs):
    import numpy as np
    import concourse.bacc as bacc
    from concourse.bass_utils import run_bass_kernel_spmd

    a = {k: np.asarray(v) for k, v in inputs.items()}

    def blocks(v):
        v = v.reshape(*v.shape[:-1], v.shape[-1] // P, P)
        return np.moveaxis(v, -1, 0)

    def rows_first(w):
        L, k, m = w.shape
        return w.reshape(L, k // P, P, m).transpose(0, 2, 1, 3).reshape(L, P, -1)

    x = a["x"].reshape(IMAGES, 3, 6, 16, 6, 16).transpose(0, 2, 4, 3, 5, 1).reshape(CHUNKS, CT, PATCH)
    tr = lambda w: w.transpose(0, 2, 1)
    A = "L0_attn_"
    laid = {
        "patches": x,
        "patchesT": x.reshape(CHUNKS, CT, KP, P).transpose(0, 3, 2, 1),
        "W_mlp": a["L0_tok_W_mlp"].reshape(KP, P, D).transpose(1, 0, 2),
        "g1b1": np.stack([blocks(a["L0_tok_g1"]), blocks(a["L0_tok_b1"])], axis=1),
        "rows": np.broadcast_to(np.stack([a["L0_tok_b_mlp"], a["L0_tok_g2"], a["L0_tok_b2"], a[A + "ln0_w"],
                                          a[A + "ln0_b"]]), (P, 5, D)),
        "rwkv_vec": np.stack([blocks(a[A + n]) for n in ("ln1_w", "ln1_b", "tmk", "tmv", "tmr", "time_decay",
                                                         "time_first", "ln2_w", "ln2_b", "cmk", "cmr")], axis=2),
        "Wkvr": np.stack([rows_first(tr(a[A + n])) for n in ("Wk", "Wv", "Wr")], axis=2).reshape(LAYERS, P, -1),
        "Wo": rows_first(tr(a[A + "Wo"])),
        "Wck": rows_first(tr(a[A + "Wck"])),
        "Wcr": rows_first(tr(a[A + "Wcr"])),
        "Wcv": rows_first(tr(a[A + "Wcv"])),
    }
    laid.update(ffn_arrays(a, blocks))
    laid.update(expert_arrays(a))
    nc = bacc.Bacc("TRN2", target_bir_lowering=False, num_devices=1)
    arrays, t = {}, {}
    for name, v in laid.items():
        v = np.ascontiguousarray(v)
        arrays["in_" + name] = v
        t[name] = nc.dram_tensor("in_" + name, v.shape, mybir.dt.from_np(v.dtype), kind="ExternalInput").ap()
    out = nc.dram_tensor("out", (N, D), F32, kind="ExternalOutput").ap()
    bass_vit_tower(nc, t, out)
    r = run_bass_kernel_spmd(nc, [arrays], core_ids=[0])
    return r.results[0]["out"].reshape(IMAGES, T, D)
```

```python
from contextlib import ExitStack

import concourse.bass as bass
from concourse import mybir

P = 128
D = 256
NB = D // P
IMAGES, T = 64, 36
N = IMAGES * T
CHUNKS = 4
CI = IMAGES // CHUNKS
CT = CI * T
HALF = CT // 2
TILES = [(0, 128), (128, 128), (256, 128), (384, 128), (512, 64)]
NT = len(TILES)
GROUPS = [(0, 1), (2, 3), (4,)]
LAYERS = 4
FF = 1024
FB = FF // P
PATCH = 768
KP = PATCH // P
TP = T + 1
CP = CI * TP
NEVER = -1e38

F32 = mybir.dt.float32
BF16 = mybir.dt.bfloat16
F16 = mybir.dt.float16
ALU = mybir.AluOpType
ACT = mybir.ActivationFunctionType
AX = mybir.AxisListType


class Made:

    def __init__(self, sem, per, steps=CHUNKS, ahead=1):
        self.sem, self.per, self.steps, self.ahead = sem, per, steps, ahead

    def at(self, step, j=None):
        layer, c = step
        j = self.per if j is None else j
        if isinstance(layer, int):
            return self.per * (self.steps * layer + c + self.ahead) + j
        return layer * (self.steps * self.per) + (self.per * (c + self.ahead) + j)


def later(step, k):
    return step[0], step[1] + k




def bass_vit_tower(nc, t, out):
    with ExitStack() as ctx:
        def sb(name, shape, dt=F32):
            return ctx.enter_context(nc.sbuf_tensor(name, shape, dt))

        X = sb("X", [P, CHUNKS * NT, D])
        H0 = sb("H0", [P, CHUNKS * NT, D])
        ident = sb("ident", [P, P])
        half_neg = sb("half_neg", [P, 8])
        LG = sb("LG", [P, CHUNKS * NT, 8])
        exp_in = nc.dram_tensor("exp_in", (2 * N + 2 * CHUNKS * NT * P, D), F32, kind="Internal").ap()
        exp_out = nc.dram_tensor("exp_out", (2 * N, D), F32, kind="Internal").ap()
        tokenizer(nc, t, X, H0, ident, half_neg)
        rwkv(nc, t, X, ident, half_neg)
        H2 = sb("H2", [P, CHUNKS * NT, D])
        attention(nc, t, X, H0, H2, LG, exp_in, ident, half_neg)
        experts(nc, t, X, H0, H2, LG, exp_in, exp_out, out)


def tokenizer(nc, t, X, H0, ident, half_neg):
    EPS_TOK, EPS_0 = -1e-05, 1e-05
    with ExitStack() as ctx:
        def sb(name, shape, dt=F32):
            return ctx.enter_context(nc.sbuf_tensor("tok_" + name, shape, dt))

        sems = []

        def sem(name):
            sems.append(ctx.enter_context(nc.semaphore("tok_" + name)))
            return sems[-1]

        W = sb("W", [P, KP, D])
        ones = sb("ones", [P, P])
        b1c = sb("b1c", [P, KP, P])
        g1b1 = sb("g1b1", [P, 2, KP])
        rows = sb("rows", [P, 5, D])
        bias = sb("bias", [P, D])
        pT = [sb(f"pT{i}", [P, KP, CT]) for i in range(2)]
        pR = [sb(f"pR{i}", [P, NT, PATCH]) for i in range(2)]
        st0 = sb("st0", [P, NT, 2, 6])
        st = sb("st", [P, NT, 1, 6])
        mv = sb("mv", [P, 3, NT, 2])
        vr = sb("vr", [P, 3, NT])
        rs = sb("rs", [P, 3, NT])
        Y = sb("Y", [P, NT, D])
        Z = sb("Z", [P, NT, D])
        Z0 = sb("Z0", [P, NT, D])
        Z1 = sb("Z1", [P, NT, D])
        psY = ctx.enter_context(nc.psum_tensor("tok_psY", [P, NT, 512], F32))
        psC = ctx.enter_context(nc.psum_tensor("tok_psC", [P, 2, 512], F32))

        w_in = sem("w_in")
        p_in = [sem("p_in0"), sem("p_in1")]
        const = sem("const")
        carrier = sem("carrier")
        diag0 = sem("diag0")
        w_scaled = sem("w_scaled")
        col_mean = sem("col_mean")
        w_ready = sem("w_ready")
        y_ready = sem("y_ready")
        patch_mv = sem("patch_mv")
        d = sem("d")
        patch_st = sem("patch_st")
        rstd = [sem(f"rstd{k}") for k in range(3)]
        var_eps = [sem(f"var_eps{k}") for k in range(3)]
        y_made = sem("y_made")
        y_mv = sem("y_mv")
        z_made = sem("z_made")
        h0_scaled = sem("h0_scaled")
        h0_made = sem("h0_made")
        h0_mv = sem("h0_mv")
        z0_made = sem("z0_made")
        x_scaled = sem("x_scaled")
        x_made = sem("x_made")
        pair = 2

        def tile(n, c, i):
            at = (c * NT + i) + n * (pair * NT)
            return slice(at, at + 1) if isinstance(n, int) else bass.ds(n * (pair * NT) + (c * NT + i), 1)

        def chunks(eng, chunk):
            with eng.Fori(0, CHUNKS // pair - 1) as n:
                for c in range(pair):
                    chunk(n, c, False)
            for c in range(pair):
                chunk(CHUNKS // pair - 1, c, c == pair - 1)


        with nc.Block() as block:
            @block.sync
            def _(sp):
                nc.sync.dma_start(W[:], t["W_mlp"]).then_inc(w_in, 16)
                nc.sync.dma_start(g1b1[:], t["g1b1"]).then_inc(w_in, 16)
                nc.sync.dma_start(rows[:], t["rows"]).then_inc(w_in, 16)
                with nc.sync.Fori(0, CHUNKS // pair) as n:
                    for c in range(pair):
                        sp.wait_ge(y_ready, n * (pair * NT) + 1)
                        sp.sem_inc(carrier, 1)
                        sp.wait_ge(patch_mv, n * pair + 1)
                        nc.sync.dma_start(pT[c][:], t["patchesT"][bass.ds(n * pair + c, 1)]
                                          .rearrange("a p k n -> p (a k) n")).then_inc(p_in[c], 16)
                        src = t["patches"][bass.ds(n * pair + c, 1)].rearrange("a n f -> (a n) f")
                        nc.sync.dma_start(pR[c][:, 0:4, :], src[0:512, :].rearrange("(i p) f -> p i f", p=P)
                                          ).then_inc(p_in[c], 16)
                        nc.sync.dma_start(pR[c][0:64, 4, :], src[512:576, :]).then_inc(p_in[c], 16)

            @block.gpsimd
            def _(pool):
                pool.sem_inc(x_made, 1)
                nc.gpsimd.memset(ones[:], 1.0).then_inc(const, 1)
                nc.gpsimd.memset(half_neg[:], -0.5).then_inc(const, 1)
                nc.gpsimd.memset(ident[:], 0.0).then_inc(diag0, 1)
                nc.gpsimd.memset(mv[:], 1.0).then_inc(const, 1)
                pool.wait_ge(diag0, 1)
                nc.gpsimd.affine_select(out=ident[:], in_=ident[:], compare_op=ALU.not_equal, fill=1.0, base=0,
                                        pattern=[[-1, P]], channel_multiplier=1).then_inc(const, 1)
                pool.wait_ge(const, 4)

                def inverse_root(n, c, k, ready, eps):
                    count = n * pair + (c + 1)
                    pool.wait_ge(ready, count + (ready is patch_mv))
                    pool.sem_inc(carrier, 1)
                    nc.gpsimd.tensor_scalar(vr[:, k, :], mv[:, k, :, 1], 1.0, eps, ALU.mult, ALU.add).then_inc(var_eps[k], 1)
                    pool.wait_ge(var_eps[k], count)
                    nc.gpsimd.tensor_tensor(rs[:, k, :], vr[:, k, :], half_neg[:, 0:NT], ALU.pow).then_inc(rstd[k], 1)

                def affine(n, c, made, src, mid, dst, scaled, done, row):
                    for i, (_, r) in enumerate(TILES):
                        pool.wait_ge(made, n * (pair * NT) + (c * NT + i + 1))
                        nc.gpsimd.tensor_tensor(mid(i, r), src(i, r), rows[0:r, row, :], ALU.mult).then_inc(scaled, 1)
                    for i, (_, r) in enumerate(TILES):
                        pool.wait_ge(scaled, n * (pair * NT) + (c * NT + i + 1))
                        nc.gpsimd.tensor_tensor(dst(i, r), mid(i, r), rows[0:r, row + 1, :], ALU.add).then_inc(done, 1)

                pool.wait_ge(w_in, 48)

                def chunk(n, c, last):
                    inverse_root(n, c, 1, y_mv, EPS_TOK)
                    affine(n, c, z_made, lambda i, r: Z[0:r, i:i + 1, :], lambda i, r: Z0[0:r, i:i + 1, :],
                           lambda i, r: H0[0:r, tile(n, c, i), :], h0_scaled, h0_made, 1)
                    if not last:
                        inverse_root(n, c + 1, 0, patch_mv, EPS_TOK)
                    inverse_root(n, c, 2, h0_mv, EPS_0)
                    affine(n, c, z0_made, lambda i, r: Z1[0:r, i:i + 1, :], lambda i, r: Z1[0:r, i:i + 1, :],
                           lambda i, r: X[0:r, tile(n, c, i), :], x_scaled, x_made, 3)

                inverse_root(0, 0, 0, patch_mv, EPS_TOK)
                chunks(nc.gpsimd, chunk)

            @block.vector
            def _(dve):
                dve.sem_inc(patch_mv, 1)
                dve.sem_inc(y_made, 1)
                dve.wait_ge(w_in, 48)
                dve.wait_ge(const, 4)
                for k in range(KP):
                    nc.vector.tensor_scalar(b1c[:, k, :], ones[:], g1b1[:, 1, k:k + 1], None, ALU.mult).then_inc(d, 1)
                dve.wait_ge(col_mean, 1)
                nc.vector.tensor_tensor(bias[:], psC[:, 1, 0:D], rows[:, 0, :], ALU.add).then_inc(d, 1)
                for k in range(KP):
                    nc.vector.tensor_scalar(W[:, k, :], W[:, k, :], g1b1[:, 0, k:k + 1], None, ALU.mult).then_inc(w_scaled, 1)
                dve.wait_ge(col_mean, 2)
                nc.vector.tensor_scalar(Y[:, 0, :], psC[:, 0, 0:D], 1.0 / PATCH, None, ALU.mult).then_inc(d, 1)
                dve.wait_ge(d, KP + 2)
                for k in range(KP):
                    nc.vector.tensor_tensor(W[:, k, :], W[:, k, :], Y[:, 0, :], ALU.subtract).then_inc(w_ready, 1)

                def statistics(n, c, k, src, ready, done, base):
                    for i, (_, r) in enumerate(TILES):
                        dve.wait_ge(ready, n * (pair * NT) + (c * NT + i + 1 + (ready is y_made)))
                        a = nc.vector.bn_stats(st[0:r, i, 0, :], src(i, r))
                    a.then_inc(d, 1)
                    dve.wait_ge(d, base)
                    dve.sem_inc(carrier, 1)
                    for i, (_, r) in enumerate(TILES):
                        a = nc.vector.bn_aggr(mv[0:r, k, i, :], st[0:r, i, 0, :])
                    a.then_inc(done, 1)

                first = KP + 2
                per = 2
                at = lambda n, c, j: n * (pair * per) + (first + c * per + j)

                def patch_statistics(n, c):
                    half = c % pair
                    dve.wait_ge(p_in[half], n * 48 + 48 * (1 + c // pair))
                    for i, (_, r) in enumerate(TILES):
                        for h in range(2):
                            a = nc.vector.bn_stats(st0[0:r, i, h, :], pR[half][0:r, i, h * (PATCH // 2):(h + 1) * (PATCH // 2)])
                    a.then_inc(patch_st, 1)
                    dve.wait_ge(patch_st, n * pair + (c + 1))
                    dve.sem_inc(carrier, 1)
                    for i, (_, r) in enumerate(TILES):
                        a = nc.vector.bn_aggr(mv[0:r, 0, i, :], st0[0:r, i, :, :])
                    a.then_inc(patch_mv, 1)

                def chunk(n, c, last):
                    dve.wait_ge(rstd[0], n * pair + (c + 1))
                    for i, (_, r) in enumerate(TILES):
                        dve.wait_ge(y_ready, n * (pair * NT) + (c * NT + i + 2))
                        nc.vector.scalar_tensor_tensor(out=Y[0:r, i, :], in0=psY[0:r, i, 0:D], scalar=rs[0:r, 0, i:i + 1],
                                                       in1=bias[0:r, :], op0=ALU.mult, op1=ALU.add).then_inc(y_made, 1)
                    statistics(n, c, 1, lambda i, r: Y[0:r, i, :], y_made, y_mv, at(n, c, 1))
                    dve.wait_ge(rstd[1], n * pair + (c + 1))
                    dve.wait_ge(y_mv, n * pair + (c + 1))
                    for i, (_, r) in enumerate(TILES):
                        nc.vector.tensor_scalar(Z[0:r, i, :], Y[0:r, i, :], mv[0:r, 1, i, 0:1], rs[0:r, 1, i:i + 1],
                                                ALU.subtract, ALU.mult).then_inc(z_made, 1)
                    if not last:
                        patch_statistics(n, c + 1)
                    statistics(n, c, 2, lambda i, r: H0[0:r, tile(n, c, i), :], h0_made, h0_mv, at(n, c, 2))
                    dve.wait_ge(rstd[2], n * pair + (c + 1))
                    dve.wait_ge(h0_mv, n * pair + (c + 1))
                    dve.wait_ge(x_made, n * (pair * NT) + (c * NT + 1))
                    for i, (_, r) in enumerate(TILES):
                        nc.vector.tensor_scalar(Z1[0:r, i:i + 1, :], H0[0:r, tile(n, c, i), :], mv[0:r, 2, i, 0:1],
                                                rs[0:r, 2, i:i + 1], ALU.subtract, ALU.mult).then_inc(z0_made, 1)

                patch_statistics(0, 0)
                chunks(nc.vector, chunk)

            @block.tensor
            def _(pe):
                pe.sem_inc(y_ready, 1)
                pe.wait_ge(w_in, 48)
                pe.wait_ge(d, KP)
                for k in range(KP):
                    a = nc.tensor.matmul(psC[:, 1, 0:D], b1c[:, k, :], W[:, k, :], start=(k == 0), stop=(k == KP - 1))
                a.then_inc(col_mean, 1)
                pe.wait_ge(w_scaled, KP)
                for k in range(KP):
                    a = nc.tensor.matmul(psC[:, 0, 0:D], ones[:], W[:, k, :], start=(k == 0), stop=(k == KP - 1))
                a.then_inc(col_mean, 1)
                pe.wait_ge(w_ready, KP)
                with nc.tensor.Fori(0, CHUNKS // pair) as n:
                    for c in range(pair):
                        pe.wait_ge(p_in[c], n * 48 + 48)
                        for i, (first, r) in enumerate(TILES):
                            pe.wait_ge(y_made, n * (pair * NT) + (c * NT + 1))
                            for k in range(KP):
                                a = nc.tensor.matmul(psY[0:r, i, 0:D], pT[c][:, k, first:first + r], W[:, k, :],
                                                     start=(k == 0), stop=(k == KP - 1))
                            a.then_inc(y_ready, 1)

        with nc.Block() as block:
            @block.gpsimd
            def _(pool):
                for x in sems:
                    pool.sem_clear(x)


def rwkv(nc, t, X, ident, half_neg):
    EPS = 1e-05
    with ExitStack() as ctx:
        def sb(name, shape, dt=F32):
            return ctx.enter_context(nc.sbuf_tensor("rw_" + name, shape, dt))

        def psum(name, shape):
            return ctx.enter_context(nc.psum_tensor("rw_" + name, shape, F32))

        def sem(name):
            return ctx.enter_context(nc.semaphore("rw_" + name))

        def made(name, per, ahead=1):
            return Made(sem(name), per, ahead=ahead)

        NPK = 11
        LN1W, LN1B, TMK, TMV, TMR, DECAY, FIRST, LN2W, LN2B, CMK, CMR = range(NPK)
        pk = sb("pk", [P, LAYERS, NPK, NB])
        pkv_a = sb("pkv_a", [P, 1, 5, NB])
        pkv_b = sb("pkv_b", [P, 1, 2, NB])
        pks_1 = sb("pks_1", [P, 1, 2, NB])
        pks_2 = sb("pks_2", [P, 1, 2, NB])
        Wa = sb("Wa", [P, 3, NB, D])
        Wo = sb("Wo", [P, NB, D])
        Wck = sb("Wck", [P, NB, FF])
        Wcr = sb("Wcr", [P, NB, D])
        Wcv = sb("Wcv", [P, FB, D])
        bs1 = sb("bs1", [P, NT, 6])
        bs2 = sb("bs2", [P, NT, 6])
        mv1 = sb("mv1", [P, NT, 2])
        mv2 = sb("mv2", [P, NT, 2])
        vr = sb("vr", [P, 2, NT])
        rs1 = sb("rs1", [P, NT])
        rs2 = sb("rs2", [P, NT])
        xn1 = sb("xn1", [P, NT, D])
        xn2 = sb("xn2", [P, NT, D])
        h1 = sb("h1", [P, NB, CT])
        h2 = sb("h2", [P, NB, CT])
        dh = sb("dh", [P, NB, CT])
        xa = sb("xa", [P, 3, NB, CT])
        xb = sb("xb", [P, 2, NB, CT])
        K = sb("K", [P, NB, CP])
        V = sb("V", [P, NB, CP])
        R = sb("R", [P, NB, CP])
        reset = sb("reset", [P, CP])
        wd = sb("wd", [P, NB, CP])
        PP = sb("PP", [P, NB, CP])
        E = sb("E", [P, 3, NB, CP])
        EV = sb("EV", [P, NB, CP])
        AA = sb("AA", [P, NB, CP])
        BB = sb("BB", [P, NB, CP])
        ys = sb("ys", [P, NB, CT])
        relu = sb("relu", [P, 2, CT])
        kf = sb("kf", [P, FB, CT])
        tr = sb("tr", [P, NT, D])
        kv = sb("kv", [P, NT, D])
        ps_mat = psum("ps_mat", [P, 4, 512])
        ps_t = psum("ps_t", [P, 2, 512])
        ps_tok = psum("ps_tok", [P, 2, 512])

        pk_in = sem("pk_in")
        carrier = sem("carrier")
        pk_made = sem("pk_made")
        zeroed = sem("zeroed")
        wa_in = sem("wa_in")
        wo_in = sem("wo_in")
        wck_in = sem("wck_in")
        wcr_in = sem("wcr_in")
        wcv_in = sem("wcv_in")
        pka_copied = sem("pka_copied")
        pkb_copied = sem("pkb_copied")
        pk1_copied = sem("pk1_copied")
        pk2_copied = sem("pk2_copied")

        t1_ready = made("t1_ready", len(GROUPS))
        t2_ready = made("t2_ready", len(GROUPS))
        a_ready = made("a_ready", 6)
        wo_ready = made("wo_ready", NT)
        ck_ready = made("ck_ready", FB)
        cr_ready = made("cr_ready", NT)
        cv_ready = made("cv_ready", NT)
        t1_out = made("t1_out", 2 * len(GROUPS))
        t2_out = made("t2_out", 2 * len(GROUPS))
        a_out = made("a_out", 6)
        e_out = made("e_out", 6)
        ck_relu = made("ck_relu", FB)
        ck_sq = made("ck_sq", FB)
        cr_out = made("cr_out", NT)
        cv_out = made("cv_out", NT)
        res1 = made("res1", NT)
        st1 = made("st1", 1)
        st2 = made("st2", 1)
        mv1_made = made("mv1_made", 1)
        mv2_made = made("mv2_made", 1)
        xn1_made = made("xn1_made", NT)
        xn2_made = made("xn2_made", NT)
        dh1 = made("dh1", 2)
        dh2 = made("dh2", 2)
        mixa = made("mixa", 6)
        mixb = made("mixb", 4)
        pp_made = made("pp_made", 2)
        ex_made = made("ex_made", 6)
        ev_made = made("ev_made", 2)
        bb_made = made("bb_made", 2)
        aa_made = made("aa_made", 2)
        n1_made = made("n1_made", 1)
        n2_made = made("n2_made", 1)
        nu_made = made("nu_made", 1)
        c1_made = made("c1_made", 1)
        den_made = made("den_made", 1)
        inv_made = made("inv_made", 1)
        yr_made = made("yr_made", 1)
        ys_made = made("ys_made", 1)
        sigmoid = made("sigmoid", len(GROUPS))
        gated = made("gated", len(GROUPS))
        res2 = made("res2", len(GROUPS), 2)
        ve1 = made("ve1", 1)
        ve2 = made("ve2", 1)
        rs1_made = made("rs1_made", 1)
        rs2_made = made("rs2_made", 1)

        def credit(eng, *sems):
            for s in sems:
                eng.sem_inc(s.sem, s.ahead * s.per)

        def has(step, k):
            return not isinstance(step[0], int) or CHUNKS * step[0] + step[1] + k < CHUNKS * LAYERS

        def tok(buf, b):
            return buf[:, b, :].rearrange("p (n t) -> p n t", t=TP)[:, :, 1:TP]

        def before(buf, b):
            return buf[:, b, :].rearrange("p (n t) -> p n t", t=TP)[:, :, 0:T]

        def tok2(buf):
            return buf[:, :, :].rearrange("p b (n t) -> p (b n) t", t=TP)[:, :, 1:TP]

        def before2(buf):
            return buf[:, :, :].rearrange("p b (n t) -> p (b n) t", t=TP)[:, :, 0:T]

        with nc.Block() as block:
            @block.sync
            def _(sp):
                nc.sync.dma_start(pk[:], t["rwkv_vec"]).then_inc(pk_in, 16)

                def load(dst, name, layer, sem_in):
                    src = t[name][layer:layer + 1] if isinstance(layer, int) else t[name][bass.ds(layer, 1)]
                    nc.sync.dma_start(dst, src.rearrange("l p n -> p (l n)")).then_inc(sem_in, 16)

                def flat(w):
                    return w.rearrange("p a n -> p (a n)")

                load(Wa.rearrange("p s b n -> p (s b n)"), "Wkvr", 0, wa_in)
                load(flat(Wo), "Wo", 0, wo_in)
                load(flat(Wck), "Wck", 0, wck_in)
                load(flat(Wcr), "Wcr", 0, wcr_in)
                load(flat(Wcv), "Wcv", 0, wcv_in)
                with nc.sync.Fori(0, LAYERS - 1) as l:
                    sp.wait_ge(a_ready.sem, a_ready.at((l, 3)))
                    sp.sem_inc(carrier, 1)
                    load(Wa.rearrange("p s b n -> p (s b n)"), "Wkvr", l + 1, wa_in)
                    sp.wait_ge(wo_ready.sem, wo_ready.at((l, 3)))
                    load(flat(Wo), "Wo", l + 1, wo_in)
                    sp.wait_ge(ck_ready.sem, ck_ready.at((l, 3)))
                    load(flat(Wck), "Wck", l + 1, wck_in)
                    sp.wait_ge(cr_ready.sem, cr_ready.at((l, 3)))
                    load(flat(Wcr), "Wcr", l + 1, wcr_in)
                    sp.wait_ge(cv_ready.sem, cv_ready.at((l, 3)))
                    load(flat(Wcv), "Wcv", l + 1, wcv_in)

            @block.gpsimd
            def _(pool):
                resets = lambda buf: buf.rearrange("p b (n t) -> p (b n) t", t=TP)[:, :, 0:1]
                nc.gpsimd.memset(resets(K[:]), NEVER).then_inc(zeroed, 1)
                nc.gpsimd.memset(resets(EV[:]), 0.0).then_inc(zeroed, 1)
                for e in range(2):
                    nc.gpsimd.memset(resets(E[:, e]), 0.0).then_inc(zeroed, 1)
                nc.gpsimd.memset(reset[:], 0.0).then_inc(zeroed, 1)
                nc.gpsimd.memset(mv1[:], 1.0).then_inc(zeroed, 1)
                nc.gpsimd.memset(mv2[:], 1.0).then_inc(zeroed, 1)
                pool.wait_ge(zeroed, 7)
                nc.gpsimd.memset(reset[:].rearrange("p (n t) -> p n t", t=TP)[:, :, 0:1], 2 * NEVER).then_inc(zeroed, 1)
                credit(pool, ve1, ve2, rs1_made, rs2_made, sigmoid, gated, res2)

                def root(mv, vr_, rs_, stats, ve, done, step):
                    pool.wait_ge(stats.sem, stats.at(step))
                    pool.sem_inc(carrier, 1)
                    nc.gpsimd.tensor_scalar(vr_, mv[:, :, 1], 1.0, EPS, ALU.mult, ALU.add).then_inc(ve.sem, 1)
                    pool.wait_ge(ve.sem, ve.at(step))
                    nc.gpsimd.tensor_tensor(rs_, vr_, half_neg[:, 0:NT], ALU.pow).then_inc(done.sem, 1)

                norm1 = lambda s: root(mv1, vr[:, 0, :], rs1[:], mv1_made, ve1, rs1_made, s)
                norm2 = lambda s: root(mv2, vr[:, 1, :], rs2[:], mv2_made, ve2, rs2_made, s)

                def step(s):
                    norm2(s)
                    if has(s, 2):
                        norm1(later(s, 2))
                    residual2(s)

                def residual2(s):
                    for q, tiles in enumerate(GROUPS):
                        r = TILES[tiles[0]][1]
                        of = slice(tiles[0], tiles[-1] + 1)
                        pool.wait_ge(cr_out.sem, cr_out.at(s, tiles[-1] + 1))
                        pool.sem_inc(carrier, 1)
                        nc.gpsimd.tensor_scalar(tr[0:r, of, :], tr[0:r, of, :], 0.5, 0.5, ALU.mult, ALU.add
                                                ).then_inc(sigmoid.sem, 1)
                    for q, tiles in enumerate(GROUPS):
                        r = TILES[tiles[0]][1]
                        of = slice(tiles[0], tiles[-1] + 1)
                        x = X[0:r, NT * s[1] + tiles[0]:NT * s[1] + tiles[-1] + 1, :]
                        pool.wait_ge(sigmoid.sem, sigmoid.at(s, q + 1))
                        pool.wait_ge(cv_out.sem, cv_out.at(s, tiles[-1] + 1))
                        nc.gpsimd.tensor_tensor(kv[0:r, of, :], tr[0:r, of, :], kv[0:r, of, :], ALU.mult).then_inc(gated.sem, 1)
                        pool.wait_ge(gated.sem, gated.at(s, q + 1))
                        nc.gpsimd.tensor_tensor(x, x, kv[0:r, of, :], ALU.add).then_inc(res2.sem, 1)

                for c in range(2):
                    norm1((0, c))
                with nc.gpsimd.Fori(0, LAYERS - 1) as l:
                    for c in range(CHUNKS):
                        step((l, c))
                for c in range(CHUNKS):
                    step((LAYERS - 1, c))

            @block.tensor
            def _(pe):
                credit(pe, t1_ready, t2_ready, a_ready, wo_ready, ck_ready, cr_ready, cv_ready)
                wait = lambda m, s, j=None: pe.wait_ge(m.sem, m.at(s, j))

                def transposes(xn, made_, ready, bank, free, s):
                    for q, tiles in enumerate(GROUPS):
                        wait(made_, s, tiles[-1] + 1)
                        free(q)
                        if TILES[tiles[0]][1] < P:
                            pe.sem_inc(carrier, 1)
                        dst = ps_t[:, bank(q), :]
                        width = sum(TILES[i][1] for i in tiles)
                        for i in tiles:
                            r = TILES[i][1]
                            at = TILES[i][0] - TILES[tiles[0]][0]
                            for b in range(NB):
                                a = nc.tensor.transpose(dst[:, b * width + at:b * width + at + r],
                                                        xn[0:r, i, b * P:(b + 1) * P], ident[0:r, 0:r])
                        a.then_inc(ready.sem, 1)

                def t1(s, first=False):
                    def free(q):
                        if first:
                            if s[1] == 1 or q == 2:
                                wait(t1_out, (0, s[1] - 1) if q < 2 else s, 6 if q < 2 else 2)
                        elif q < 2:
                            wait(t2_out, later(s, -2), 2 * q + 4)
                        else:
                            wait(t1_out, s, 2)
                    transposes(xn1, xn1_made, t1_ready, lambda q: (q + 1) % 2, free, s)

                def t2(s):
                    def free(q):
                        if q == 2:
                            wait(t2_out, s, 2)
                        elif has(s, 1):
                            wait(t1_out, later(s, 1), 2 * q + 4)
                        else:
                            wait(t2_out, later(s, -1), 6 - 2 * q)
                    transposes(xn2, xn2_made, t2_ready, lambda q: q % 2, free, s)

                def channel_major(dst_pair, w, x):
                    for h in range(2):
                        for b in range(NB):
                            a = nc.tensor.matmul(ps_mat[:, 2 * dst_pair + h, 0:HALF], w(b),
                                                 x(b)[:, h * HALF:(h + 1) * HALF], start=(b == 0), stop=(b == NB - 1))
                    return a

                def keys(s, js, after_ck):
                    for j in js:
                        stream, m = divmod(j, 2)
                        wait(mixa, s, 2 * stream + 2)
                        if j >= 2:
                            wait(a_out, s, j - 1)
                        elif after_ck is not None:
                            wait(ck_relu, after_ck, FB - 1 + j)
                        channel_major(j % 2, lambda b: Wa[:, stream, b, m * P:(m + 1) * P],
                                      lambda b: xa[:, stream, b, :]).then_inc(a_ready.sem, 1)

                def bank_of(s, kind, i):
                    return (3 * NT * s[1] + kind * NT + i) % 2

                def free_tok(s, kind, i):
                    users = (res1, cr_out, cv_out)
                    n = kind * NT + i - 2
                    if n < 0:
                        wait(cv_out, later(s, -1), n + NT + 1)
                    else:
                        wait(users[n // NT], s, n % NT + 1)

                def output(s):
                    wait(ys_made, s)
                    for i, (first, r) in enumerate(TILES):
                        free_tok(s, 0, i)
                        for b in range(NB):
                            a = nc.tensor.matmul(ps_tok[0:r, bank_of(s, 0, i), 0:D], ys[:, b, first:first + r], Wo[:, b, :],
                                                 start=(b == 0), stop=(b == NB - 1))
                        a.then_inc(wo_ready.sem, 1)

                def channel_keys(s):
                    wait(mixb, s, 2)
                    for m in range(FB):
                        if m >= 2:
                            wait(ck_relu, s, m - 1)
                        elif has(s, 1):
                            wait(a_out, later(s, 1), 5 + m)
                        else:
                            wait(ck_relu, later(s, -1), FB - 1 + m)
                        channel_major(m % 2, lambda b: Wck[:, b, m * P:(m + 1) * P], lambda b: xb[:, 0, b, :]
                                      ).then_inc(ck_ready.sem, 1)

                def channel_gate(s):
                    wait(mixb, s, 4)
                    for i, (first, r) in enumerate(TILES):
                        free_tok(s, 1, i)
                        for b in range(NB):
                            a = nc.tensor.matmul(ps_tok[0:r, bank_of(s, 1, i), 0:D], xb[:, 1, b, first:first + r],
                                                 Wcr[:, b, :], start=(b == 0), stop=(b == NB - 1))
                        a.then_inc(cr_ready.sem, 1)

                def channel_values(s):
                    wait(ck_sq, s)
                    for i, (first, r) in enumerate(TILES):
                        free_tok(s, 2, i)
                        for m in range(FB):
                            a = nc.tensor.matmul(ps_tok[0:r, bank_of(s, 2, i), 0:D], kf[:, m, first:first + r],
                                                 Wcv[:, m, :], start=(m == 0), stop=(m == FB - 1))
                        a.then_inc(cv_ready.sem, 1)

                def weights(sem_in, s):
                    if s[1] % CHUNKS == 0:
                        layer = s[0] + s[1] // CHUNKS
                        pe.wait_ge(sem_in, layer * 16 + 16)

                def step(s):
                    weights(wo_in, s)
                    output(s)
                    if has(s, 1):
                        weights(wa_in, later(s, 1))
                        keys(later(s, 1), range(4), later(s, -1))
                    t2(s)
                    if has(s, 1):
                        keys(later(s, 1), (4, 5), None)
                    if has(s, 2):
                        t1(later(s, 2))
                    weights(wck_in, s)
                    channel_keys(s)
                    weights(wcr_in, s)
                    channel_gate(s)
                    weights(wcv_in, s)
                    channel_values(s)

                t1((0, 0), True)
                weights(wa_in, (0, 0))
                keys((0, 0), range(6), None)
                t1((0, 1), True)
                with nc.tensor.Fori(0, LAYERS - 1) as l:
                    for c in range(CHUNKS):
                        step((l, c))
                for c in range(CHUNKS):
                    step((LAYERS - 1, c))

            @block.scalar
            def _(act):
                credit(act, t1_out, t2_out, a_out, e_out, ck_relu, ck_sq, cr_out, cv_out)
                wait = lambda m, s, j=None: act.wait_ge(m.sem, m.at(s, j))
                act.wait_ge(pk_in, 16)
                nc.scalar.activation(pk[:, :, DECAY, :], pk[:, :, DECAY, :], ACT.Exp).then_inc(pk_made, 1)

                def copy_pack(dst, layer, k, done):
                    src = pk[:, layer:layer + 1, k:k + 2, :] if isinstance(layer, int) else pk[:, bass.ds(layer, 1), k:k + 2, :]
                    nc.scalar.activation(dst[:], src, ACT.Copy).then_inc(done, 1)

                def evict(ready, h, par, par_copied, out_, bank, s, layer):
                    act.wait_ge(par_copied, layer + 1)
                    for q, tiles in enumerate(GROUPS):
                        width = sum(TILES[i][1] for i in tiles)
                        first = TILES[tiles[0]][0]
                        wait(ready, s, q + 1)
                        for b in range(NB):
                            nc.scalar.activation(h[:, b, first:first + width], ps_t[:, bank(q), b * width:(b + 1) * width],
                                                 ACT.Identity, bias=par[:, 0, 1, b:b + 1], scale=par[:, 0, 0, b:b + 1]
                                                 ).then_inc(out_.sem, 1)

                def t1(s):
                    if s[1] % CHUNKS == 0:
                        layer = s[0] + s[1] // CHUNKS
                        copy_pack(pks_1, layer, LN1W, pk1_copied)
                    wait(mixa, later(s, -1))
                    evict(t1_ready, h1, pks_1, pk1_copied, t1_out, lambda q: (q + 1) % 2, s, s[0] + s[1] // CHUNKS)

                def t2(s):
                    if s[1] == 0:
                        copy_pack(pks_2, s[0], LN2W, pk2_copied)
                    wait(mixb, later(s, -1))
                    evict(t2_ready, h2, pks_2, pk2_copied, t2_out, lambda q: q % 2, s, s[0])

                def images(ap):
                    return ap.rearrange("p h (n t) -> p h n t", t=T)

                def keys(s, js):
                    wait(ys_made, later(s, -1))
                    for j in js:
                        stream, m = divmod(j, 2)
                        wait(a_ready, s, j + 1)
                        src = images(ps_mat[:, 2 * (j % 2):2 * (j % 2) + 2, 0:HALF])
                        dst = tok((K, V, R)[stream], m).rearrange("p (h n) t -> p h n t", h=2)
                        if stream < 2:
                            a = nc.scalar.activation(dst, src, ACT.Identity)
                        else:
                            a = nc.scalar.activation(dst, src, ACT.Tanh, scale=0.5)
                        a.then_inc(a_out.sem, 1)

                def exponentials(s, b):
                    for e in range(3):
                        wait(ex_made, s, 3 * b + e + 1)
                        x = tok(E[:, e], b)
                        if e < 2:
                            a = nc.scalar.activation(x, x, ACT.Exp)
                        else:
                            a = nc.scalar.activation(x, x, ACT.Tanh, scale=-0.5)
                        a.then_inc(e_out.sem, 1)

                def channel_keys(s, ms):
                    for m in ms:
                        wait(ck_ready, s, m + 1)
                        wait(ck_sq, (s[0], s[1]), m - 1) if m >= 2 else wait(ck_sq, later(s, -1), FB - 1 + m)
                        dst = relu[:, m % 2, :].rearrange("p (h n) -> p h n", h=2)
                        nc.scalar.activation(dst, ps_mat[:, 2 * (m % 2):2 * (m % 2) + 2, 0:HALF], ACT.Relu
                                             ).then_inc(ck_relu.sem, 1)
                        wait(ck_relu, s, m + 1)
                        if m == 0:
                            wait(cv_ready, later(s, -1))
                        nc.scalar.activation(kf[:, m, :], relu[:, m % 2, :], ACT.Square).then_inc(ck_sq.sem, 1)

                def channel_gate(s):
                    wait(res2, later(s, -1))
                    for i, (_, r) in enumerate(TILES):
                        wait(cr_ready, s, i + 1)
                        nc.scalar.activation(tr[0:r, i, :], ps_tok[0:r, (3 * NT * s[1] + NT + i) % 2, 0:D], ACT.Tanh,
                                             scale=0.5).then_inc(cr_out.sem, 1)

                def channel_values(s):
                    for i, (_, r) in enumerate(TILES):
                        wait(cv_ready, s, i + 1)
                        nc.scalar.activation(kv[0:r, i, :], ps_tok[0:r, (3 * NT * s[1] + 2 * NT + i) % 2, 0:D], ACT.Copy
                                             ).then_inc(cv_out.sem, 1)

                def step(s):
                    if has(s, 1):
                        keys(later(s, 1), range(4))
                    t2(s)
                    if has(s, 1):
                        keys(later(s, 1), (4, 5))
                    if has(s, 2):
                        t1(later(s, 2))
                    channel_keys(s, (0, 1))
                    if has(s, 1):
                        exponentials(later(s, 1), 0)
                    channel_keys(s, (2, 3))
                    if has(s, 1):
                        exponentials(later(s, 1), 1)
                    channel_keys(s, (4, 5, 6, 7))
                    channel_gate(s)
                    channel_values(s)

                act.wait_ge(zeroed, 8)
                t1((0, 0))
                keys((0, 0), range(6))
                t1((0, 1))
                exponentials((0, 0), 0)
                exponentials((0, 0), 1)
                with nc.scalar.Fori(0, LAYERS - 1) as l:
                    for c in range(CHUNKS):
                        step((l, c))
                for c in range(CHUNKS):
                    step((LAYERS - 1, c))

            @block.vector
            def _(dve):
                credit(dve, res1, st1, st2, mv1_made, mv2_made, xn1_made, xn2_made, dh1, dh2, mixa, mixb, pp_made,
                       ex_made, ev_made, bb_made, aa_made, n1_made, n2_made, nu_made, c1_made, den_made, inv_made,
                       yr_made, ys_made)
                wait = lambda m, s, j=None: dve.wait_ge(m.sem, m.at(s, j))
                dve.wait_ge(pk_made, 1)
                dve.wait_ge(zeroed, 8)
                nc.vector.tensor_scalar(pk[:, :, DECAY, :], pk[:, :, DECAY, :], -1.0, None, ALU.mult).then_inc(pk_made, 1)
                nc.vector.tensor_scalar(pk[:, :, TMK:TMR + 1, :], pk[:, :, TMK:TMR + 1, :], -1.0, None, ALU.add
                                        ).then_inc(pk_made, 1)
                nc.vector.tensor_scalar(pk[:, :, CMK:CMR + 1, :], pk[:, :, CMK:CMR + 1, :], -1.0, None, ALU.add
                                        ).then_inc(pk_made, 1)
                dve.wait_ge(pk_made, 4)

                def tile(s, i):
                    return s[1] % CHUNKS * NT + i

                def statistics(s, bs, st_, mv, mv_made, ready):
                    for i, (_, r) in enumerate(TILES):
                        ready(i)
                        a = nc.vector.bn_stats(bs[0:r, i, :], X[0:r, tile(s, i), :])
                    a.then_inc(st_.sem, 1)
                    wait(st_, s)
                    dve.sem_inc(carrier, 1)
                    for i, (_, r) in enumerate(TILES):
                        a = nc.vector.bn_aggr(mv[0:r, i, :], bs[0:r, i, :])
                    a.then_inc(mv_made.sem, 1)

                def normalise(s, mv, mv_made, rs, rs_made, xn, xn_made, free):
                    wait(free, later(s, -1))
                    wait(mv_made, s)
                    wait(rs_made, s)
                    for i, (_, r) in enumerate(TILES):
                        nc.vector.tensor_scalar(xn[0:r, i, :], X[0:r, tile(s, i), :], mv[0:r, i, 0:1], rs[0:r, i:i + 1],
                                                ALU.subtract, ALU.mult).then_inc(xn_made.sem, 1)

                def statistics1(s):
                    def ready(i):
                        if i == 0 and not (isinstance(s[0], int) and CHUNKS * s[0] + s[1] < CHUNKS):
                            wait(res2, later(s, -CHUNKS))
                    statistics(s, bs1, st1, mv1, mv1_made, ready)

                def statistics2(s):
                    statistics(s, bs2, st2, mv2, mv2_made, lambda i: wait(res1, s, i + 1))

                norm1 = lambda s: normalise(s, mv1, mv1_made, rs1, rs1_made, xn1, xn1_made, t1_ready)
                norm2 = lambda s: normalise(s, mv2, mv2_made, rs2, rs2_made, xn2, xn2_made, t2_ready)

                def residual1(s):
                    for i, (_, r) in enumerate(TILES):
                        wait(wo_ready, s, i + 1)
                        x = X[0:r, tile(s, i), :]
                        nc.vector.scalar_tensor_tensor(out=x, in0=ps_tok[0:r, (3 * NT * s[1] + i) % 2, 0:D], scalar=0.5,
                                                       in1=x, op0=ALU.mult, op1=ALU.add).then_inc(res1.sem, 1)

                def differences(s, h, out_, done):
                    wait(out_, s)
                    nc.vector.tensor_tensor(dh[:, :, 1:CT], h[:, :, 1:CT], h[:, :, 0:CT - 1], ALU.subtract).then_inc(done.sem, 1)
                    wait(done, s, 1)
                    first = lambda x: x[:, :, :].rearrange("p b (n t) -> p (b n) t", t=T)[:, :, 0:1]
                    nc.vector.tensor_copy(first(dh), first(h)).then_inc(done.sem, 1)
                    wait(done, s, 2)

                def mix(h, pack, k, dst, b, done):
                    nc.vector.scalar_tensor_tensor(out=dst, in0=dh[:, b, :], scalar=pack[:, 0, k, b:b + 1], in1=h[:, b, :],
                                                   op0=ALU.mult, op1=ALU.add).then_inc(done.sem, 1)

                def one(buf, layer, a, z):
                    return buf[:, layer:layer + 1, a:z, :] if isinstance(layer, int) else buf[:, bass.ds(layer, 1), a:z, :]

                def mix_a(s):
                    if s[1] % CHUNKS == 0:
                        layer = s[0] + s[1] // CHUNKS
                        if s[1] == CHUNKS:
                            wait(ex_made, later(s, -1))
                        nc.vector.tensor_copy(pkv_a[:], one(pk, layer, TMK, FIRST + 1)).then_inc(pka_copied, 1)
                        dve.wait_ge(pka_copied, layer * 3 + 1)
                        for b in range(NB):
                            nc.vector.tensor_scalar(wd[:, b, :], reset[:], pkv_a[:, 0, 3, b:b + 1], None, ALU.add
                                                    ).then_inc(pka_copied, 1)
                    if not (isinstance(s[0], int) and CHUNKS * s[0] + s[1] < 2):
                        wait(mixb, later(s, -2))
                    differences(s, h1, t1_out, dh1)
                    wait(a_ready, later(s, -1))
                    for stream in range(3):
                        for b in range(NB):
                            mix(h1, pkv_a, stream, xa[:, stream, b, :], b, mixa)

                def mix_b(s):
                    if s[1] == 0:
                        nc.vector.tensor_copy(pkv_b[:], one(pk, s[0], CMK, CMR + 1)).then_inc(pkb_copied, 1)
                        dve.wait_ge(pkb_copied, s[0] + 1)
                    differences(s, h2, t2_out, dh2)
                    wait(cr_ready, later(s, -1))
                    for stream in range(2):
                        for b in range(NB):
                            mix(h2, pkv_b, stream, xb[:, stream, b, :], b, mixb)

                def scan(s, between=lambda: None):
                    w, u = (lambda b: pkv_a[:, 0, 3, b:b + 1]), (lambda b: pkv_a[:, 0, 4, b:b + 1])
                    layer = s[0] + s[1] // CHUNKS
                    dve.wait_ge(pka_copied, layer * 3 + 3)
                    for b in range(NB):
                        wait(a_out, s, b + 1)
                        nc.vector.tensor_tensor_scan(PP[:, b, :], wd[:, b, :], K[:, b, :], 0.0, ALU.add, ALU.max
                                                     ).then_inc(pp_made.sem, 1)
                    for b in range(NB):
                        wait(pp_made, s, b + 1)
                        nc.vector.scalar_tensor_tensor(out=tok(E[:, 0], b), in0=before(PP, b), scalar=w(b), in1=tok(PP, b),
                                                       op0=ALU.add, op1=ALU.subtract).then_inc(ex_made.sem, 1)
                        nc.vector.tensor_tensor(tok(E[:, 1], b), tok(K, b), tok(PP, b), ALU.subtract).then_inc(ex_made.sem, 1)
                        nc.vector.scalar_tensor_tensor(out=tok(E[:, 2], b), in0=tok(K, b), scalar=u(b), in1=before(PP, b),
                                                       op0=ALU.add, op1=ALU.subtract).then_inc(ex_made.sem, 1)
                    between()
                    for b in range(NB):
                        wait(e_out, s, 3 * b + 2)
                        wait(a_out, s, 3 + b)
                        nc.vector.tensor_tensor(tok(EV, b), tok(E[:, 1], b), tok(V, b), ALU.mult).then_inc(ev_made.sem, 1)
                        nc.vector.tensor_tensor_scan(BB[:, b, :], E[:, 0, b, :], E[:, 1, b, :], 0.0, ALU.mult, ALU.add
                                                     ).then_inc(bb_made.sem, 1)
                        wait(ev_made, s, b + 1)
                        nc.vector.tensor_tensor_scan(AA[:, b, :], E[:, 0, b, :], EV[:, b, :], 0.0, ALU.mult, ALU.add
                                                     ).then_inc(aa_made.sem, 1)
                    wait(e_out, s, 6)
                    th = tok2(E[:, 2])
                    stt = nc.vector.scalar_tensor_tensor
                    wait(bb_made, s, 2)
                    stt(out=tok2(PP), in0=th, scalar=1.0, in1=before2(BB), op0=ALU.add, op1=ALU.mult).then_inc(c1_made.sem, 1)
                    wait(aa_made, s, 2)
                    stt(out=tok2(EV), in0=th, scalar=-1.0, in1=tok2(V), op0=ALU.add, op1=ALU.mult).then_inc(n2_made.sem, 1)
                    wait(c1_made, s)
                    stt(out=tok2(K), in0=th, scalar=1.0, in1=before2(AA), op0=ALU.add, op1=ALU.mult).then_inc(n1_made.sem, 1)
                    stt(out=tok2(PP), in0=tok2(PP), scalar=1.0, in1=th, op0=ALU.add, op1=ALU.subtract).then_inc(den_made.sem, 1)
                    wait(n1_made, s)
                    nc.vector.tensor_tensor(tok2(K), tok2(K), tok2(EV), ALU.subtract).then_inc(nu_made.sem, 1)
                    wait(den_made, s)
                    nc.vector.reciprocal(tok2(BB), tok2(PP)).then_inc(inv_made.sem, 1)
                    wait(a_out, s, 6)
                    wait(nu_made, s)
                    stt(out=tok2(K), in0=tok2(R), scalar=1.0, in1=tok2(K), op0=ALU.add, op1=ALU.mult).then_inc(yr_made.sem, 1)
                    wait(yr_made, s)
                    wait(inv_made, s)
                    wait(wo_ready, later(s, -1))
                    nc.vector.tensor_tensor(ys[:, :, :].rearrange("p b (n t) -> p (b n) t", t=T), tok2(K), tok2(BB),
                                            ALU.mult).then_inc(ys_made.sem, 1)

                def step(s):
                    residual1(s)
                    statistics2(s)
                    if has(s, 2):
                        statistics1(later(s, 2))
                    norm2(s)
                    if has(s, 2):
                        norm1(later(s, 2))
                    mix_b(s)
                    if has(s, 1):
                        scan(later(s, 1), (lambda: mix_a(later(s, 2))) if has(s, 2) else (lambda: None))

                statistics1((0, 0))
                norm1((0, 0))
                statistics1((0, 1))
                mix_a((0, 0))
                norm1((0, 1))
                scan((0, 0), lambda: mix_a((0, 1)))
                with nc.vector.Fori(0, LAYERS - 1) as l:
                    for c in range(CHUNKS):
                        step((l, c))
                for c in range(CHUNKS):
                    step((LAYERS - 1, c))



def attention(nc, t, X, H0, H2, LG, exp_in, ident, half_neg):
    EPS = 1e-05
    HEADS, HD = 16, 16
    HB = HEADS // NB
    REP = 3
    HG = [(b, h, min(REP, HB - h)) for b in range(NB) for h in range(0, HB, REP)]
    NG = len(HG)
    RK = REP * T
    VC = HD + 1
    PAIRS = CI // 2
    SECOND = 64
    BOTH = SECOND + T
    AUG = 32 + T
    with ExitStack() as ctx:
        def sb(name, shape, dt=F32):
            return ctx.enter_context(nc.sbuf_tensor("at_" + name, shape, dt))

        def psum(name, shape, dt=F32):
            return ctx.enter_context(nc.psum_tensor("at_" + name, shape, dt))

        def made(name, per):
            return Made(ctx.enter_context(nc.semaphore("at_" + name)), per, 1)

        def sem(name):
            return ctx.enter_context(nc.semaphore("at_" + name))

        Wqk = sb("Wqk", [P, 4, NB, D])
        Wv = sb("Wv", [P, NB, D])
        Wp = sb("Wp", [P, NB, D])
        Wg = sb("Wg", [P, NB, 8])
        vec = sb("vec", [P, 4, NB])
        row = sb("row", [P, 2, D])
        cs = sb("cs", [P, 2, T])
        hmask = sb("hmask", [P, NB * HB])
        vmask = sb("vmask", [RK, HEADS])
        negk = sb("negk", [T, HB * T], BF16)
        identb = sb("identb", [P, P], BF16)
        sel = sb("sel", [AUG, NG, RK], BF16)
        st = sb("st", [P, 3, NT, 6])
        mv = sb("mv", [P, 3, NT, 2])
        vr = sb("vr", [P, 3, NT])
        rs = sb("rs", [P, 3, NT])
        S = sb("S", [P, NT, D])
        xn1 = sb("xn1", [P, NT, D])
        xn2 = sb("xn2", [P, NT, D])
        h1n = sb("h1n", [P, NB, CT])
        h1 = sb("h1", [P, NB, CT])
        h2 = sb("h2", [P, NB, CT])
        rot = sb("rot", [P, 2, 2, HALF])
        QKn = sb("QKn", [P, 2, NB, CT])
        QK = sb("QK", [P, 2, NB, CT])
        kbd = sb("kbd", [P, 2, 2, NB, HB, T])
        hr = sb("hr", [P, 2, 2, NB, RK])
        vbd = sb("vbd", [RK, 2, 2, HEADS, VC])
        mx = sb("mx", [P, 2, HEADS], BF16)
        aug = sb("aug", [AUG, 2, 2 * T], BF16)
        PT = sb("PT", [RK, 2, 2, NG * T])
        inv = sb("inv", [P, 2, HEADS])
        O = sb("O", [P, 2, D])
        aT = sb("aT", [P, NB, CT])
        zeros = sb("zeros", [P, 2 * N // CHUNKS // P * D])
        zero_rows = sem("zero_rows")
        exp_zeroed = sem("exp_zeroed")
        ps_a = psum("ps_a", [P, 4, 512])
        ps_st = psum("ps_st", [P, 512])
        ps_o = psum("ps_o", [P, 512])
        ps_v = psum("ps_v", [P, 512])
        ps_x = psum("ps_x", [P, 512])
        ps_mT = ps_st[:, 448:512].bitcast(BF16)
        ps_oT = ps_x[:, 128:128 + 2 * BOTH]

        w_in = sem("w_in")
        h2_made = sem("h2_made")
        h2_scaled = made("h2_scaled", NT)
        const = sem("const")
        carrier = sem("carrier")
        zero = sem("zero")
        summed = made("summed", NT)
        st_made = [made(f"st_made{k}", 1) for k in range(3)]
        mv_made = [made(f"mv_made{k}", 1) for k in range(3)]
        h0_made = made("h0_made", NT)
        xn1_made = made("xn1_made", NT)
        rot_made = made("rot_made", 16)
        qk_copied = made("qk_copied", 1)
        v_out = made("v_out", 2 * PAIRS)
        mx_made = made("mx_made", PAIRS)
        inv_made = made("inv_made", PAIRS)
        o_made = made("o_made", PAIRS)
        x_made = made("x_made", NT)
        xn2_made = made("xn2_made", NT)
        ve = [made(f"ve{k}", 1) for k in range(3)]
        rs_made = [made(f"rs_made{k}", 1) for k in range(3)]
        rope = made("rope", 8)
        kbd_made = made("kbd_made", 2 * PAIRS)
        t1_ready = made("t1_ready", len(GROUPS))
        qk_ready = made("qk_ready", 8)
        v_ready = made("v_ready", PAIRS)
        s_ready = made("s_ready", PAIRS)
        mT_ready = made("mT_ready", PAIRS)
        st_ready = made("st_ready", PAIRS)
        o_ready = made("o_ready", PAIRS)
        oT_ready = made("oT_ready", PAIRS)
        p_ready = made("p_ready", NT)
        t2_ready = made("t2_ready", len(GROUPS))
        lg_ready = made("lg_ready", NT)
        t1_out = made("t1_out", 2 * len(GROUPS))
        h1_copied = made("h1_copied", 1)
        hr_made = made("hr_made", 2 * PAIRS)
        mT_out = made("mT_out", PAIRS)
        e_out = made("e_out", PAIRS)
        oT_out = made("oT_out", PAIRS)
        t2_out = made("t2_out", 2 * len(GROUPS))
        lg_out = made("lg_out", 2)

        def credit(eng, *sems):
            for s in sems:
                eng.sem_inc(s.sem, s.per)

        combos = [(x, b, h) for x in range(2) for b in range(NB) for h in range(2)]
        SLOTS = {3: (0,), 4: (1,), 5: (2,), 6: (3,), 7: (4,), 8: (5,), 9: (6,), 10: (7,)}

        def tile(s, i):
            if isinstance(s[0], int):
                return slice((s[0] + s[1]) * NT + i, (s[0] + s[1]) * NT + i + 1)
            return bass.ds(s[0] * NT + (s[1] * NT + i), 1)

        def chunks(eng, front, first_pair, body):
            front((0, 0))
            first_pair((0, 0))
            with eng.Fori(0, CHUNKS - 1) as n:
                body((n, 0), (n, 1))
            body((CHUNKS - 1, 0), None)

        with nc.Block() as block:
            @block.sync
            def _(sp):
                for dst, name in ((Wqk, "Wqk"), (Wv, "Wv"), (Wp, "Wproj"), (Wg, "Wgate"), (vec, "ffn_vec"), (row, "ffn_rows"),
                                  (cs, "cos_sin"), (hmask, "head_mask"), (vmask, "value_mask"), (negk, "causal"),
                                  (identb, "identb"), (sel, "select")):
                    nc.sync.dma_start(dst[:], t[name]).then_inc(w_in, 16)
                for p in range(2):
                    for i in range(2):
                        nc.sync.dma_start(aug[32:AUG, p, i * T:(i + 1) * T], t["causalT"]).then_inc(w_in, 16)
                sp.wait_ge(zero_rows, 1)
                for part in range(CHUNKS):
                    rows = exp_in[part * (2 * N // CHUNKS):(part + 1) * (2 * N // CHUNKS), :]
                    nc.sync.dma_start(rows.rearrange("(p r) d -> p (r d)", p=P), zeros[:]).then_inc(exp_zeroed, 16)
                sp.wait_ge(exp_zeroed, 16 * CHUNKS)
            LOADS = 16 * (12 + 4)

            @block.gpsimd
            def _(pool):
                wait = lambda m, s, j=None: pool.wait_ge(m.sem, m.at(s, j))
                nc.gpsimd.memset(zeros[:], 0.0).then_inc(zero_rows, 1)
                nc.gpsimd.memset(mv[:], 1.0).then_inc(const, 1)
                nc.gpsimd.memset(LG[:], 0.0).then_inc(const, 1)
                nc.gpsimd.memset(aug[0:32, :, :], 0.0).then_inc(const, 1)
                credit(pool, *ve, *rs_made, rope, kbd_made)
                pool.wait_ge(w_in, LOADS)
                pool.wait_ge(const, 3)

                def root(s, k):
                    wait(mv_made[k], s)
                    pool.sem_inc(carrier, 1)
                    nc.gpsimd.tensor_scalar(vr[:, k, :], mv[:, k, :, 1], 1.0, EPS, ALU.mult, ALU.add).then_inc(ve[k].sem, 1)
                    wait(ve[k], s)
                    nc.gpsimd.tensor_tensor(rs[:, k, :], vr[:, k, :], half_neg[:, 0:NT], ALU.pow).then_inc(rs_made[k].sem, 1)

                def add_rotated(s, js):
                    for j in js:
                        x, b, h = combos[j]
                        wait(rot_made, s, 2 * j + 2)
                        if j == 0:
                            wait(qk_copied, later(s, -1))
                        nc.gpsimd.tensor_tensor(QKn[:, x, b, h * HALF:(h + 1) * HALF], rot[:, j % 2, 0, :], rot[:, j % 2, 1, :],
                                                ALU.add).then_inc(rope.sem, 1)

                def keys_by_head(s, p):
                    if p == 0:
                        wait(qk_copied, s)
                        wait(st_ready, later(s, -1))
                    if p >= 2:
                        wait(st_ready, s, p - 1)
                    for i in range(2):
                        first = (2 * p + i) * T
                        for b in range(NB):
                            k = QK[:, 1, b:b + 1, first:first + T].to_broadcast([P, HB, T])
                            m = hmask[:, b * HB:(b + 1) * HB].rearrange("p (h a) -> p h a", a=1).to_broadcast([P, HB, T])
                            a = nc.gpsimd.tensor_tensor(kbd[:, p % 2, i, b, :, :], k, m, ALU.mult)
                        a.then_inc(kbd_made.sem, 1)

                def front(s):
                    root(s, 0)
                    root(s, 1)
                    add_rotated(s, range(8))

                def first_pair(s):
                    keys_by_head(s, 0)

                def body(s, nxt):
                    for k in range(PAIRS + 4):
                        if nxt:
                            add_rotated(nxt, SLOTS.get(k - 1, ()))
                        if k + 1 < PAIRS:
                            keys_by_head(s, k + 1)
                        if nxt and k < 2:
                            root(nxt, k)
                    if nxt:
                        first_pair(nxt)
                    root(s, 2)

                chunks(nc.gpsimd, front, first_pair, body)

            @block.tensor
            def _(pe):
                wait = lambda m, s, j=None: pe.wait_ge(m.sem, m.at(s, j))
                credit(pe, t1_ready, qk_ready, v_ready, s_ready, mT_ready, st_ready, o_ready, oT_ready, p_ready, t2_ready,
                       lg_ready)
                pe.wait_ge(w_in, LOADS)
                pe.wait_ge(const, 3)
                pe.wait_ge(zero, 7)

                def transposes(xn, made_, ready, free, s):
                    for q, tiles in enumerate(GROUPS):
                        wait(made_, s, tiles[-1] + 1)
                        free(q)
                        if TILES[tiles[0]][1] < P:
                            pe.sem_inc(carrier, 1)
                        width = sum(TILES[i][1] for i in tiles)
                        for i in tiles:
                            r = TILES[i][1]
                            at = TILES[i][0] - TILES[tiles[0]][0]
                            for b in range(NB):
                                a = nc.tensor.transpose(ps_a[:, q % 2, b * width + at:b * width + at + r],
                                                        xn[0:r, i, b * P:(b + 1) * P], ident[0:r, 0:r])
                        a.then_inc(ready.sem, 1)

                def queries_keys(s, js, spread):
                    for j in js:
                        x, b, h = combos[j]
                        if j == 0:
                            wait(t1_out, s)
                        if j >= 1 + spread:
                            wait(rot_made, s, 2 * (j - spread))
                        for v in range(2):
                            for kb in range(NB):
                                a = nc.tensor.matmul(ps_a[:, (2 * (j % 2) if spread else 0) + v, 0:HALF],
                                                     Wqk[:, 2 * x + v, kb, b * P:(b + 1) * P],
                                                     h1n[:, kb, h * HALF:(h + 1) * HALF], start=(kb == 0), stop=(kb == NB - 1))
                        a.then_inc(qk_ready.sem, 1)

                def values_scores(s, p):
                    if p >= 1:
                        wait(v_out, s, 2 * p)
                    else:
                        wait(v_out, later(s, -1))
                    wait(hr_made, s, 2 * p + 2)
                    for i in range(2):
                        for kb in range(NB):
                            a = nc.tensor.matmul(ps_v[0:RK, i * D:(i + 1) * D], hr[:, p % 2, i, kb, :], Wv[:, kb, :],
                                                 start=(kb == 0), stop=(kb == NB - 1))
                    a.then_inc(v_ready.sem, 1)
                    wait(kbd_made, s, 2 * p + 2)
                    if p >= 1:
                        wait(mx_made, s, p)
                    else:
                        wait(mx_made, later(s, -1))
                        wait(rot_made, s)
                    for i in range(2):
                        first = (2 * p + i) * T
                        for b in range(NB):
                            dst = ps_a[SECOND * i:SECOND * i + T, 2 + b, 0:HB * T].rearrange("p (h k) -> p h k", k=T)
                            nc.tensor.matmul(dst, QK[:, 0, b, first:first + T], kbd[:, p % 2, i, b, :, :],
                                             start=True, stop=False)
                            a = nc.tensor.matmul(dst, identb[0:T, 0:T], negk[:, :].rearrange("p (h k) -> p h k", k=T),
                                                 start=False, stop=True)
                    a.then_inc(s_ready.sem, 1)

                def maxima(s, p):
                    wait(mx_made, s, p + 1)
                    if p >= 1:
                        wait(mT_out, s, p)
                    nc.tensor.transpose(ps_mT[0:HEADS, 0:BOTH], mx[0:BOTH, p % 2, :], identb[0:BOTH, 0:BOTH]
                                        ).then_inc(mT_ready.sem, 1)

                def scores_transposed(s, p):
                    wait(mT_out, s, p + 1)
                    wait(e_out, s, p) if p >= 1 else wait(e_out, later(s, -1))
                    for i in range(2):
                        first = (2 * p + i) * T
                        for g, (b, h, m) in enumerate(HG):
                            dst = ps_st[0:m * T, (i * NG + g) * T:(i * NG + g + 1) * T]
                            nc.tensor.matmul(dst, kbd[:, p % 2, i, b, h:h + m, :].rearrange("p h k -> p (h k)"), QK[:, 0, b, first:first + T],
                                             start=True, stop=False)
                            a = nc.tensor.matmul(dst, sel[:, g, 0:m * T], aug[:, p % 2, i * T:(i + 1) * T], start=False, stop=True)
                    a.then_inc(st_ready.sem, 1)

                def outputs(s, p):
                    wait(e_out, s, p + 1)
                    wait(v_out, s, 2 * p + 2)
                    wait(o_made, s, p) if p >= 1 else wait(o_made, later(s, -1))
                    for i in range(2):
                        for g, (b, h, m) in enumerate(HG):
                            h0 = b * HB + h
                            a = nc.tensor.matmul(ps_o[SECOND * i:SECOND * i + T, h0 * VC:(h0 + m) * VC],
                                                 PT[0:m * T, p % 2, i, g * T:(g + 1) * T],
                                                 vbd[0:m * T, p % 2, i, h0:h0 + m, :].rearrange("p h v -> p (h v)"),
                                                 start=True, stop=True)
                    a.then_inc(o_ready.sem, 1)

                def outputs_transposed(s, p):
                    wait(o_made, s, p + 1)
                    wait(oT_out, s, p) if p >= 1 else wait(oT_out, later(s, -1))
                    for b in range(NB):
                        a = nc.tensor.transpose(ps_oT[:, b * BOTH:(b + 1) * BOTH], O[0:BOTH, p % 2, b * P:(b + 1) * P],
                                                ident[0:BOTH, 0:BOTH])
                    a.then_inc(oT_ready.sem, 1)

                def t1(s, free_banks):
                    transposes(xn1, xn1_made, t1_ready, lambda q: free_banks() if q < 2 else wait(t1_out, s, 2), s)

                def front(s):
                    t1(s, lambda: None)
                    queries_keys(s, range(8), True)

                def first_pair(s):
                    values_scores(s, 0)

                def body(s, nxt):
                    def free():
                        wait(lg_out, later(s, -1))
                        wait(rot_made, s)

                    for k in range(PAIRS + 2):
                        if k >= 2:
                            outputs(s, k - 2)
                        if nxt and k == 3:
                            t1(nxt, free)
                        if 1 <= k <= PAIRS:
                            maxima(s, k - 1)
                        if 1 <= k < PAIRS:
                            values_scores(s, k)
                        if k >= 2:
                            outputs_transposed(s, k - 2)
                        if 1 <= k <= PAIRS:
                            scores_transposed(s, k - 1)
                        if nxt:
                            queries_keys(nxt, SLOTS.get(k, ()), False)
                    if nxt:
                        queries_keys(nxt, SLOTS[PAIRS + 2], False)
                    wait(oT_out, s)
                    if nxt:
                        wait(rot_made, nxt)
                    for i, (first, r) in enumerate(TILES):
                        if i >= 2:
                            wait(x_made, s, i - 1)
                        for b in range(NB):
                            a = nc.tensor.matmul(ps_a[0:r, i % 2, 0:D], aT[:, b, first:first + r], Wp[:, b, :], start=(b == 0),
                                                 stop=(b == NB - 1))
                        a.then_inc(p_ready.sem, 1)
                    if nxt:
                        first_pair(nxt)
                    transposes(xn2, xn2_made, t2_ready,
                               lambda q: wait(x_made, s) if q < 2 else wait(t2_out, s, 2), s)
                    wait(t2_out, s)
                    for i, (first, r) in enumerate(TILES):
                        for b in range(NB):
                            a = nc.tensor.matmul(ps_a[0:r, 1, 8 * i:8 * i + 8], h2[:, b, first:first + r], Wg[:, b, :],
                                                 start=(b == 0), stop=(b == NB - 1))
                        a.then_inc(lg_ready.sem, 1)

                chunks(nc.tensor, front, first_pair, body)

            @block.scalar
            def _(act):
                wait = lambda m, s, j=None: act.wait_ge(m.sem, m.at(s, j))
                credit(act, t1_out, h1_copied, hr_made, mT_out, e_out, oT_out, t2_out, lg_out)
                act.wait_ge(w_in, LOADS)
                act.wait_ge(const, 3)
                act.wait_ge(zero, 7)

                def evict(ready, h, k, out_, s):
                    for q, tiles in enumerate(GROUPS):
                        width = sum(TILES[i][1] for i in tiles)
                        first = TILES[tiles[0]][0]
                        wait(ready, s, q + 1)
                        for b in range(NB):
                            nc.scalar.activation(h[:, b, first:first + width], ps_a[:, q % 2, b * width:(b + 1) * width],
                                                 ACT.Identity, bias=vec[:, k + 1, b:b + 1], scale=vec[:, k, b:b + 1]
                                                 ).then_inc(out_.sem, 1)

                def front(s):
                    wait(h1_copied, later(s, -1))
                    wait(qk_ready, later(s, -1))
                    evict(t1_ready, h1n, 0, t1_out, s)

                def repeated(s, p):
                    if p == 0:
                        wait(h1_copied, s)
                    wait(v_ready, s, p - 1) if p >= 2 else wait(v_ready, later(s, -1))
                    for i in range(2):
                        first = (2 * p + i) * T
                        src = h1[:, :, first:first + T].rearrange("p b (a t) -> p b a t", a=1)
                        nc.scalar.activation(hr[:, p % 2, i, :, :].rearrange("p b (a t) -> p b a t", t=T),
                                             src.to_broadcast([P, NB, REP, T]), ACT.Copy).then_inc(hr_made.sem, 1)

                def maxima(s, p):
                    wait(mT_ready, s, p + 1)
                    wait(st_ready, s, p - 1) if p >= 2 else wait(st_ready, later(s, -1))
                    nc.scalar.activation(aug[0:HEADS, p % 2, :].rearrange("p (i q) -> p i q", i=2),
                                         ps_mT[0:HEADS, 0:2 * SECOND].rearrange("p (i q) -> p i q", i=2)[:, :, 0:T],
                                         ACT.Copy).then_inc(mT_out.sem, 1)

                def exponentials(s, p):
                    wait(st_ready, s, p + 1)
                    wait(o_ready, s, p - 1) if p >= 2 else wait(o_ready, later(s, -1))
                    nc.scalar.activation(PT[:, p % 2, :, :], ps_st[0:RK, 0:2 * NG * T].rearrange("p (i x) -> p i x", i=2),
                                         ACT.Exp, scale=float(HD) ** -0.5).then_inc(e_out.sem, 1)

                def transposed(s, p):
                    wait(oT_ready, s, p + 1)
                    if p == 0:
                        wait(p_ready, later(s, -1))
                    for b in range(NB):
                        src = ps_oT[:, b * BOTH:b * BOTH + BOTH]
                        for i in range(2):
                            a = nc.scalar.activation(aT[:, b, (2 * p + i) * T:(2 * p + i + 1) * T],
                                                     src[:, SECOND * i:SECOND * i + T], ACT.Copy)
                    a.then_inc(oT_out.sem, 1)

                def first_pair(s):
                    wait(hr_made, later(s, -1))
                    wait(t1_out, s)
                    nc.scalar.activation(h1[:], h1n[:], ACT.Copy).then_inc(h1_copied.sem, 1)
                    repeated(s, 0)

                def body(s, nxt):
                    for k in range(PAIRS + 2):
                        if nxt and k == 3:
                            front(nxt)
                        if k + 1 < PAIRS:
                            repeated(s, k + 1)
                        if 1 <= k <= PAIRS:
                            maxima(s, k - 1)
                        if k >= 2:
                            transposed(s, k - 2)
                        if 1 <= k <= PAIRS:
                            exponentials(s, k - 1)
                    if nxt:
                        first_pair(nxt)
                    wait(lg_ready, later(s, -1))
                    evict(t2_ready, h2, 2, t2_out, s)
                    wait(lg_ready, s)
                    for first, tiles, r in ((0, NT - 1, P), (NT - 1, 1, TILES[-1][1])):
                        of = (slice(s[0] * NT + first, s[0] * NT + first + tiles) if isinstance(s[0], int)
                              else bass.ds(s[0] * NT + first, tiles))
                        nc.scalar.activation(LG[0:r, of, :],
                                             ps_a[0:r, 1, 8 * first:8 * (first + tiles)].rearrange("p (i e) -> p i e", e=8),
                                             ACT.Copy).then_inc(lg_out.sem, 1)

                chunks(nc.scalar, front, first_pair, body)

            @block.vector
            def _(dve):
                wait = lambda m, s, j=None: dve.wait_ge(m.sem, m.at(s, j))
                nc.vector.memset(ps_a[:], 0.0).then_inc(zero, 1)
                nc.vector.memset(ps_st[:], 0.0).then_inc(zero, 1)
                nc.vector.memset(ps_o[:], 1.0).then_inc(zero, 1)
                credit(dve, summed, *st_made, *mv_made, h0_made, xn1_made, rot_made, qk_copied, h2_scaled, v_out, mx_made, inv_made, o_made, x_made,
                       xn2_made)
                dve.wait_ge(w_in, LOADS)
                dve.wait_ge(const, 3)
                for p in range(2):
                    for i in range(2):
                        nc.vector.tensor_copy(vbd[:, p, i, :, HD:VC], vmask[:, :].rearrange("p (h a) -> p h a", a=1)
                                              ).then_inc(zero, 1)
                dve.wait_ge(zero, 7)

                def stats(s, k, src, ready):
                    for i, (_, r) in enumerate(TILES):
                        wait(ready, s, i + 1)
                        dve.sem_inc(carrier, 1)
                        a = nc.vector.bn_stats(st[0:r, k, i, :], src(i, r))
                    a.then_inc(st_made[k].sem, 1)
                    wait(st_made[k], s)
                    dve.sem_inc(carrier, 1)
                    for i, (_, r) in enumerate(TILES):
                        a = nc.vector.bn_aggr(mv[0:r, k, i, :], st[0:r, k, i, :])
                    a.then_inc(mv_made[k].sem, 1)

                def normed(s, k, src, dst, done):
                    wait(mv_made[k], s)
                    wait(rs_made[k], s)
                    for i, (_, r) in enumerate(TILES):
                        nc.vector.tensor_scalar(dst(i, r), src(i, r), mv[0:r, k, i, 0:1], rs[0:r, k, i:i + 1],
                                                ALU.subtract, ALU.mult).then_inc(done.sem, 1)

                def front_norms(s, k):
                    h0 = lambda i, r: H0[0:r, tile(s, i), :]
                    if k == 0:
                        for i, (_, r) in enumerate(TILES):
                            nc.vector.tensor_tensor(S[0:r, i:i + 1, :], X[0:r, tile(s, i), :], h0(i, r), ALU.add
                                                    ).then_inc(summed.sem, 1)
                        stats(s, 0, lambda i, r: S[0:r, i, :], summed)
                    if k == 1:
                        normed(s, 0, lambda i, r: S[0:r, i:i + 1, :], h0, h0_made)
                        stats(s, 1, h0, h0_made)
                    if k == 2:
                        wait(t1_ready, later(s, -1))
                        normed(s, 1, h0, lambda i, r: xn1[0:r, i:i + 1, :], xn1_made)

                def rotate(s, js, spread):
                    for j in js:
                        wait(qk_ready, s, j + 1)
                        wait(rope, s, j - 1) if j >= 2 else wait(rope, later(s, -1))
                        for v in range(2):
                            nc.vector.tensor_tensor(rot[:, j % 2, v, :].rearrange("p (n t) -> p n t", t=T),
                                                    ps_a[:, (2 * (j % 2) if spread else 0) + v, 0:HALF]
                                                    .rearrange("p (n t) -> p n t", t=T),
                                                    cs[:, v:v + 1, :].to_broadcast([P, CI // 2, T]), ALU.mult
                                                    ).then_inc(rot_made.sem, 1)

                def values(s, p):
                    wait(v_ready, s, p + 1)
                    wait(o_ready, s, p - 1) if p >= 2 else wait(o_ready, later(s, -1))
                    m = vmask[:, :].rearrange("p (h a) -> p h a", a=1).to_broadcast([RK, HEADS, HD])
                    for i in range(2):
                        nc.vector.tensor_tensor(vbd[:, p % 2, i, :, 0:HD],
                                                ps_v[0:RK, i * D:(i + 1) * D].rearrange("p (h v) -> p h v", v=HD), m, ALU.mult
                                                ).then_inc(v_out.sem, 1)

                def maxima(s, p):
                    wait(s_ready, s, p + 1)
                    wait(mT_ready, s, p - 1) if p >= 2 else wait(mT_ready, later(s, -1))
                    nc.vector.tensor_reduce(mx[0:BOTH, p % 2, :].rearrange("p (b h) -> p b h", b=NB),
                                            ps_a[0:BOTH, 2:4, 0:HB * T].rearrange("p b (h k) -> p b h k", k=T), AX.X, ALU.max
                                            ).then_inc(mx_made.sem, 1)

                def normalise(s, p):
                    wait(o_ready, s, p + 1)
                    o = ps_o[0:BOTH, 0:HEADS * VC].rearrange("p (h v) -> p h v", v=VC)
                    nc.vector.reciprocal(inv[0:BOTH, p % 2, :].rearrange("p (h a) -> p h a", a=1), o[:, :, HD:VC]
                                         ).then_inc(inv_made.sem, 1)
                    wait(inv_made, s, p + 1)
                    wait(oT_ready, s, p - 1) if p >= 2 else wait(oT_ready, later(s, -1))
                    nc.vector.tensor_tensor(O[0:BOTH, p % 2, :].rearrange("p (h v) -> p h v", v=HD), o[:, :, 0:HD],
                                            inv[0:BOTH, p % 2, :].rearrange("p (h a) -> p h a", a=1
                                                                            ).to_broadcast([BOTH, HEADS, HD]), ALU.mult
                                            ).then_inc(o_made.sem, 1)

                def front(s):
                    for k in range(3):
                        front_norms(s, k)
                    rotate(s, range(8), True)

                def copy_qk(s):
                    wait(rope, s)
                    wait(st_ready, later(s, -1))
                    wait(kbd_made, later(s, -1))
                    nc.vector.tensor_copy(QK[:], QKn[:]).then_inc(qk_copied.sem, 1)

                def first_pair(s):
                    copy_qk(s)
                    values(s, 0)
                    maxima(s, 0)

                def body(s, nxt):
                    for k in range(PAIRS + 4):
                        if 2 <= k < PAIRS + 2:
                            normalise(s, k - 2)
                        if nxt:
                            rotate(nxt, SLOTS.get(k - 1, ()), False)
                        if 1 <= k < PAIRS:
                            values(s, k)
                            maxima(s, k)
                        if nxt and k < 3:
                            front_norms(nxt, k)
                    if nxt:
                        copy_qk(nxt)
                    for i, (_, r) in enumerate(TILES):
                        wait(p_ready, s, i + 1)
                        nc.vector.tensor_tensor(X[0:r, tile(s, i), :], ps_a[0:r, i % 2:i % 2 + 1, 0:D], H0[0:r, tile(s, i), :], ALU.add
                                                ).then_inc(x_made.sem, 1)
                    x = lambda i, r: X[0:r, tile(s, i), :]
                    stats(s, 2, x, x_made)
                    if nxt:
                        values(nxt, 0)
                    wait(t2_ready, later(s, -1))
                    normed(s, 2, x, lambda i, r: xn2[0:r, i:i + 1, :], xn2_made)
                    if nxt:
                        maxima(nxt, 0)
                    wait(xn2_made, s)
                    for i, (_, r) in enumerate(TILES):
                        nc.vector.tensor_tensor(H2[0:r, tile(s, i), :], xn2[0:r, i:i + 1, :], row[0:r, 0:1, :], ALU.mult
                                                ).then_inc(h2_scaled.sem, 1)
                    for i, (_, r) in enumerate(TILES):
                        wait(h2_scaled, s, i + 1)
                        a = nc.vector.tensor_tensor(H2[0:r, tile(s, i), :], H2[0:r, tile(s, i), :], row[0:r, 1:2, :], ALU.add)
                    a.then_inc(h2_made, 1)

                chunks(nc.vector, front, first_pair, body)


def ffn_arrays(a, blocks):
    import numpy as np

    F = "L0_ffn_"
    hb, hd, rep = 8, 16, 3
    bf16 = mybir.dt.np(BF16)
    w = a[F + "Wqkv"].reshape(D, 16, 3, hd)
    q, k, v = (w[:, :, i] for i in range(3))
    swap = lambda m: np.concatenate([m[..., hd // 2:], m[..., :hd // 2]], -1)
    rows = lambda m: m.reshape(NB, P, -1).transpose(1, 0, 2)
    freq = (1.0 / 10000.0 ** (np.arange(0, hd, 2, dtype=np.float32) / np.float32(hd))).astype(np.float32)
    ang = np.arange(T, dtype=np.float32)[:, None] * freq
    cos, sin = np.cos(ang).astype(np.float32).T, np.sin(ang).astype(np.float32).T
    cs = np.stack([np.tile(np.concatenate([cos, cos]), (hb, 1)), np.tile(np.concatenate([-sin, sin]), (hb, 1))], 1)
    head = np.arange(P) // hd
    rep_of = (np.arange(16) % hb) % rep
    groups = [(b, h, min(rep, hb - h)) for b in range(NB) for h in range(0, hb, rep)]
    sel = np.zeros((32 + T, len(groups), rep * T), np.float32)
    for g, (b, h, m) in enumerate(groups):
        for r in range(m):
            sel[b * hb + h + r, g, r * T:(r + 1) * T] = -1
            sel[32 + np.arange(T), g, r * T + np.arange(T)] = 1
    later_key = np.where(np.arange(T)[None, :] > np.arange(T)[:, None], np.float32(-1e30), np.float32(0))
    return {
        "Wqk": np.stack([rows(np.ascontiguousarray(m).reshape(D, D)) for m in (q, swap(q), k, swap(k))], 1),
        "Wv": rows(v.reshape(D, D)),
        "Wproj": rows(a[F + "Wproj"]),
        "Wgate": rows(a[F + "Wgate"]),
        "ffn_vec": np.stack([blocks(a[F + n]) for n in ("ln1_g", "ln1_b", "ln2_g", "ln2_b")], 1),
        "ffn_rows": np.broadcast_to(np.stack([a[F + "ln2_g"], a[F + "ln2_b"]]), (P, 2, D)),
        "cos_sin": cs,
        "head_mask": np.tile((head[:, None] == np.arange(hb)[None, :]).astype(np.float32), (1, NB)),
        "value_mask": (np.arange(rep * T)[:, None] // T == rep_of[None, :]).astype(np.float32),
        "causal": np.tile(later_key, (1, hb)).astype(bf16),
        "causalT": later_key.T.astype(bf16),
        "identb": np.eye(P).astype(bf16),
        "select": sel.astype(bf16),
    }


def experts(nc, t, X, H0, H2, LG, exp_in, exp_out, out):
    EPS = 1e-05
    E = 8
    CAPACITY = CT
    assert CAPACITY == 2 * N // E
    TT = CHUNKS * NT
    with ExitStack() as ctx:
        def sb(name, shape, dt=F32):
            return ctx.enter_context(nc.sbuf_tensor("ex_" + name, shape, dt))

        def sem(name):
            return ctx.enter_context(nc.semaphore("ex_" + name))

        iota8 = sb("iota8", [P, E])
        absent = sb("absent", [P, TT, 2])
        carry = sb("carry", [P, E, TT])
        spare = sb("spare", [P, 2, TT])
        upto = sb("upto", [P, P], BF16)
        ones = sb("ones", [P, P], BF16)
        top = sb("top", [P, TT])
        ex = sb("ex", [P, TT, E])
        total = sb("total", [P, TT])
        inv = sb("inv", [P, TT])
        gates = sb("gates", [P, TT, E])
        best = sb("best", [P, TT, 8])
        which = sb("which", [P, TT, 8], mybir.dt.uint32)
        who = sb("who", [P, TT, 2])
        chosen = sb("chosen", [P, 2, E, TT])
        mask = sb("mask", [P, E, TT])
        maskb = sb("maskb", [P, E, TT], BF16)
        upto_tile = sb("upto_tile", [P, E, TT])
        before = sb("before", [P, E, TT], BF16)
        place = sb("place", [P, 2, E, TT])
        pos = sb("pos", [P, 2, TT])
        keep = sb("keep", [P, 2, TT])
        slot = sb("slot", [P, 2, TT])
        gate = sb("gate", [P, 2, TT])
        dst = sb("dst", [P, 2, TT])
        src = sb("src", [P, 2, TT])
        dst_i = sb("dst_i", [P, 2, TT], mybir.dt.uint32)
        src_i = sb("src_i", [P, 2, TT], mybir.dt.uint32)
        c_in = sem("c_in")
        d = sem("d")
        logits_exp = sem("logits_exp")
        masks_made = sem("masks_made")
        counted = sem("counted")
        scattered = sem("scattered")

        with nc.psum_tensor("ex_ps_pos", [P, 512], F32) as ps_pos, nc.Block() as block:
            @block.sync
            def _(sp):
                for buf, name in ((iota8, "iota8"), (absent, "absent"), (carry, "carry"), (spare, "spare"), (upto, "upto"),
                                  (ones, "onesb")):
                    nc.sync.dma_start(buf[:], t[name]).then_inc(c_in, 16)

            count = [0]

            @block.vector
            def _(dve):
                def then(ins):
                    count[0] += 1
                    ins.then_inc(d, 1)
                    dve.wait_ge(d, count[0])

                V = nc.vector
                by_e = lambda x: x.rearrange("p (n a) -> p n a", a=1).to_broadcast([P, TT, E])
                dve.wait_ge(c_in, 16 * 6)
                then(V.tensor_reduce(top[:], LG[:], AX.X, ALU.max))
                then(V.tensor_tensor(ex[:], LG[:], by_e(top[:]), ALU.subtract))
                dve.wait_ge(logits_exp, 1)
                then(V.tensor_reduce(total[:], ex[:], AX.X, ALU.add))
                then(V.reciprocal(inv[:], total[:]))
                then(V.tensor_tensor(gates[:], ex[:], by_e(inv[:]), ALU.mult))
                for i in range(TT):
                    a = V.max(best[:, i, :], gates[:, i, :])
                then(a)
                for i in range(TT):
                    a = V.max_index(which[:, i, :], best[:, i, :], gates[:, i, :])
                then(a)
                then(V.tensor_copy(who[:], which[:, :, 0:2]))
                then(V.tensor_tensor(who[:], who[:], absent[:], ALU.add))
                for k in range(2):
                    a = V.tensor_tensor(chosen[:, k], iota8[:].rearrange("p (e a) -> p e a", a=1).to_broadcast([P, E, TT]),
                                        who[:, :, k:k + 1].rearrange("p n a -> p a n").to_broadcast([P, E, TT]), ALU.is_equal)
                then(a)
                then(V.tensor_tensor(mask[:], chosen[:, 0], chosen[:, 1], ALU.add))
                flat = lambda x: x.rearrange("p e n -> p (e n)")
                V.tensor_copy(maskb[:], mask[:])
                then(V.tensor_tensor_scan(flat(upto_tile[:]), flat(carry[:]), flat(mask[:]), 0.0, ALU.mult, ALU.add))
                V.tensor_tensor(before[:], upto_tile[:], mask[:], ALU.subtract).then_inc(masks_made, 1)
                dve.wait_ge(counted, 1)
                for k in range(2):
                    a = V.tensor_tensor(place[:, k], ps_pos[:, 0:E * TT].rearrange("p (e n) -> p e n", e=E), chosen[:, k], ALU.mult)
                then(a)
                for k in range(2):
                    a = V.tensor_reduce(pos[:, k, :], place[:, k].rearrange("p e n -> p n e"), AX.X, ALU.add)
                then(a)
                V.tensor_scalar(keep[:], pos[:], float(CAPACITY), None, ALU.is_le)
                then(V.scalar_tensor_tensor(out=slot[:], in0=who[:].rearrange("p n k -> p k n"), scalar=float(CAPACITY), in1=pos[:],
                                            op0=ALU.mult, op1=ALU.add))
                then(V.tensor_scalar(slot[:], slot[:], -1.0, None, ALU.add))
                V.tensor_tensor(dst[:], slot[:], spare[:], ALU.subtract)
                V.tensor_tensor(gate[:], best[:, :, 0:2].rearrange("p n k -> p k n"), keep[:], ALU.mult)
                then(V.tensor_tensor(src[:], slot[:], keep[:], ALU.mult))
                then(V.tensor_tensor(dst[:], dst[:], keep[:], ALU.mult))
                then(V.tensor_tensor(dst[:], dst[:], spare[:], ALU.add))
                V.tensor_copy(src_i[:], src[:])
                then(V.tensor_copy(dst_i[:], dst[:]))
            INDICES = count[0]

            @block.scalar
            def _(act):
                act.wait_ge(d, 2)
                nc.scalar.activation(ex[:], ex[:], ACT.Exp).then_inc(logits_exp, 1)

            @block.tensor
            def _(pe):
                pe.wait_ge(masks_made, 1)
                nc.tensor.matmul(ps_pos[:, 0:E * TT], upto[:], maskb[:].rearrange("p e n -> p (e n)"), start=True, stop=False)
                nc.tensor.matmul(ps_pos[:, 0:E * TT], ones[:], before[:].rearrange("p e n -> p (e n)"), start=False, stop=True
                                 ).then_inc(counted, 1)

            @block.gpsimd
            def _(pool):
                pool.wait_ge(d, INDICES)
                for k in range(2):
                    for i in range(TT):
                        r = TILES[i % NT][1]
                        nc.gpsimd.indirect_dma_start(out=exp_in, out_offset=bass.IndirectOffsetOnAxis(ap=dst_i[0:r, k, i:i + 1], axis=0),
                                                     in_=H2[0:r, i, :], in_offset=None).then_inc(scattered, 16)
                pool.wait_ge(scattered, 16 * 2 * TT)

        expert_products(nc, t, exp_in, exp_out)

        got = sb("got", [P, TT, 2, D])
        S = sb("S", [P, TT, D])
        st = sb("st", [P, TT, 6])
        mv = sb("mv", [P, TT, 2])
        vr = sb("vr", [P, TT])
        rs = sb("rs", [P, TT])
        y = sb("y", [P, TT, D])
        gathered = [sem(f"gathered{c}") for c in range(CHUNKS)]
        added = sem("added")
        st_made = sem("st_made")
        mv_made = sem("mv_made")
        ve = sem("ve")
        rs_made = sem("rs_made")
        y_made = sem("y_made")
        stored = sem("stored")
        ones_in = sem("ones_in")
        with nc.Block() as block:
            @block.gpsimd
            def _(pool):
                nc.gpsimd.memset(mv[:], 1.0).then_inc(ones_in, 1)
                nc.gpsimd.memset(keep[:], -0.5).then_inc(ones_in, 1)

                def gather(c):
                    for i in range(c * NT, (c + 1) * NT):
                        for k in range(2):
                            nc.gpsimd.indirect_dma_start(out=got[0:TILES[i % NT][1], i, k, :], out_offset=None, in_=exp_out,
                                                         in_offset=bass.IndirectOffsetOnAxis(
                                                             ap=src_i[0:TILES[i % NT][1], k, i:i + 1], axis=0)
                                                         ).then_inc(gathered[c], 16)

                def root(c):
                    part = slice(c * NT, (c + 1) * NT)
                    pool.wait_ge(mv_made, c + 1)
                    nc.gpsimd.tensor_scalar(vr[:, part], mv[:, part, 1], 1.0, EPS, ALU.mult, ALU.add).then_inc(ve, 1)
                    pool.wait_ge(ve, c + 1)
                    nc.gpsimd.tensor_tensor(rs[:, part], vr[:, part], keep[:, 0, 0:NT], ALU.pow).then_inc(rs_made, 1)

                gather(0)
                pool.wait_ge(ones_in, 2)
                for c in range(1, CHUNKS):
                    gather(c)
                    root(c - 1)
                root(CHUNKS - 1)

            @block.vector
            def _(dve):
                V = nc.vector
                dve.wait_ge(ones_in, 2)
                tiles = lambda c: [(c * NT + i, r) for i, (_, r) in enumerate(TILES)]
                for c in range(CHUNKS):
                    for i, r in tiles(c):
                        V.tensor_tensor(S[0:r, i, :], X[0:r, i, :], H0[0:r, i, :], ALU.add).then_inc(added, 1)
                for c in range(CHUNKS):
                    dve.wait_ge(gathered[c], 16 * 2 * NT)
                    for k in range(2):
                        for i, r in tiles(c):
                            dve.wait_ge(added, TT + (2 * c + k - 1) * NT + i % NT + 1 if k else i + 1)
                            V.scalar_tensor_tensor(out=S[0:r, i, :], in0=got[0:r, i, k, :], scalar=gate[0:r, k, i:i + 1],
                                                   in1=S[0:r, i, :], op0=ALU.mult, op1=ALU.add).then_inc(added, 1)
                    for i, r in tiles(c):
                        dve.wait_ge(added, TT + (2 * c + 1) * NT + i % NT + 1)
                        a = V.bn_stats(st[0:r, i, :], S[0:r, i, :])
                    a.then_inc(st_made, 1)
                    dve.wait_ge(st_made, c + 1)
                    for i, r in tiles(c):
                        a = V.bn_aggr(mv[0:r, i, :], st[0:r, i, :])
                    a.then_inc(mv_made, 1)
                    dve.wait_ge(mv_made, c + 1)
                    dve.wait_ge(rs_made, c + 1)
                    for i, r in tiles(c):
                        a = V.tensor_scalar(y[0:r, i, :], S[0:r, i, :], mv[0:r, i, 0:1], rs[0:r, i:i + 1], ALU.subtract, ALU.mult)
                    a.then_inc(y_made, 1)

            @block.sync
            def _(sp):
                for c in range(CHUNKS):
                    sp.wait_ge(y_made, c + 1)
                    rows = out[c * CT:(c + 1) * CT, :]
                    nc.sync.dma_start(rows[0:4 * P, :].rearrange("(i p) d -> p i d", p=P), y[:, c * NT:c * NT + 4, :]
                                      ).then_inc(stored, 16)
                    nc.sync.dma_start(rows[4 * P:CT, :], y[0:CT - 4 * P, c * NT + 4, :]).then_inc(stored, 16)
                sp.wait_ge(stored, 32 * CHUNKS)


def expert_products(nc, t, exp_in, exp_out):
    E = 8
    TURN = 2
    with ExitStack() as ctx:
        def sb(name, shape, dt=F32):
            return ctx.enter_context(nc.sbuf_tensor("ep_" + name, shape, dt))

        def psum(name, shape, dt=F32):
            return ctx.enter_context(nc.psum_tensor("ep_" + name, shape, dt))

        def made(name, per):
            return Made(ctx.enter_context(nc.semaphore("ep_" + name)), per, TURN, TURN)

        ident = sb("ident", [P, P])
        W1 = sb("W1", [P, TURN, NB, FF])
        W2 = sb("W2", [P, TURN, FB, D])
        b1 = sb("b1", [P, TURN, FB])
        b2 = sb("b2", [P, TURN, D])
        xr = sb("xr", [P, TURN, NT, D])
        W1s = sb("W1s", [P, TURN, 2, NB, FF], F16)
        W2s = sb("W2s", [P, TURN, 2, FB, D], F16)
        xT = sb("xT", [P, TURN, 2, NB, CT], F16)
        hid = sb("hid", [P, 2, CT])
        hids = sb("hids", [P, 2, FB, CT], F16)
        y = sb("y", [P, TURN, NT, D])
        ps_h = psum("ps_h", [P, 4, 512])
        ps_t = psum("ps_t", [P, 2, 512])
        ps_y = psum("ps_y", [P, 2, 512])

        diag = ctx.enter_context(nc.semaphore("ep_diag"))
        carrier = ctx.enter_context(nc.semaphore("ep_carrier"))
        w1_in = [ctx.enter_context(nc.semaphore(f"ep_w1_in{c}")) for c in range(TURN)]
        w2_in = [ctx.enter_context(nc.semaphore(f"ep_w2_in{c}")) for c in range(TURN)]
        x_in = [ctx.enter_context(nc.semaphore(f"ep_x_in{c}")) for c in range(TURN)]
        t_ready = made("t_ready", len(GROUPS))
        h_ready = made("h_ready", FB)
        y_ready = made("y_ready", NT)
        t_high = made("t_high", 2 * len(GROUPS))
        t_out = made("t_out", 2 * len(GROUPS))
        w1_high, w1_out, w2_high, w2_out = (made(x, 1) for x in ("w1_high", "w1_out", "w2_high", "w2_out"))
        h_gelu = made("h_gelu", FB)
        h_high = made("h_high", FB)
        h_out = made("h_out", FB)
        PASSES = ((0, 0), (0, 1), (1, 0))
        y_out = made("y_out", NT)
        y_stored = [ctx.enter_context(nc.semaphore(f"ep_y_stored{c}")) for c in range(TURN)]

        def credit(eng, *sems):
            for s in sems:
                eng.sem_inc(s.sem, s.ahead * s.per)

        with nc.Block() as block:
            @block.sync
            def _(sp):
                wait = lambda m, s, j=None: sp.wait_ge(m.sem, m.at(s, j))

                def load(c, e):
                    one = (lambda v: v[e:e + 1]) if isinstance(e, int) else (lambda v: v[bass.ds(e, 1)])
                    rows = one(exp_in[0:E * CT, :].rearrange("(e r) d -> e r d", e=E))
                    nc.sync.dma_start(xr[:, c, 0:4, :], rows[:, 0:4 * P, :].rearrange("e (i p) d -> p (e i) d", p=P)
                                      ).then_inc(x_in[c], 16)
                    nc.sync.dma_start(xr[0:64, c, 4, :], rows[:, 4 * P:CT, :].rearrange("e r d -> (e r) d")).then_inc(x_in[c], 16)
                    for dst, name, into in ((W1[:, c].rearrange("p k f -> p (k f)"), "W1", w1_in), (b1[:, c, :], "b1", w1_in),
                                            (W2[:, c].rearrange("p k f -> p (k f)"), "W2", w2_in), (b2[:, c, :], "b2", w2_in)):
                        nc.sync.dma_start(dst, one(t[name]).rearrange("e p n -> p (e n)")).then_inc(into[c], 16)

                def store(c, s, e):
                    wait(y_out, s)
                    rows = exp_out[:, :].rearrange("(e r) d -> e r d", e=E)
                    rows = rows[e:e + 1] if isinstance(e, int) else rows[bass.ds(e, 1)]
                    nc.sync.dma_start(rows[:, 0:4 * P, :].rearrange("e (i p) d -> p (e i) d", p=P), y[:, c, 0:4, :]
                                      ).then_inc(y_stored[c], 16)
                    nc.sync.dma_start(rows[:, 4 * P:CT, :].rearrange("e r d -> (e r) d"), y[0:64, c, 4, :]
                                      ).then_inc(y_stored[c], 16)

                for c in range(TURN):
                    sp.sem_inc(y_stored[c], 32)
                    load(c, c)
                with nc.sync.Fori(0, E // TURN - 1) as n:
                    for c in range(TURN):
                        store(c, (n, c), n * TURN + c)
                        load(c, n * TURN + (TURN + c))
                for c in range(TURN):
                    store(c, (E // TURN - 1, c), E - TURN + c)
                for c in range(TURN):
                    sp.wait_ge(y_stored[c], 32 + 32 * E // TURN)

            @block.gpsimd
            def _(pool):
                nc.gpsimd.memset(ident[:], 0.0).then_inc(diag, 1)
                pool.wait_ge(diag, 1)
                nc.gpsimd.affine_select(out=ident[:], in_=ident[:], compare_op=ALU.not_equal, fill=1.0, base=0,
                                        pattern=[[-1, P]], channel_multiplier=1).then_inc(diag, 1)

            def turns(eng, step):
                with eng.Fori(0, E // TURN - 1) as n:
                    for c in range(TURN):
                        step((n, c), (n, c + 1))
                for c in range(TURN):
                    step((E // TURN - 1, c), (E // TURN - 1, c + 1) if c < TURN - 1 else None)

            def loads(s):
                return s[0] * 32 + 32 * (1 + s[1] // TURN)

            @block.tensor
            def _(pe):
                wait = lambda m, s, j=None: pe.wait_ge(m.sem, m.at(s, j))
                credit(pe, t_ready, h_ready, y_ready)
                pe.wait_ge(diag, 2)

                def transposes(s):
                    c = s[1] % TURN
                    pe.wait_ge(x_in[c], loads(s))
                    for q, tiles in enumerate(GROUPS):
                        wait(t_out, s, 2 * q - 2) if q == 2 else wait(t_out, later(s, -1))
                        if TILES[tiles[0]][1] < P:
                            pe.sem_inc(carrier, 1)
                        width = sum(TILES[i][1] for i in tiles)
                        for i in tiles:
                            r = TILES[i][1]
                            at = TILES[i][0] - TILES[tiles[0]][0]
                            for b in range(NB):
                                a = nc.tensor.transpose(ps_t[:, q % 2, b * width + at:b * width + at + r],
                                                        xr[0:r, c, i, b * P:(b + 1) * P], ident[0:r, 0:r])
                        a.then_inc(t_ready.sem, 1)

                def step(s, nxt):
                    c = s[1]
                    wait(t_out, s)
                    wait(w1_out, s)
                    for m in range(FB):
                        wait(h_high, s, m - 1) if m >= 2 else wait(h_high, later(s, -1))
                        for h in range(2):
                            for k, (w, x) in enumerate(PASSES):
                                for b in range(NB):
                                    a = nc.tensor.matmul(ps_h[:, 2 * (m % 2) + h, 0:HALF], W1s[:, c, w, b, m * P:(m + 1) * P],
                                                         xT[:, c, x, b, h * HALF:(h + 1) * HALF],
                                                         start=(k == b == 0), stop=(k == 2 and b == NB - 1))
                        a.then_inc(h_ready.sem, 1)
                    if nxt:
                        transposes(nxt)
                    wait(w2_out, s)
                    wait(h_out, s)
                    for i, (first, r) in enumerate(TILES):
                        wait(y_out, s, i - 1) if i >= 2 else wait(y_out, later(s, -1))
                        for k, (x, w) in enumerate(PASSES):
                            for m in range(FB):
                                a = nc.tensor.matmul(ps_y[0:r, i % 2, 0:D], hids[:, x, m, first:first + r], W2s[:, c, w, m, :],
                                                     start=(k == m == 0), stop=(k == 2 and m == FB - 1))
                        a.then_inc(y_ready.sem, 1)

                transposes((0, 0))
                turns(nc.tensor, step)

            @block.scalar
            def _(act):
                wait = lambda m, s, j=None: act.wait_ge(m.sem, m.at(s, j))
                credit(act, t_high, w1_high, w2_high, h_gelu, h_high)

                def high_parts(s):
                    c = s[1] % TURN
                    wait(h_ready, later(s, -TURN))
                    for q, tiles in enumerate(GROUPS):
                        width = sum(TILES[i][1] for i in tiles)
                        first = TILES[tiles[0]][0]
                        wait(t_ready, s, q + 1)
                        for b in range(NB):
                            nc.scalar.activation(xT[:, c, 0, b, first:first + width], ps_t[:, q % 2, b * width:(b + 1) * width],
                                                 ACT.Copy).then_inc(t_high.sem, 1)
                    act.wait_ge(w1_in[c], loads(s))
                    nc.scalar.activation(W1s[:, c, 0], W1[:, c], ACT.Copy).then_inc(w1_high.sem, 1)
                    act.wait_ge(w2_in[c], loads(s))
                    wait(y_ready, later(s, -TURN))
                    nc.scalar.activation(W2s[:, c, 0], W2[:, c], ACT.Copy).then_inc(w2_high.sem, 1)

                def step(s, nxt):
                    for m in range(FB):
                        wait(h_ready, s, m + 1)
                        wait(h_out, s, m - 1) if m >= 2 else wait(h_out, later(s, -1))
                        nc.scalar.activation(hid[:, m % 2, :].rearrange("p (h n) -> p h n", h=2),
                                             ps_h[:, 2 * (m % 2):2 * (m % 2) + 2, 0:HALF], ACT.Gelu,
                                             bias=b1[:, s[1], m:m + 1]).then_inc(h_gelu.sem, 1)
                        wait(h_gelu, s, m + 1)
                        if m == 0:
                            wait(y_ready, later(s, -1))
                        nc.scalar.activation(hids[:, 0, m, :], hid[:, m % 2, :], ACT.Copy).then_inc(h_high.sem, 1)
                    if nxt:
                        high_parts(nxt)

                high_parts((0, 0))
                turns(nc.scalar, step)

            @block.vector
            def _(dve):
                wait = lambda m, s, j=None: dve.wait_ge(m.sem, m.at(s, j))
                credit(dve, t_out, w1_out, w2_out, h_out, y_out)

                def low_rows(s):
                    c = s[1] % TURN
                    for q, tiles in enumerate(GROUPS):
                        width = sum(TILES[i][1] for i in tiles)
                        first = TILES[tiles[0]][0]
                        wait(t_high, s, 2 * q + 2)
                        for b in range(NB):
                            of = slice(first, first + width)
                            nc.vector.tensor_tensor(xT[:, c, 1, b, of], ps_t[:, q % 2, b * width:(b + 1) * width],
                                                    xT[:, c, 0, b, of], ALU.subtract).then_inc(t_out.sem, 1)

                def low_weights(s, W, Ws, high, out_):
                    c = s[1] % TURN
                    wait(high, s)
                    nc.vector.tensor_tensor(Ws[:, c, 1], W[:, c], Ws[:, c, 0], ALU.subtract).then_inc(out_.sem, 1)

                def result(s, i):
                    c, r = s[1], TILES[i][1]
                    wait(y_ready, s, i + 1)
                    nc.vector.tensor_tensor(y[0:r, c, i, :], ps_y[0:r, i % 2, 0:D], b2[0:r, c, :], ALU.add).then_inc(y_out.sem, 1)

                def step(s, nxt):
                    for m in range(FB):
                        wait(h_high, s, m + 1)
                        nc.vector.tensor_tensor(hids[:, 1, m, :], hid[:, m % 2, :], hids[:, 0, m, :], ALU.subtract
                                                ).then_inc(h_out.sem, 1)
                    if nxt:
                        low_rows(nxt)
                    dve.wait_ge(y_stored[s[1]], s[0] * 32 + 32)
                    result(s, 0)
                    if nxt:
                        low_weights(nxt, W1, W1s, w1_high, w1_out)
                    result(s, 1)
                    result(s, 2)
                    if nxt:
                        low_weights(nxt, W2, W2s, w2_high, w2_out)
                    result(s, 3)
                    result(s, 4)

                low_rows((0, 0))
                low_weights((0, 0), W1, W1s, w1_high, w1_out)
                low_weights((0, 0), W2, W2s, w2_high, w2_out)
                turns(nc.vector, step)


def expert_arrays(a):
    import numpy as np

    F = "L0_ffn_"
    E, TT = 8, CHUNKS * NT
    valid = np.array([[p < TILES[i % NT][1] for i in range(TT)] for p in range(P)])
    carry = np.ones((P, E, TT), np.float32)
    carry[:, :, 0] = 0
    return {
        "iota8": np.broadcast_to(np.arange(E, dtype=np.float32), (P, E)),
        "absent": np.broadcast_to(np.where(valid, 0, 99).astype(np.float32)[:, :, None], (P, TT, 2)),
        "carry": carry,
        "spare": (2 * N + np.arange(2)[None, :, None] * TT * P + np.arange(TT)[None, None, :] * P
                  + np.arange(P)[:, None, None]).astype(np.float32),
        "upto": np.triu(np.ones((P, P))).astype(mybir.dt.np(BF16)),
        "onesb": np.ones((P, P)).astype(mybir.dt.np(BF16)),
        "W1": a[F + "W1"].reshape(E, NB, P, FF).transpose(0, 2, 1, 3).reshape(E, P, -1),
        "W2": a[F + "W2"].reshape(E, FB, P, D).transpose(0, 2, 1, 3).reshape(E, P, -1),
        "b1": a[F + "b1"].reshape(E, FB, P).transpose(0, 2, 1),
        "b2": np.broadcast_to(a[F + "b2"][:, None, :], (E, P, D)),
    }




def kernel(**inputs):
    import numpy as np
    import concourse.bacc as bacc
    from concourse.bass_utils import run_bass_kernel_spmd

    a = {k: np.asarray(v) for k, v in inputs.items()}

    def blocks(v):
        v = v.reshape(*v.shape[:-1], v.shape[-1] // P, P)
        return np.moveaxis(v, -1, 0)

    def rows_first(w):
        L, k, m = w.shape
        return w.reshape(L, k // P, P, m).transpose(0, 2, 1, 3).reshape(L, P, -1)

    x = a["x"].reshape(IMAGES, 3, 6, 16, 6, 16).transpose(0, 2, 4, 3, 5, 1).reshape(CHUNKS, CT, PATCH)
    tr = lambda w: w.transpose(0, 2, 1)
    A = "L0_attn_"
    laid = {
        "patches": x,
        "patchesT": x.reshape(CHUNKS, CT, KP, P).transpose(0, 3, 2, 1),
        "W_mlp": a["L0_tok_W_mlp"].reshape(KP, P, D).transpose(1, 0, 2),
        "g1b1": np.stack([blocks(a["L0_tok_g1"]), blocks(a["L0_tok_b1"])], axis=1),
        "rows": np.broadcast_to(np.stack([a["L0_tok_b_mlp"], a["L0_tok_g2"], a["L0_tok_b2"], a[A + "ln0_w"],
                                          a[A + "ln0_b"]]), (P, 5, D)),
        "rwkv_vec": np.stack([blocks(a[A + n]) for n in ("ln1_w", "ln1_b", "tmk", "tmv", "tmr", "time_decay",
                                                         "time_first", "ln2_w", "ln2_b", "cmk", "cmr")], axis=2),
        "Wkvr": np.stack([rows_first(tr(a[A + n])) for n in ("Wk", "Wv", "Wr")], axis=2).reshape(LAYERS, P, -1),
        "Wo": rows_first(tr(a[A + "Wo"])),
        "Wck": rows_first(tr(a[A + "Wck"])),
        "Wcr": rows_first(tr(a[A + "Wcr"])),
        "Wcv": rows_first(tr(a[A + "Wcv"])),
    }
    laid.update(ffn_arrays(a, blocks))
    laid.update(expert_arrays(a))
    nc = bacc.Bacc("TRN2", target_bir_lowering=False, num_devices=1)
    arrays, t = {}, {}
    for name, v in laid.items():
        v = np.ascontiguousarray(v)
        arrays["in_" + name] = v
        t[name] = nc.dram_tensor("in_" + name, v.shape, mybir.dt.from_np(v.dtype), kind="ExternalInput").ap()
    out = nc.dram_tensor("out", (N, D), F32, kind="ExternalOutput").ap()
    bass_vit_tower(nc, t, out)
    r = run_bass_kernel_spmd(nc, [arrays], core_ids=[0])
    return r.results[0]["out"].reshape(IMAGES, T, D)
```

```python
from contextlib import ExitStack

import concourse.bass as bass
from concourse import mybir

P = 128
D = 256
NB = D // P
IMAGES, T = 64, 36
N = IMAGES * T
CHUNKS = 4
CI = IMAGES // CHUNKS
CT = CI * T
HALF = CT // 2
TILES = [(0, 128), (128, 128), (256, 128), (384, 128), (512, 64)]
NT = len(TILES)
GROUPS = [(0, 1), (2, 3), (4,)]
LAYERS = 4
FF = 1024
FB = FF // P
PATCH = 768
KP = PATCH // P
TP = T + 1
CP = CI * TP
NEVER = -1e38

F32 = mybir.dt.float32
BF16 = mybir.dt.bfloat16
F16 = mybir.dt.float16
ALU = mybir.AluOpType
ACT = mybir.ActivationFunctionType
AX = mybir.AxisListType


class Made:

    def __init__(self, sem, per, steps=CHUNKS, ahead=1):
        self.sem, self.per, self.steps, self.ahead = sem, per, steps, ahead

    def at(self, step, j=None):
        layer, c = step
        j = self.per if j is None else j
        if isinstance(layer, int):
            return self.per * (self.steps * layer + c + self.ahead) + j
        return layer * (self.steps * self.per) + (self.per * (c + self.ahead) + j)


def later(step, k):
    return step[0], step[1] + k




def bass_vit_tower(nc, t, out):
    with ExitStack() as ctx:
        def sb(name, shape, dt=F32):
            return ctx.enter_context(nc.sbuf_tensor(name, shape, dt))

        X = sb("X", [P, CHUNKS * NT, D])
        H0 = sb("H0", [P, CHUNKS * NT, D])
        ident = sb("ident", [P, P])
        half_neg = sb("half_neg", [P, 8])
        exp_in = nc.dram_tensor("exp_in", (2 * N + 2 * CHUNKS * NT * P, D), F32, kind="Internal").ap()
        exp_out = nc.dram_tensor("exp_out", (2 * N, D), F32, kind="Internal").ap()
        used = tokenizer(nc, t, X, H0, ident, half_neg)
        rwkv(nc, t, X, H0, ident, half_neg, used)
        gate = sb("gate", [P, 2, CHUNKS * NT])
        src_i = sb("src_i", [P, 2, CHUNKS * NT], mybir.dt.uint32)
        H2 = sb("H2", [P, NT, D])
        dst_i = sb("dst_i", [P, 2, NT], mybir.dt.uint32)
        scattered = ctx.enter_context(nc.semaphore("scattered"))

        def scatter(i):
            r = TILES[i][1]
            for k in range(2):
                nc.gpsimd.indirect_dma_start(out=exp_in, out_offset=bass.IndirectOffsetOnAxis(ap=dst_i[0:r, k, i:i + 1], axis=0),
                                             in_=H2[0:r, i, :], in_offset=None).then_inc(scattered, 16)

        attention(nc, t, X, H0, H2, gate, src_i, dst_i, scatter, scattered, exp_in, ident, half_neg)
        experts(nc, t, X, H0, gate, src_i, scatter, scattered, exp_in, exp_out, out, half_neg)


def tokenizer(nc, t, X, H0, ident, half_neg):
    EPS_TOK, EPS_0 = -1e-05, 1e-05
    with ExitStack() as ctx:
        def sb(name, shape, dt=F32):
            return ctx.enter_context(nc.sbuf_tensor("tok_" + name, shape, dt))

        used = []

        def sem(name):
            used.append(ctx.enter_context(nc.semaphore("tok_" + name)))
            return used[-1]

        W = sb("W", [P, KP, D])
        ones = sb("ones", [P, P])
        b1c = sb("b1c", [P, KP, P])
        g1b1 = sb("g1b1", [P, 2, KP])
        rows = sb("rows", [P, 5, D])
        bias = sb("bias", [P, D])
        pT = [sb(f"pT{i}", [P, KP, CT]) for i in range(2)]
        pR = [sb(f"pR{i}", [P, NT, PATCH]) for i in range(2)]
        st0 = sb("st0", [P, NT, 2, 6])
        st = sb("st", [P, NT, 1, 6])
        mv = sb("mv", [P, 3, NT, 2])
        vr = sb("vr", [P, 3, NT])
        rs = sb("rs", [P, 3, NT])
        Y = sb("Y", [P, NT, D])
        Z = sb("Z", [P, NT, D])
        Z0 = sb("Z0", [P, NT, D])
        Z1 = sb("Z1", [P, NT, D])
        psY = ctx.enter_context(nc.psum_tensor("tok_psY", [P, NT, 512], F32))
        psC = ctx.enter_context(nc.psum_tensor("tok_psC", [P, 2, 512], F32))

        w_in = sem("w_in")
        p_in = [sem("p_in0"), sem("p_in1")]
        const = sem("const")
        carrier = sem("carrier")
        diag0 = sem("diag0")
        w_scaled = sem("w_scaled")
        col_mean = sem("col_mean")
        w_ready = sem("w_ready")
        y_ready = sem("y_ready")
        patch_mv = sem("patch_mv")
        d = sem("d")
        patch_st = sem("patch_st")
        rstd = [sem(f"rstd{k}") for k in range(3)]
        var_eps = [sem(f"var_eps{k}") for k in range(3)]
        y_made = sem("y_made")
        y_mv = sem("y_mv")
        z_made = sem("z_made")
        h0_scaled = sem("h0_scaled")
        h0_made = sem("h0_made")
        h0_mv = sem("h0_mv")
        z0_made = sem("z0_made")
        x_scaled = sem("x_scaled")
        x_made = sem("x_made")
        pair = 2

        def tile(n, c, i):
            at = (c * NT + i) + n * (pair * NT)
            return slice(at, at + 1) if isinstance(n, int) else bass.ds(n * (pair * NT) + (c * NT + i), 1)

        def chunks(eng, chunk):
            with eng.Fori(0, CHUNKS // pair - 1) as n:
                for c in range(pair):
                    chunk(n, c, False)
            for c in range(pair):
                chunk(CHUNKS // pair - 1, c, c == pair - 1)


        with nc.Block() as block:
            @block.sync
            def _(sp):
                nc.sync.dma_start(W[:], t["W_mlp"]).then_inc(w_in, 16)
                nc.sync.dma_start(g1b1[:], t["g1b1"]).then_inc(w_in, 16)
                nc.sync.dma_start(rows[:], t["rows"]).then_inc(w_in, 16)
                with nc.sync.Fori(0, CHUNKS // pair) as n:
                    for c in range(pair):
                        sp.wait_ge(y_ready, n * (pair * NT) + 1)
                        sp.sem_inc(carrier, 1)
                        sp.wait_ge(patch_mv, n * pair + 1)
                        nc.sync.dma_start(pT[c][:], t["patchesT"][bass.ds(n * pair + c, 1)]
                                          .rearrange("a p k n -> p (a k) n")).then_inc(p_in[c], 16)
                        src = t["patches"][bass.ds(n * pair + c, 1)].rearrange("a n f -> (a n) f")
                        nc.sync.dma_start(pR[c][:, 0:4, :], src[0:512, :].rearrange("(i p) f -> p i f", p=P)
                                          ).then_inc(p_in[c], 16)
                        nc.sync.dma_start(pR[c][0:64, 4, :], src[512:576, :]).then_inc(p_in[c], 16)

            @block.gpsimd
            def _(pool):
                pool.sem_inc(x_made, 1)
                nc.gpsimd.memset(ones[:], 1.0).then_inc(const, 1)
                nc.gpsimd.memset(half_neg[:], -0.5).then_inc(const, 1)
                nc.gpsimd.memset(ident[:], 0.0).then_inc(diag0, 1)
                nc.gpsimd.memset(mv[:], 1.0).then_inc(const, 1)
                pool.wait_ge(diag0, 1)
                nc.gpsimd.affine_select(out=ident[:], in_=ident[:], compare_op=ALU.not_equal, fill=1.0, base=0,
                                        pattern=[[-1, P]], channel_multiplier=1).then_inc(const, 1)
                pool.wait_ge(const, 4)

                def inverse_root(n, c, k, ready, eps):
                    count = n * pair + (c + 1)
                    pool.wait_ge(ready, count + (ready is patch_mv))
                    pool.sem_inc(carrier, 1)
                    nc.gpsimd.tensor_scalar(vr[:, k, :], mv[:, k, :, 1], 1.0, eps, ALU.mult, ALU.add).then_inc(var_eps[k], 1)
                    pool.wait_ge(var_eps[k], count)
                    nc.gpsimd.tensor_tensor(rs[:, k, :], vr[:, k, :], half_neg[:, 0:NT], ALU.pow).then_inc(rstd[k], 1)

                def affine(n, c, made, src, mid, dst, scaled, done, row):
                    for i, (_, r) in enumerate(TILES):
                        pool.wait_ge(made, n * (pair * NT) + (c * NT + i + 1))
                        nc.gpsimd.tensor_tensor(mid(i, r), src(i, r), rows[0:r, row, :], ALU.mult).then_inc(scaled, 1)
                    for i, (_, r) in enumerate(TILES):
                        pool.wait_ge(scaled, n * (pair * NT) + (c * NT + i + 1))
                        nc.gpsimd.tensor_tensor(dst(i, r), mid(i, r), rows[0:r, row + 1, :], ALU.add).then_inc(done, 1)

                pool.wait_ge(w_in, 48)

                def chunk(n, c, last):
                    inverse_root(n, c, 1, y_mv, EPS_TOK)
                    if not last:
                        affine(n, c, z_made, lambda i, r: Z[0:r, i:i + 1, :], lambda i, r: Z0[0:r, i:i + 1, :],
                               lambda i, r: H0[0:r, tile(n, c, i), :], h0_scaled, h0_made, 1)
                    if not last:
                        inverse_root(n, c + 1, 0, patch_mv, EPS_TOK)
                    inverse_root(n, c, 2, h0_mv, EPS_0)
                    if not last:
                        affine(n, c, z0_made, lambda i, r: Z1[0:r, i:i + 1, :], lambda i, r: Z1[0:r, i:i + 1, :],
                               lambda i, r: X[0:r, tile(n, c, i), :], x_scaled, x_made, 3)

                inverse_root(0, 0, 0, patch_mv, EPS_TOK)
                chunks(nc.gpsimd, chunk)

            @block.vector
            def _(dve):
                dve.sem_inc(patch_mv, 1)
                dve.sem_inc(y_made, 1)
                dve.wait_ge(w_in, 48)
                dve.wait_ge(const, 4)
                for k in range(KP):
                    nc.vector.tensor_scalar(b1c[:, k, :], ones[:], g1b1[:, 1, k:k + 1], None, ALU.mult).then_inc(d, 1)
                dve.wait_ge(col_mean, 1)
                nc.vector.tensor_tensor(bias[:], psC[:, 1, 0:D], rows[:, 0, :], ALU.add).then_inc(d, 1)
                for k in range(KP):
                    nc.vector.tensor_scalar(W[:, k, :], W[:, k, :], g1b1[:, 0, k:k + 1], None, ALU.mult).then_inc(w_scaled, 1)
                dve.wait_ge(col_mean, 2)
                nc.vector.tensor_scalar(Y[:, 0, :], psC[:, 0, 0:D], 1.0 / PATCH, None, ALU.mult).then_inc(d, 1)
                dve.wait_ge(d, KP + 2)
                for k in range(KP):
                    nc.vector.tensor_tensor(W[:, k, :], W[:, k, :], Y[:, 0, :], ALU.subtract).then_inc(w_ready, 1)

                def statistics(n, c, k, src, ready, done, base):
                    for i, (_, r) in enumerate(TILES):
                        dve.wait_ge(ready, n * (pair * NT) + (c * NT + i + 1 + (ready is y_made)))
                        a = nc.vector.bn_stats(st[0:r, i, 0, :], src(i, r))
                    a.then_inc(d, 1)
                    dve.wait_ge(d, base)
                    dve.sem_inc(carrier, 1)
                    for i, (_, r) in enumerate(TILES):
                        a = nc.vector.bn_aggr(mv[0:r, k, i, :], st[0:r, i, 0, :])
                    a.then_inc(done, 1)

                def last_affine(made, src, mid, dst, scaled, done, row):
                    before = (CHUNKS - 1) * NT
                    for i, (_, r) in enumerate(TILES):
                        dve.wait_ge(made, before + i + 1)
                        nc.vector.tensor_tensor(mid[0:r, i, :], src[0:r, i, :], rows[0:r, row, :], ALU.mult).then_inc(scaled, 1)
                    for i, (_, r) in enumerate(TILES):
                        dve.wait_ge(scaled, before + i + 1)
                        nc.vector.tensor_tensor(dst[0:r, before + i, :], mid[0:r, i, :], rows[0:r, row + 1, :], ALU.add
                                                ).then_inc(done, 1)

                first = KP + 2
                per = 2
                at = lambda n, c, j: n * (pair * per) + (first + c * per + j)

                def patch_statistics(n, c):
                    half = c % pair
                    dve.wait_ge(p_in[half], n * 48 + 48 * (1 + c // pair))
                    for i, (_, r) in enumerate(TILES):
                        for h in range(2):
                            a = nc.vector.bn_stats(st0[0:r, i, h, :], pR[half][0:r, i, h * (PATCH // 2):(h + 1) * (PATCH // 2)])
                    a.then_inc(patch_st, 1)
                    dve.wait_ge(patch_st, n * pair + (c + 1))
                    dve.sem_inc(carrier, 1)
                    for i, (_, r) in enumerate(TILES):
                        a = nc.vector.bn_aggr(mv[0:r, 0, i, :], st0[0:r, i, :, :])
                    a.then_inc(patch_mv, 1)

                def chunk(n, c, last):
                    dve.wait_ge(rstd[0], n * pair + (c + 1))
                    for i, (_, r) in enumerate(TILES):
                        dve.wait_ge(y_ready, n * (pair * NT) + (c * NT + i + 2))
                        nc.vector.scalar_tensor_tensor(out=Y[0:r, i, :], in0=psY[0:r, i, 0:D], scalar=rs[0:r, 0, i:i + 1],
                                                       in1=bias[0:r, :], op0=ALU.mult, op1=ALU.add).then_inc(y_made, 1)
                    statistics(n, c, 1, lambda i, r: Y[0:r, i, :], y_made, y_mv, at(n, c, 1))
                    dve.wait_ge(rstd[1], n * pair + (c + 1))
                    dve.wait_ge(y_mv, n * pair + (c + 1))
                    for i, (_, r) in enumerate(TILES):
                        nc.vector.tensor_scalar(Z[0:r, i, :], Y[0:r, i, :], mv[0:r, 1, i, 0:1], rs[0:r, 1, i:i + 1],
                                                ALU.subtract, ALU.mult).then_inc(z_made, 1)
                    if last:
                        last_affine(z_made, Z, Z0, H0, h0_scaled, h0_made, 1)
                    else:
                        patch_statistics(n, c + 1)
                    statistics(n, c, 2, lambda i, r: H0[0:r, tile(n, c, i), :], h0_made, h0_mv, at(n, c, 2))
                    dve.wait_ge(rstd[2], n * pair + (c + 1))
                    dve.wait_ge(h0_mv, n * pair + (c + 1))
                    dve.wait_ge(x_made, n * (pair * NT) + (c * NT + 1))
                    for i, (_, r) in enumerate(TILES):
                        nc.vector.tensor_scalar(Z1[0:r, i:i + 1, :], H0[0:r, tile(n, c, i), :], mv[0:r, 2, i, 0:1],
                                                rs[0:r, 2, i:i + 1], ALU.subtract, ALU.mult).then_inc(z0_made, 1)
                    if last:
                        last_affine(z0_made, Z1, Z1, X, x_scaled, x_made, 3)

                patch_statistics(0, 0)
                chunks(nc.vector, chunk)

            @block.tensor
            def _(pe):
                pe.sem_inc(y_ready, 1)
                pe.wait_ge(w_in, 48)
                pe.wait_ge(d, KP)
                for k in range(KP):
                    a = nc.tensor.matmul(psC[:, 1, 0:D], b1c[:, k, :], W[:, k, :], start=(k == 0), stop=(k == KP - 1))
                a.then_inc(col_mean, 1)
                pe.wait_ge(w_scaled, KP)
                for k in range(KP):
                    a = nc.tensor.matmul(psC[:, 0, 0:D], ones[:], W[:, k, :], start=(k == 0), stop=(k == KP - 1))
                a.then_inc(col_mean, 1)
                pe.wait_ge(w_ready, KP)
                with nc.tensor.Fori(0, CHUNKS // pair) as n:
                    for c in range(pair):
                        pe.wait_ge(p_in[c], n * 48 + 48)
                        for i, (first, r) in enumerate(TILES):
                            pe.wait_ge(y_made, n * (pair * NT) + (c * NT + 1))
                            for k in range(KP):
                                a = nc.tensor.matmul(psY[0:r, i, 0:D], pT[c][:, k, first:first + r], W[:, k, :],
                                                     start=(k == 0), stop=(k == KP - 1))
                            a.then_inc(y_ready, 1)
    return used


def rwkv(nc, t, X, H0, ident, half_neg, used):
    EPS = 1e-05
    PIECES = 4
    PIECE = NB * FF // PIECES
    PASSES = ((0, 0), (0, 1), (1, 0))
    with ExitStack() as ctx:
        def sb(name, shape, dt=F32):
            return ctx.enter_context(nc.sbuf_tensor("rw_" + name, shape, dt))

        def psum(name, shape):
            return ctx.enter_context(nc.psum_tensor("rw_" + name, shape, F32))

        def sem(name):
            return ctx.enter_context(nc.semaphore("rw_" + name))

        def made(name, per, ahead=1):
            return Made(sem(name), per, ahead=ahead)

        NPK = 11
        LN1W, LN1B, TMK, TMV, TMR, DECAY, FIRST, LN2W, LN2B, CMK, CMR = range(NPK)
        pk = sb("pk", [P, LAYERS, NPK, NB])
        pkv_a = sb("pkv_a", [P, 1, 5, NB])
        pkv_b = sb("pkv_b", [P, 1, 2, NB])
        pks_1 = sb("pks_1", [P, 1, 2, NB])
        pks_2 = sb("pks_2", [P, 1, 2, NB])
        Wa = sb("Wa", [P, 3, NB, D])
        Wo = sb("Wo", [P, NB, D])
        Wck = sb("Wck", [P, 2, PIECE])
        Wcks = sb("Wcks", [P, 2, NB * FF], F16)
        Wcr = sb("Wcr", [P, NB, D])
        Wcv = sb("Wcv", [P, FB, D])
        bs1 = sb("bs1", [P, NT, 6])
        bs2 = sb("bs2", [P, NT, 6])
        mv1 = sb("mv1", [P, NT, 2])
        mv2 = sb("mv2", [P, NT, 2])
        vr = sb("vr", [P, 2, NT])
        rs1 = sb("rs1", [P, NT])
        rs2 = sb("rs2", [P, NT])
        xn1 = sb("xn1", [P, NT, D])
        xn2 = sb("xn2", [P, NT, D])
        h1 = sb("h1", [P, NB, CT])
        h2 = sb("h2", [P, NB, CT])
        dh = sb("dh", [P, NB, CT])
        xa = sb("xa", [P, 3, NB, CT])
        xk = sb("xk", [P, 2, NB, CT], F16)
        xr = sb("xr", [P, NB, CT])
        K = sb("K", [P, NB, CP])
        V = sb("V", [P, NB, CP])
        R = sb("R", [P, NB, CP])
        reset = sb("reset", [P, CP])
        wd = sb("wd", [P, NB, CP])
        PP = sb("PP", [P, NB, CP])
        E = sb("E", [P, 3, NB, CP])
        EV = sb("EV", [P, NB, CP])
        AA = sb("AA", [P, NB, CP])
        BB = sb("BB", [P, NB, CP])
        ys = sb("ys", [P, NB, CT])
        relu = sb("relu", [P, 2, CT])
        kf = sb("kf", [P, FB, CT])
        tr = sb("tr", [P, NT, D])
        kv = sb("kv", [P, NT, D])
        ps_mat = psum("ps_mat", [P, 4, 512])
        ps_t = psum("ps_t", [P, 2, 512])
        ps_tok = psum("ps_tok", [P, 2, 512])

        pk_in = sem("pk_in")
        carrier = sem("carrier")
        pk_made = sem("pk_made")
        zeroed = sem("zeroed")
        wa_in = sem("wa_in")
        wo_in = sem("wo_in")
        wck_in = [sem(f"wck_in{half}") for half in range(2)]
        wck_high = sem("wck_high")
        wck_low = sem("wck_low")
        wcr_in = sem("wcr_in")
        wcv_in = sem("wcv_in")
        pka_copied = sem("pka_copied")
        pkb_copied = sem("pkb_copied")
        pk1_copied = sem("pk1_copied")
        pk2_copied = sem("pk2_copied")

        t1_ready = made("t1_ready", len(GROUPS))
        t2_ready = made("t2_ready", len(GROUPS))
        a_ready = made("a_ready", 6)
        wo_ready = made("wo_ready", NT)
        ck_ready = made("ck_ready", FB)
        cr_ready = made("cr_ready", NT)
        cv_ready = made("cv_ready", NT)
        t1_out = made("t1_out", 2 * len(GROUPS))
        t2_out = made("t2_out", 2 * len(GROUPS))
        a_out = made("a_out", 6)
        e_out = made("e_out", 6)
        ck_relu = made("ck_relu", FB)
        ck_sq = [made(f"ck_sq{odd}", FB // 2) for odd in range(2)]
        xk_high = made("xk_high", NB)
        xk_low = made("xk_low", NB)
        cr_out = made("cr_out", NT)
        cv_out = made("cv_out", NT)
        res1 = made("res1", NT)
        st1 = made("st1", 1)
        st2 = made("st2", 1)
        mv1_made = made("mv1_made", 1)
        mv2_made = made("mv2_made", 1)
        xn1_made = made("xn1_made", NT)
        xn2_made = made("xn2_made", NT)
        dh1 = made("dh1", 2)
        dh2 = made("dh2", 2)
        mixa = made("mixa", 6)
        mixb = made("mixb", 4)
        pp_made = made("pp_made", 2)
        ex_made = made("ex_made", 6)
        ev_made = made("ev_made", 2)
        bb_made = made("bb_made", 2)
        aa_made = made("aa_made", 2)
        n1_made = made("n1_made", 1)
        n2_made = made("n2_made", 1)
        nu_made = made("nu_made", 1)
        c1_made = made("c1_made", 1)
        den_made = made("den_made", 1)
        inv_made = made("inv_made", 1)
        yr_made = made("yr_made", 1)
        ys_made = made("ys_made", 1)
        sigmoid = made("sigmoid", len(GROUPS))
        gated = made("gated", len(GROUPS))
        res2 = made("res2", len(GROUPS), 2)
        ve1 = made("ve1", 1)
        ve2 = made("ve2", 1)
        rs1_made = made("rs1_made", 1)
        rs2_made = made("rs2_made", 1)

        def credit(eng, *sems):
            for s in sems:
                eng.sem_inc(s.sem, s.ahead * s.per)

        def has(step, k):
            return not isinstance(step[0], int) or CHUNKS * step[0] + step[1] + k < CHUNKS * LAYERS

        def tok(buf, b):
            return buf[:, b, :].rearrange("p (n t) -> p n t", t=TP)[:, :, 1:TP]

        def before(buf, b):
            return buf[:, b, :].rearrange("p (n t) -> p n t", t=TP)[:, :, 0:T]

        def tok2(buf):
            return buf[:, :, :].rearrange("p b (n t) -> p (b n) t", t=TP)[:, :, 1:TP]

        def before2(buf):
            return buf[:, :, :].rearrange("p b (n t) -> p (b n) t", t=TP)[:, :, 0:T]

        with nc.Block() as block:
            @block.sync
            def _(sp):
                nc.sync.dma_start(pk[:], t["rwkv_vec"]).then_inc(pk_in, 16)

                def load(dst, name, layer, sem_in):
                    src = t[name][layer:layer + 1] if isinstance(layer, int) else t[name][bass.ds(layer, 1)]
                    nc.sync.dma_start(dst, src.rearrange("l p n -> p (l n)")).then_inc(sem_in, 16)

                def flat(w):
                    return w.rearrange("p a n -> p (a n)")

                load(Wa.rearrange("p s b n -> p (s b n)"), "Wkvr", 0, wa_in)
                load(flat(Wo), "Wo", 0, wo_in)

                def load_piece(layer, q):
                    half = q % 2
                    if not isinstance(layer, int) or PIECES * layer + q >= 2:
                        sp.wait_ge(wck_low, layer * PIECES + (q - 1))
                        sp.sem_inc(carrier, 1)
                    src = t["Wck"][layer:layer + 1] if isinstance(layer, int) else t["Wck"][bass.ds(layer, 1)]
                    nc.sync.dma_start(Wck[:, half], src[:, :, q * PIECE:(q + 1) * PIECE].rearrange("l p n -> p (l n)")
                                      ).then_inc(wck_in[half], 16)

                for q in range(2):
                    load_piece(0, q)
                load(flat(Wcr), "Wcr", 0, wcr_in)
                load(flat(Wcv), "Wcv", 0, wcv_in)
                for x in used:
                    sp.sem_clear(x)
                with nc.sync.Fori(0, LAYERS - 1) as l:
                    for q in range(2, PIECES):
                        load_piece(l, q)
                    for q in range(2):
                        load_piece(l + 1, q)
                    sp.wait_ge(a_ready.sem, a_ready.at((l, 3)))
                    sp.sem_inc(carrier, 1)
                    load(Wa.rearrange("p s b n -> p (s b n)"), "Wkvr", l + 1, wa_in)
                    sp.wait_ge(wo_ready.sem, wo_ready.at((l, 3)))
                    load(flat(Wo), "Wo", l + 1, wo_in)
                    sp.wait_ge(cr_ready.sem, cr_ready.at((l, 3)))
                    load(flat(Wcr), "Wcr", l + 1, wcr_in)
                    sp.wait_ge(cv_ready.sem, cv_ready.at((l, 3)))
                    load(flat(Wcv), "Wcv", l + 1, wcv_in)
                for q in range(2, PIECES):
                    load_piece(LAYERS - 1, q)

            @block.gpsimd
            def _(pool):
                resets = lambda buf: buf.rearrange("p b (n t) -> p (b n) t", t=TP)[:, :, 0:1]
                nc.gpsimd.memset(resets(K[:]), NEVER).then_inc(zeroed, 1)
                nc.gpsimd.memset(resets(EV[:]), 0.0).then_inc(zeroed, 1)
                for e in range(2):
                    nc.gpsimd.memset(resets(E[:, e]), 0.0).then_inc(zeroed, 1)
                nc.gpsimd.memset(reset[:], 0.0).then_inc(zeroed, 1)
                nc.gpsimd.memset(mv1[:], 1.0).then_inc(zeroed, 1)
                nc.gpsimd.memset(mv2[:], 1.0).then_inc(zeroed, 1)
                pool.wait_ge(zeroed, 7)
                nc.gpsimd.memset(reset[:].rearrange("p (n t) -> p n t", t=TP)[:, :, 0:1], 2 * NEVER).then_inc(zeroed, 1)
                credit(pool, ve1, ve2, rs1_made, rs2_made, ck_sq[1], sigmoid, gated, res2)

                def root(mv, vr_, rs_, stats, ve, done, step):
                    pool.wait_ge(stats.sem, stats.at(step))
                    pool.sem_inc(carrier, 1)
                    nc.gpsimd.tensor_scalar(vr_, mv[:, :, 1], 1.0, EPS, ALU.mult, ALU.add).then_inc(ve.sem, 1)
                    pool.wait_ge(ve.sem, ve.at(step))
                    nc.gpsimd.tensor_tensor(rs_, vr_, half_neg[:, 0:NT], ALU.pow).then_inc(done.sem, 1)

                norm1 = lambda s: root(mv1, vr[:, 0, :], rs1[:], mv1_made, ve1, rs1_made, s)
                norm2 = lambda s: root(mv2, vr[:, 1, :], rs2[:], mv2_made, ve2, rs2_made, s)

                def step(s):
                    low_pieces(s, range(2))
                    norm2(s)
                    if has(s, 2):
                        norm1(later(s, 2))
                    low_pieces(s, range(2, PIECES))
                    squares(s)
                    if not has(s, 1):
                        norm1(later(s, 1))
                    residual2(s)

                def squares(s):
                    pool.wait_ge(cv_ready.sem, cv_ready.at(later(s, -1)))
                    for m in range(1, FB, 2):
                        pool.wait_ge(ck_relu.sem, ck_relu.at(s, m + 1))
                        nc.gpsimd.tensor_tensor(kf[:, m, :], relu[:, 1, :], relu[:, 1, :], ALU.mult).then_inc(ck_sq[1].sem, 1)

                def low_pieces(s, qs):
                    if s[1] == 0:
                        for q in qs:
                            pool.wait_ge(wck_high, s[0] * PIECES + (q + 1))
                            of = slice(q * PIECE, (q + 1) * PIECE)
                            nc.gpsimd.tensor_tensor(Wcks[:, 1, of], Wck[:, q % 2], Wcks[:, 0, of], ALU.subtract
                                                    ).then_inc(wck_low, 1)

                def residual2(s):
                    for q, tiles in enumerate(GROUPS):
                        r = TILES[tiles[0]][1]
                        of = slice(tiles[0], tiles[-1] + 1)
                        pool.wait_ge(cr_out.sem, cr_out.at(s, tiles[-1] + 1))
                        pool.sem_inc(carrier, 1)
                        nc.gpsimd.tensor_scalar(tr[0:r, of, :], tr[0:r, of, :], 0.5, 0.5, ALU.mult, ALU.add
                                                ).then_inc(sigmoid.sem, 1)
                    for q, tiles in enumerate(GROUPS):
                        r = TILES[tiles[0]][1]
                        of = slice(tiles[0], tiles[-1] + 1)
                        x = X[0:r, NT * s[1] + tiles[0]:NT * s[1] + tiles[-1] + 1, :]
                        pool.wait_ge(sigmoid.sem, sigmoid.at(s, q + 1))
                        pool.wait_ge(cv_out.sem, cv_out.at(s, tiles[-1] + 1))
                        nc.gpsimd.tensor_tensor(kv[0:r, of, :], tr[0:r, of, :], kv[0:r, of, :], ALU.mult).then_inc(gated.sem, 1)
                        pool.wait_ge(gated.sem, gated.at(s, q + 1))
                        nc.gpsimd.tensor_tensor(x, x, kv[0:r, of, :], ALU.add).then_inc(res2.sem, 1)

                for c in range(2):
                    norm1((0, c))
                with nc.gpsimd.Fori(0, LAYERS - 1) as l:
                    for c in range(CHUNKS):
                        step((l, c))
                for c in range(CHUNKS):
                    step((LAYERS - 1, c))

            @block.tensor
            def _(pe):
                credit(pe, t1_ready, t2_ready, a_ready, wo_ready, ck_ready, cr_ready, cv_ready)
                wait = lambda m, s, j=None: pe.wait_ge(m.sem, m.at(s, j))

                def transposes(xn, made_, ready, bank, free, s):
                    for q, tiles in enumerate(GROUPS):
                        wait(made_, s, tiles[-1] + 1)
                        free(q)
                        if TILES[tiles[0]][1] < P:
                            pe.sem_inc(carrier, 1)
                        dst = ps_t[:, bank(q), :]
                        width = sum(TILES[i][1] for i in tiles)
                        for i in tiles:
                            r = TILES[i][1]
                            at = TILES[i][0] - TILES[tiles[0]][0]
                            for b in range(NB):
                                a = nc.tensor.transpose(dst[:, b * width + at:b * width + at + r],
                                                        xn[0:r, i, b * P:(b + 1) * P], ident[0:r, 0:r])
                        a.then_inc(ready.sem, 1)

                def t1(s, first=False):
                    def free(q):
                        if first:
                            if s[1] == 1 or q == 2:
                                wait(t1_out, (0, s[1] - 1) if q < 2 else s, 6 if q < 2 else 2)
                        elif q < 2:
                            wait(t2_out, later(s, -2), 2 * q + 4)
                        else:
                            wait(t1_out, s, 2)
                    transposes(xn1, xn1_made, t1_ready, lambda q: (q + 1) % 2, free, s)

                def t2(s):
                    def free(q):
                        if q == 2:
                            wait(t2_out, s, 2)
                        elif has(s, 1):
                            wait(t1_out, later(s, 1), 2 * q + 4)
                        else:
                            wait(t2_out, later(s, -1), 6 - 2 * q)
                    transposes(xn2, xn2_made, t2_ready, lambda q: q % 2, free, s)

                def channel_major(dst_pair, w, x):
                    for h in range(2):
                        for b in range(NB):
                            a = nc.tensor.matmul(ps_mat[:, 2 * dst_pair + h, 0:HALF], w(b),
                                                 x(b)[:, h * HALF:(h + 1) * HALF], start=(b == 0), stop=(b == NB - 1))
                    return a

                def keys(s, js, after_ck):
                    for j in js:
                        stream, m = divmod(j, 2)
                        wait(mixa, s, 2 * stream + 2)
                        if j >= 2:
                            wait(a_out, s, j - 1)
                        elif after_ck is not None:
                            wait(ck_relu, after_ck, FB - 1 + j)
                        channel_major(j % 2, lambda b: Wa[:, stream, b, m * P:(m + 1) * P],
                                      lambda b: xa[:, stream, b, :]).then_inc(a_ready.sem, 1)

                def bank_of(s, kind, i):
                    return (3 * NT * s[1] + kind * NT + i) % 2

                def free_tok(s, kind, i):
                    users = (res1, cr_out, cv_out)
                    n = kind * NT + i - 2
                    if n < 0:
                        wait(cv_out, later(s, -1), n + NT + 1)
                    else:
                        wait(users[n // NT], s, n % NT + 1)

                def output(s):
                    wait(ys_made, s)
                    for i, (first, r) in enumerate(TILES):
                        free_tok(s, 0, i)
                        for b in range(NB):
                            a = nc.tensor.matmul(ps_tok[0:r, bank_of(s, 0, i), 0:D], ys[:, b, first:first + r], Wo[:, b, :],
                                                 start=(b == 0), stop=(b == NB - 1))
                        a.then_inc(wo_ready.sem, 1)

                def channel_keys(s):
                    wait(xk_high, s)
                    for m in range(FB):
                        if m >= 2:
                            wait(ck_relu, s, m - 1)
                        elif has(s, 1):
                            wait(a_out, later(s, 1), 5 + m)
                        else:
                            wait(ck_relu, later(s, -1), FB - 1 + m)
                        for h in range(2):
                            for k, (x, w) in enumerate(PASSES):
                                if m == h == 0 and k == 2:
                                    wait(xk_low, s)
                                for b in range(NB):
                                    a = nc.tensor.matmul(ps_mat[:, 2 * (m % 2) + h, 0:HALF],
                                                         Wcks[:, w, b * FF + m * P:b * FF + (m + 1) * P],
                                                         xk[:, x, b, h * HALF:(h + 1) * HALF],
                                                         start=(k == b == 0), stop=(k == 2 and b == NB - 1))
                        a.then_inc(ck_ready.sem, 1)

                def channel_gate(s):
                    wait(mixb, s, 4)
                    for i, (first, r) in enumerate(TILES):
                        free_tok(s, 1, i)
                        for b in range(NB):
                            a = nc.tensor.matmul(ps_tok[0:r, bank_of(s, 1, i), 0:D], xr[:, b, first:first + r],
                                                 Wcr[:, b, :], start=(b == 0), stop=(b == NB - 1))
                        a.then_inc(cr_ready.sem, 1)

                def channel_values(s):
                    for odd in range(2):
                        wait(ck_sq[odd], s)
                    for i, (first, r) in enumerate(TILES):
                        free_tok(s, 2, i)
                        for m in range(FB):
                            a = nc.tensor.matmul(ps_tok[0:r, bank_of(s, 2, i), 0:D], kf[:, m, first:first + r],
                                                 Wcv[:, m, :], start=(m == 0), stop=(m == FB - 1))
                        a.then_inc(cv_ready.sem, 1)

                def weights(sem_in, s):
                    if s[1] % CHUNKS == 0:
                        layer = s[0] + s[1] // CHUNKS
                        pe.wait_ge(sem_in, layer * 16 + 16)

                def step(s):
                    weights(wo_in, s)
                    output(s)
                    if has(s, 1):
                        weights(wa_in, later(s, 1))
                        keys(later(s, 1), range(4), later(s, -1))
                    t2(s)
                    if has(s, 1):
                        keys(later(s, 1), (4, 5), None)
                    if has(s, 2):
                        t1(later(s, 2))
                    if s[1] == 0:
                        pe.wait_ge(wck_low, s[0] * PIECES + PIECES)
                    channel_keys(s)
                    weights(wcr_in, s)
                    channel_gate(s)
                    weights(wcv_in, s)
                    channel_values(s)

                t1((0, 0), True)
                weights(wa_in, (0, 0))
                keys((0, 0), range(6), None)
                t1((0, 1), True)
                with nc.tensor.Fori(0, LAYERS - 1) as l:
                    for c in range(CHUNKS):
                        step((l, c))
                for c in range(CHUNKS):
                    step((LAYERS - 1, c))

            @block.scalar
            def _(act):
                credit(act, t1_out, t2_out, a_out, e_out, ck_relu, ck_sq[0], xk_high, cr_out, cv_out)
                wait = lambda m, s, j=None: act.wait_ge(m.sem, m.at(s, j))
                act.wait_ge(pk_in, 16)
                nc.scalar.activation(pk[:, :, DECAY, :], pk[:, :, DECAY, :], ACT.Exp).then_inc(pk_made, 1)

                def copy_pack(dst, layer, k, done):
                    src = pk[:, layer:layer + 1, k:k + 2, :] if isinstance(layer, int) else pk[:, bass.ds(layer, 1), k:k + 2, :]
                    nc.scalar.activation(dst[:], src, ACT.Copy).then_inc(done, 1)

                def evict(ready, h, par, par_copied, out_, bank, s, layer, between=lambda: None):
                    act.wait_ge(par_copied, layer + 1)
                    for q, tiles in enumerate(GROUPS):
                        width = sum(TILES[i][1] for i in tiles)
                        first = TILES[tiles[0]][0]
                        wait(ready, s, q + 1)
                        for b in range(NB):
                            nc.scalar.activation(h[:, b, first:first + width], ps_t[:, bank(q), b * width:(b + 1) * width],
                                                 ACT.Identity, bias=par[:, 0, 1, b:b + 1], scale=par[:, 0, 0, b:b + 1]
                                                 ).then_inc(out_.sem, 1)
                        if q == 0:
                            between()

                def t1(s, between=lambda: None):
                    if s[1] % CHUNKS == 0:
                        layer = s[0] + s[1] // CHUNKS
                        copy_pack(pks_1, layer, LN1W, pk1_copied)
                    wait(mixa, later(s, -1))
                    evict(t1_ready, h1, pks_1, pk1_copied, t1_out, lambda q: (q + 1) % 2, s, s[0] + s[1] // CHUNKS,
                          between)

                def t2(s):
                    if s[1] == 0:
                        copy_pack(pks_2, s[0], LN2W, pk2_copied)
                    wait(mixb, later(s, -1))
                    evict(t2_ready, h2, pks_2, pk2_copied, t2_out, lambda q: q % 2, s, s[0])

                def images(ap):
                    return ap.rearrange("p h (n t) -> p h n t", t=T)

                def keys(s, js):
                    wait(ys_made, later(s, -1))
                    for j in js:
                        stream, m = divmod(j, 2)
                        wait(a_ready, s, j + 1)
                        src = images(ps_mat[:, 2 * (j % 2):2 * (j % 2) + 2, 0:HALF])
                        dst = tok((K, V, R)[stream], m).rearrange("p (h n) t -> p h n t", h=2)
                        if stream < 2:
                            a = nc.scalar.activation(dst, src, ACT.Identity)
                        else:
                            a = nc.scalar.activation(dst, src, ACT.Tanh, scale=0.5)
                        a.then_inc(a_out.sem, 1)

                def exponentials(s, b):
                    for e in range(3):
                        wait(ex_made, s, 3 * b + e + 1)
                        x = tok(E[:, e], b)
                        if e < 2:
                            a = nc.scalar.activation(x, x, ACT.Exp)
                        else:
                            a = nc.scalar.activation(x, x, ACT.Tanh, scale=-0.5)
                        a.then_inc(e_out.sem, 1)

                def channel_keys(s, ms):
                    for m in ms:
                        wait(ck_ready, s, m + 1)
                        wait(ck_sq[m % 2], s, m // 2) if m >= 2 else wait(ck_sq[m], later(s, -1))
                        dst = relu[:, m % 2, :].rearrange("p (h n) -> p h n", h=2)
                        nc.scalar.activation(dst, ps_mat[:, 2 * (m % 2):2 * (m % 2) + 2, 0:HALF], ACT.Relu
                                             ).then_inc(ck_relu.sem, 1)
                        if m % 2 == 0:
                            wait(ck_relu, s, m + 1)
                            if m == 0:
                                wait(cv_ready, later(s, -1))
                            nc.scalar.activation(kf[:, m, :], relu[:, 0, :], ACT.Square).then_inc(ck_sq[0].sem, 1)

                def channel_gate(s):
                    wait(res2, later(s, -1))
                    for i, (_, r) in enumerate(TILES):
                        wait(cr_ready, s, i + 1)
                        nc.scalar.activation(tr[0:r, i, :], ps_tok[0:r, (3 * NT * s[1] + NT + i) % 2, 0:D], ACT.Tanh,
                                             scale=0.5).then_inc(cr_out.sem, 1)

                def channel_values(s):
                    for i, (_, r) in enumerate(TILES):
                        wait(cv_ready, s, i + 1)
                        nc.scalar.activation(kv[0:r, i, :], ps_tok[0:r, (3 * NT * s[1] + 2 * NT + i) % 2, 0:D], ACT.Copy
                                             ).then_inc(cv_out.sem, 1)

                def high_keys_input(s):
                    wait(ck_ready, later(s, -1))
                    for b in range(NB):
                        wait(mixb, s, b + 1)
                        nc.scalar.activation(xk[:, 0, b, :], relu[:, b, :], ACT.Copy).then_inc(xk_high.sem, 1)

                def high_pieces(s, qs):
                    if s[1] == 0:
                        wait(ck_ready, later(s, -1))
                        for q in qs:
                            act.wait_ge(wck_in[q % 2], (s[0] * (PIECES // 2) + (q // 2 + 1)) * 16)
                            nc.scalar.activation(Wcks[:, 0, q * PIECE:(q + 1) * PIECE], Wck[:, q % 2], ACT.Copy
                                                 ).then_inc(wck_high, 1)

                def step(s):
                    high_pieces(s, range(2))
                    if has(s, 1):
                        keys(later(s, 1), range(4))
                    high_pieces(s, range(2, PIECES))
                    t2(s)
                    if has(s, 1):
                        keys(later(s, 1), (4, 5))
                    if has(s, 2):
                        t1(later(s, 2), lambda: high_keys_input(s))
                    else:
                        high_keys_input(s)
                    channel_keys(s, (0, 1))
                    if has(s, 1):
                        exponentials(later(s, 1), 0)
                    channel_keys(s, (2, 3))
                    if has(s, 1):
                        exponentials(later(s, 1), 1)
                    channel_keys(s, (4, 5, 6, 7))
                    channel_gate(s)
                    channel_values(s)

                act.wait_ge(zeroed, 8)
                t1((0, 0))
                keys((0, 0), range(6))
                t1((0, 1))
                exponentials((0, 0), 0)
                exponentials((0, 0), 1)
                with nc.scalar.Fori(0, LAYERS - 1) as l:
                    for c in range(CHUNKS):
                        step((l, c))
                for c in range(CHUNKS):
                    step((LAYERS - 1, c))

            @block.vector
            def _(dve):
                credit(dve, res1, st1, st2, mv1_made, mv2_made, xn1_made, xn2_made, dh1, dh2, mixa, mixb, pp_made,
                       ex_made, ev_made, bb_made, aa_made, n1_made, n2_made, nu_made, c1_made, den_made, inv_made,
                       yr_made, ys_made, xk_low)
                wait = lambda m, s, j=None: dve.wait_ge(m.sem, m.at(s, j))
                dve.wait_ge(pk_made, 1)
                dve.wait_ge(zeroed, 8)
                nc.vector.tensor_scalar(pk[:, :, DECAY, :], pk[:, :, DECAY, :], -1.0, None, ALU.mult).then_inc(pk_made, 1)
                nc.vector.tensor_scalar(pk[:, :, TMK:TMR + 1, :], pk[:, :, TMK:TMR + 1, :], -1.0, None, ALU.add
                                        ).then_inc(pk_made, 1)
                nc.vector.tensor_scalar(pk[:, :, CMK:CMR + 1, :], pk[:, :, CMK:CMR + 1, :], -1.0, None, ALU.add
                                        ).then_inc(pk_made, 1)
                dve.wait_ge(pk_made, 4)

                def tile(s, i):
                    return s[1] % CHUNKS * NT + i

                def statistics(s, bs, st_, mv, mv_made, ready):
                    for i, (_, r) in enumerate(TILES):
                        ready(i)
                        a = nc.vector.bn_stats(bs[0:r, i, :], X[0:r, tile(s, i), :])
                    a.then_inc(st_.sem, 1)
                    wait(st_, s)
                    dve.sem_inc(carrier, 1)
                    for i, (_, r) in enumerate(TILES):
                        a = nc.vector.bn_aggr(mv[0:r, i, :], bs[0:r, i, :])
                    a.then_inc(mv_made.sem, 1)

                def normalise(s, mv, mv_made, rs, rs_made, xn, xn_made, free):
                    wait(free, later(s, -1))
                    wait(mv_made, s)
                    wait(rs_made, s)
                    for i, (_, r) in enumerate(TILES):
                        nc.vector.tensor_scalar(xn[0:r, i, :], X[0:r, tile(s, i), :], mv[0:r, i, 0:1], rs[0:r, i:i + 1],
                                                ALU.subtract, ALU.mult).then_inc(xn_made.sem, 1)

                def statistics1(s):
                    def ready(i):
                        if i == 0 and not (isinstance(s[0], int) and CHUNKS * s[0] + s[1] < CHUNKS):
                            wait(res2, later(s, -CHUNKS))
                    statistics(s, bs1, st1, mv1, mv1_made, ready)

                def next_stage(s):
                    wait(res2, later(s, -CHUNKS))
                    for i, (_, r) in enumerate(TILES):
                        nc.vector.tensor_tensor(X[0:r, i, :], X[0:r, i, :], H0[0:r, i, :], ALU.add).then_inc(res1.sem, 1)
                    statistics(s, bs1, st1, mv1, mv1_made, lambda i: wait(res1, s, i + 1))
                    wait(mv1_made, s)
                    wait(rs1_made, s)
                    for i, (_, r) in enumerate(TILES):
                        nc.vector.tensor_scalar(H0[0:r, i, :], X[0:r, i, :], mv1[0:r, i, 0:1], rs1[0:r, i:i + 1],
                                                ALU.subtract, ALU.mult).then_inc(xn1_made.sem, 1)

                def statistics2(s):
                    statistics(s, bs2, st2, mv2, mv2_made, lambda i: wait(res1, s, i + 1))

                norm1 = lambda s: normalise(s, mv1, mv1_made, rs1, rs1_made, xn1, xn1_made, t1_ready)
                norm2 = lambda s: normalise(s, mv2, mv2_made, rs2, rs2_made, xn2, xn2_made, t2_ready)

                def residual1(s):
                    for i, (_, r) in enumerate(TILES):
                        wait(wo_ready, s, i + 1)
                        x = X[0:r, tile(s, i), :]
                        nc.vector.scalar_tensor_tensor(out=x, in0=ps_tok[0:r, (3 * NT * s[1] + i) % 2, 0:D], scalar=0.5,
                                                       in1=x, op0=ALU.mult, op1=ALU.add).then_inc(res1.sem, 1)

                def differences(s, h, out_, done):
                    wait(out_, s)
                    nc.vector.tensor_tensor(dh[:, :, 1:CT], h[:, :, 1:CT], h[:, :, 0:CT - 1], ALU.subtract).then_inc(done.sem, 1)
                    wait(done, s, 1)
                    first = lambda x: x[:, :, :].rearrange("p b (n t) -> p (b n) t", t=T)[:, :, 0:1]
                    nc.vector.tensor_copy(first(dh), first(h)).then_inc(done.sem, 1)
                    wait(done, s, 2)

                def mix(h, pack, k, dst, b, done):
                    nc.vector.scalar_tensor_tensor(out=dst, in0=dh[:, b, :], scalar=pack[:, 0, k, b:b + 1], in1=h[:, b, :],
                                                   op0=ALU.mult, op1=ALU.add).then_inc(done.sem, 1)

                def one(buf, layer, a, z):
                    return buf[:, layer:layer + 1, a:z, :] if isinstance(layer, int) else buf[:, bass.ds(layer, 1), a:z, :]

                def mix_a(s):
                    if s[1] % CHUNKS == 0:
                        layer = s[0] + s[1] // CHUNKS
                        if s[1] == CHUNKS:
                            wait(ex_made, later(s, -1))
                        nc.vector.tensor_copy(pkv_a[:], one(pk, layer, TMK, FIRST + 1)).then_inc(pka_copied, 1)
                        dve.wait_ge(pka_copied, layer * 3 + 1)
                        for b in range(NB):
                            nc.vector.tensor_scalar(wd[:, b, :], reset[:], pkv_a[:, 0, 3, b:b + 1], None, ALU.add
                                                    ).then_inc(pka_copied, 1)
                    if not (isinstance(s[0], int) and CHUNKS * s[0] + s[1] < 2):
                        wait(mixb, later(s, -2))
                    differences(s, h1, t1_out, dh1)
                    wait(a_ready, later(s, -1))
                    for stream in range(3):
                        for b in range(NB):
                            mix(h1, pkv_a, stream, xa[:, stream, b, :], b, mixa)

                def mix_b(s):
                    if s[1] == 0:
                        nc.vector.tensor_copy(pkv_b[:], one(pk, s[0], CMK, CMR + 1)).then_inc(pkb_copied, 1)
                        dve.wait_ge(pkb_copied, s[0] + 1)
                    differences(s, h2, t2_out, dh2)
                    for odd in range(2):
                        wait(ck_sq[odd], later(s, -1))
                    wait(cr_ready, later(s, -1))
                    for stream, dst in enumerate((relu, xr)):
                        for b in range(NB):
                            mix(h2, pkv_b, stream, dst[:, b, :], b, mixb)
                    for b in range(NB):
                        wait(xk_high, s, b + 1)
                        nc.vector.tensor_tensor(xk[:, 1, b, :], relu[:, b, :], xk[:, 0, b, :], ALU.subtract
                                                ).then_inc(xk_low.sem, 1)

                def scan(s, between=lambda: None):
                    w, u = (lambda b: pkv_a[:, 0, 3, b:b + 1]), (lambda b: pkv_a[:, 0, 4, b:b + 1])
                    layer = s[0] + s[1] // CHUNKS
                    dve.wait_ge(pka_copied, layer * 3 + 3)
                    for b in range(NB):
                        wait(a_out, s, b + 1)
                        nc.vector.tensor_tensor_scan(PP[:, b, :], wd[:, b, :], K[:, b, :], 0.0, ALU.add, ALU.max
                                                     ).then_inc(pp_made.sem, 1)
                    for b in range(NB):
                        wait(pp_made, s, b + 1)
                        nc.vector.scalar_tensor_tensor(out=tok(E[:, 0], b), in0=before(PP, b), scalar=w(b), in1=tok(PP, b),
                                                       op0=ALU.add, op1=ALU.subtract).then_inc(ex_made.sem, 1)
                        nc.vector.tensor_tensor(tok(E[:, 1], b), tok(K, b), tok(PP, b), ALU.subtract).then_inc(ex_made.sem, 1)
                        nc.vector.scalar_tensor_tensor(out=tok(E[:, 2], b), in0=tok(K, b), scalar=u(b), in1=before(PP, b),
                                                       op0=ALU.add, op1=ALU.subtract).then_inc(ex_made.sem, 1)
                    between()
                    for b in range(NB):
                        wait(e_out, s, 3 * b + 2)
                        wait(a_out, s, 3 + b)
                        nc.vector.tensor_tensor(tok(EV, b), tok(E[:, 1], b), tok(V, b), ALU.mult).then_inc(ev_made.sem, 1)
                        nc.vector.tensor_tensor_scan(BB[:, b, :], E[:, 0, b, :], E[:, 1, b, :], 0.0, ALU.mult, ALU.add
                                                     ).then_inc(bb_made.sem, 1)
                        wait(ev_made, s, b + 1)
                        nc.vector.tensor_tensor_scan(AA[:, b, :], E[:, 0, b, :], EV[:, b, :], 0.0, ALU.mult, ALU.add
                                                     ).then_inc(aa_made.sem, 1)
                    wait(e_out, s, 6)
                    th = tok2(E[:, 2])
                    stt = nc.vector.scalar_tensor_tensor
                    wait(bb_made, s, 2)
                    stt(out=tok2(PP), in0=th, scalar=1.0, in1=before2(BB), op0=ALU.add, op1=ALU.mult).then_inc(c1_made.sem, 1)
                    wait(aa_made, s, 2)
                    stt(out=tok2(EV), in0=th, scalar=-1.0, in1=tok2(V), op0=ALU.add, op1=ALU.mult).then_inc(n2_made.sem, 1)
                    wait(c1_made, s)
                    stt(out=tok2(K), in0=th, scalar=1.0, in1=before2(AA), op0=ALU.add, op1=ALU.mult).then_inc(n1_made.sem, 1)
                    stt(out=tok2(PP), in0=tok2(PP), scalar=1.0, in1=th, op0=ALU.add, op1=ALU.subtract).then_inc(den_made.sem, 1)
                    wait(n1_made, s)
                    nc.vector.tensor_tensor(tok2(K), tok2(K), tok2(EV), ALU.subtract).then_inc(nu_made.sem, 1)
                    wait(den_made, s)
                    nc.vector.reciprocal(tok2(BB), tok2(PP)).then_inc(inv_made.sem, 1)
                    wait(a_out, s, 6)
                    wait(nu_made, s)
                    stt(out=tok2(K), in0=tok2(R), scalar=1.0, in1=tok2(K), op0=ALU.add, op1=ALU.mult).then_inc(yr_made.sem, 1)
                    wait(yr_made, s)
                    wait(inv_made, s)
                    wait(wo_ready, later(s, -1))
                    nc.vector.tensor_tensor(ys[:, :, :].rearrange("p b (n t) -> p (b n) t", t=T), tok2(K), tok2(BB),
                                            ALU.mult).then_inc(ys_made.sem, 1)

                def step(s):
                    residual1(s)
                    statistics2(s)
                    if has(s, 2):
                        statistics1(later(s, 2))
                    norm2(s)
                    if has(s, 2):
                        norm1(later(s, 2))
                    mix_b(s)
                    if has(s, 1):
                        scan(later(s, 1), (lambda: mix_a(later(s, 2))) if has(s, 2) else (lambda: None))

                statistics1((0, 0))
                norm1((0, 0))
                statistics1((0, 1))
                mix_a((0, 0))
                norm1((0, 1))
                scan((0, 0), lambda: mix_a((0, 1)))
                with nc.vector.Fori(0, LAYERS - 1) as l:
                    for c in range(CHUNKS):
                        step((l, c))
                for c in range(CHUNKS):
                    step((LAYERS - 1, c))
                next_stage((LAYERS - 1, CHUNKS))



def attention(nc, t, X, H0, H2, gate, src_i, dst_i, scatter, scattered, exp_in, ident, half_neg):
    EPS = 1e-05
    HEADS, HD = 16, 16
    HB = HEADS // NB
    REP = 3
    HG = [(b, h, min(REP, HB - h)) for b in range(NB) for h in range(0, HB, REP)]
    NG = len(HG)
    RK = REP * T
    VC = HD + 1
    PAIRS = CI // 2
    SECOND = 64
    BOTH = SECOND + T
    E = 8
    CAPACITY = CT
    assert CAPACITY == 2 * N // E
    AUG = 32 + T
    with ExitStack() as ctx:
        def sb(name, shape, dt=F32):
            return ctx.enter_context(nc.sbuf_tensor("at_" + name, shape, dt))

        def psum(name, shape, dt=F32):
            return ctx.enter_context(nc.psum_tensor("at_" + name, shape, dt))

        def made(name, per):
            return Made(ctx.enter_context(nc.semaphore("at_" + name)), per, 1)

        def sem(name):
            return ctx.enter_context(nc.semaphore("at_" + name))

        Wqk = sb("Wqk", [P, 4, NB, D])
        Wv = sb("Wv", [P, NB, D])
        Wp = sb("Wp", [P, NB, D])
        Wg = sb("Wg", [P, NB, 8])
        vec = sb("vec", [P, 4, NB])
        row = sb("row", [P, 2, D])
        cs = sb("cs", [P, 2, T])
        hmask = sb("hmask", [P, NB * HB])
        vmask = sb("vmask", [RK, HEADS])
        negk = sb("negk", [T, HB * T], BF16)
        identb = sb("identb", [P, P], BF16)
        sel = sb("sel", [AUG, NG, RK], BF16)
        st = sb("st", [P, 3, NT, 6])
        mv = sb("mv", [P, 3, NT, 2])
        vr = sb("vr", [P, 3, NT])
        rs = sb("rs", [P, 3, NT])
        S = sb("S", [P, NT, D])
        xn1 = sb("xn1", [P, NT, D])
        xn2 = sb("xn2", [P, NT, D])
        h1n = sb("h1n", [P, NB, CT])
        h1 = sb("h1", [P, NB, CT])
        h2 = sb("h2", [P, NB, CT])
        rot = sb("rot", [P, 2, 2, HALF])
        QKn = sb("QKn", [P, 2, NB, CT])
        QK = sb("QK", [P, 2, NB, CT])
        kbd = sb("kbd", [P, 2, 2, NB, HB, T])
        hr = sb("hr", [P, 2, 2, NB, RK])
        vbd = sb("vbd", [RK, 2, 2, HEADS, VC])
        mx = sb("mx", [P, 2, HEADS], BF16)
        aug = sb("aug", [AUG, 2, 2 * T], BF16)
        PT = sb("PT", [RK, 2, 2, NG * T])
        inv = sb("inv", [P, 2, HEADS])
        O = sb("O", [P, 2, D])
        aT = sb("aT", [P, NB, CT])
        LG = sb("LG", [P, NT, E])
        iota8 = sb("iota8", [P, E])
        absent = sb("absent", [P, NT, 2])
        carry = sb("carry", [P, E, NT])
        spare = sb("spare", [P, 2, NT])
        upto = sb("upto", [P, P], BF16)
        ones = sb("ones", [P, P], BF16)
        top = sb("top", [P, NT])
        ex = sb("ex", [P, NT, E])
        total = sb("total", [P, NT])
        inv_total = sb("inv_total", [P, NT])
        gates = sb("gates", [P, NT, E])
        best = sb("best", [P, NT, 8])
        which = sb("which", [P, NT, 8], mybir.dt.uint32)
        who = sb("who", [P, NT, 2])
        chosen = sb("chosen", [P, 2, E, NT])
        mask = sb("mask", [P, E, NT])
        maskb = sb("maskb", [P, E, NT], BF16)
        upto_tile = sb("upto_tile", [P, E, NT])
        counts = sb("counts", [P, E])
        before_tile = sb("before_tile", [P, E, NT])
        before = sb("before", [P, E, NT], BF16)
        place = sb("place", [P, 2, E, NT])
        pos = sb("pos", [P, 2, NT])
        keep = sb("keep", [P, 2, NT])
        slot = sb("slot", [P, 2, NT])
        dst = sb("dst", [P, 2, NT])
        src = sb("src", [P, 2, NT])
        zeros = sb("zeros", [P, 2 * N // CHUNKS // P * D])
        zero_rows = sem("zero_rows")
        exp_zeroed = sem("exp_zeroed")
        ps_a = psum("ps_a", [P, 4, 512])
        ps_st = psum("ps_st", [P, 512])
        ps_o = psum("ps_o", [P, 512])
        ps_v = psum("ps_v", [P, 512])
        ps_x = psum("ps_x", [P, 512])
        ps_mT = ps_st[:, 448:512].bitcast(BF16)
        ps_oT = ps_x[:, 128:128 + 2 * BOTH]
        ps_pos = ps_a[:, 0, 0:E * NT]

        w_in = sem("w_in")
        h2_scaled = made("h2_scaled", NT)
        const = sem("const")
        carrier = sem("carrier")
        zero = sem("zero")
        summed = made("summed", NT)
        st_made = [made(f"st_made{k}", 1) for k in range(3)]
        mv_made = [made(f"mv_made{k}", 1) for k in range(3)]
        h0_made = made("h0_made", NT)
        xn1_made = made("xn1_made", NT)
        rot_made = made("rot_made", 16)
        qk_copied = made("qk_copied", 1)
        v_out = made("v_out", 2 * PAIRS)
        mx_made = made("mx_made", PAIRS)
        inv_made = made("inv_made", PAIRS)
        o_made = made("o_made", PAIRS)
        x_made = made("x_made", NT)
        xn2_made = made("xn2_made", NT)
        ve = [made(f"ve{k}", 1) for k in range(3)]
        rs_made = [made(f"rs_made{k}", 1) for k in range(3)]
        rope = made("rope", 8)
        kbd_made = made("kbd_made", 2 * PAIRS)
        t1_ready = made("t1_ready", len(GROUPS))
        qk_ready = made("qk_ready", 8)
        v_ready = made("v_ready", PAIRS)
        s_ready = made("s_ready", PAIRS)
        mT_ready = made("mT_ready", PAIRS)
        st_ready = made("st_ready", PAIRS)
        o_ready = made("o_ready", PAIRS)
        oT_ready = made("oT_ready", PAIRS)
        p_ready = made("p_ready", NT)
        t2_ready = made("t2_ready", len(GROUPS))
        lg_ready = made("lg_ready", NT)
        t1_out = made("t1_out", 2 * len(GROUPS))
        h1_copied = made("h1_copied", 1)
        hr_made = made("hr_made", 2 * PAIRS)
        mT_out = made("mT_out", PAIRS)
        e_out = made("e_out", PAIRS)
        oT_out = made("oT_out", PAIRS)
        t2_out = made("t2_out", 2 * len(GROUPS))
        lg_out = made("lg_out", 2)
        MASKED, PLACED, ROUTE = 16, 18, 28
        routed = made("routed", ROUTE)
        logits_exp = made("logits_exp", 1)
        counted = made("counted", 1)
        kept = sem("kept")

        def credit(eng, *sems):
            for s in sems:
                eng.sem_inc(s.sem, s.per)

        combos = [(x, b, h) for x in range(2) for b in range(NB) for h in range(2)]
        SLOTS = {3: (0,), 4: (1,), 5: (2,), 6: (3,), 7: (4,), 8: (5,), 9: (6,), 10: (7,)}

        def tile(s, i):
            if isinstance(s[0], int):
                return slice((s[0] + s[1]) * NT + i, (s[0] + s[1]) * NT + i + 1)
            return bass.ds(s[0] * NT + (s[1] * NT + i), 1)

        def chunks(eng, front, first_pair, body):
            front((0, 0))
            first_pair((0, 0))
            body(None, (0, 0), (1, 0))
            with eng.Fori(0, CHUNKS - 2) as n:
                body((n, 0), (n, 1), (n, 2))
            body((CHUNKS - 2, 0), (CHUNKS - 1, 0), None)

        with nc.Block() as block:
            @block.sync
            def _(sp):
                for dst, name in ((Wqk, "Wqk"), (Wv, "Wv"), (Wp, "Wproj"), (Wg, "Wgate"), (vec, "ffn_vec"), (row, "ffn_rows"),
                                  (cs, "cos_sin"), (hmask, "head_mask"), (vmask, "value_mask"), (negk, "causal"),
                                  (identb, "identb"), (sel, "select"), (iota8, "iota8"), (absent, "absent"), (carry, "carry"),
                                  (spare, "spare"), (upto, "upto"), (ones, "onesb")):
                    nc.sync.dma_start(dst[:], t[name]).then_inc(w_in, 16)
                for p in range(2):
                    for i in range(2):
                        nc.sync.dma_start(aug[32:AUG, p, i * T:(i + 1) * T], t["causalT"]).then_inc(w_in, 16)
                sp.wait_ge(zero_rows, 1)
                for part in range(CHUNKS):
                    rows = exp_in[part * (2 * N // CHUNKS):(part + 1) * (2 * N // CHUNKS), :]
                    nc.sync.dma_start(rows.rearrange("(p r) d -> p (r d)", p=P), zeros[:]).then_inc(exp_zeroed, 16)
                sp.wait_ge(exp_zeroed, 16 * CHUNKS)
            LOADS = 16 * (18 + 4)

            @block.gpsimd
            def _(pool):
                wait = lambda m, s, j=None: pool.wait_ge(m.sem, m.at(s, j))
                nc.gpsimd.memset(zeros[:], 0.0).then_inc(zero_rows, 1)
                nc.gpsimd.memset(mv[:], 1.0).then_inc(const, 1)
                nc.gpsimd.memset(LG[:], 0.0).then_inc(const, 1)
                nc.gpsimd.memset(aug[0:32, :, :], 0.0).then_inc(const, 1)
                credit(pool, *ve, *rs_made, rope, kbd_made)
                credit(pool, ve[0], rs_made[0])
                pool.wait_ge(const, 3)

                def root(s, k):
                    wait(mv_made[k], s)
                    pool.sem_inc(carrier, 1)
                    nc.gpsimd.tensor_scalar(vr[:, k, :], mv[:, k, :, 1], 1.0, EPS, ALU.mult, ALU.add).then_inc(ve[k].sem, 1)
                    wait(ve[k], s)
                    nc.gpsimd.tensor_tensor(rs[:, k, :], vr[:, k, :], half_neg[:, 0:NT], ALU.pow).then_inc(rs_made[k].sem, 1)

                def add_rotated(s, js):
                    for j in js:
                        x, b, h = combos[j]
                        wait(rot_made, s, 2 * j + 2)
                        if j == 0:
                            wait(qk_copied, later(s, -1))
                        nc.gpsimd.tensor_tensor(QKn[:, x, b, h * HALF:(h + 1) * HALF], rot[:, j % 2, 0, :], rot[:, j % 2, 1, :],
                                                ALU.add).then_inc(rope.sem, 1)

                def keys_by_head(s, p):
                    if p == 0:
                        wait(qk_copied, s)
                        wait(st_ready, later(s, -1))
                    if p >= 2:
                        wait(st_ready, s, p - 1)
                    for i in range(2):
                        first = (2 * p + i) * T
                        for b in range(NB):
                            k = QK[:, 1, b:b + 1, first:first + T].to_broadcast([P, HB, T])
                            m = hmask[:, b * HB:(b + 1) * HB].rearrange("p (h a) -> p h a", a=1).to_broadcast([P, HB, T])
                            a = nc.gpsimd.tensor_tensor(kbd[:, p % 2, i, b, :, :], k, m, ALU.mult)
                        a.then_inc(kbd_made.sem, 1)

                def front(s):
                    root(s, 1)
                    pool.wait_ge(w_in, LOADS)
                    add_rotated(s, range(8))

                def first_pair(s):
                    keys_by_head(s, 0)

                def body(prev, s, nxt):
                    for k in range(PAIRS + 4):
                        if nxt:
                            add_rotated(nxt, SLOTS.get(k - 1, ()))
                        if k + 1 < PAIRS:
                            keys_by_head(s, k + 1)
                        if nxt and k < 2:
                            root(nxt, k)
                        if prev and 4 <= k < 9:
                            if k == 4:
                                pool.wait_ge(exp_zeroed, 16 * CHUNKS)
                                wait(routed, prev)
                                pool.sem_inc(carrier, 1)
                            scatter(k - 4)
                    if nxt:
                        first_pair(nxt)
                    root(s, 2)

                chunks(nc.gpsimd, front, first_pair, body)

            @block.tensor
            def _(pe):
                wait = lambda m, s, j=None: pe.wait_ge(m.sem, m.at(s, j))
                credit(pe, t1_ready, qk_ready, v_ready, s_ready, mT_ready, st_ready, o_ready, oT_ready, p_ready, t2_ready,
                       lg_ready, counted)
                pe.wait_ge(w_in, LOADS)
                pe.wait_ge(const, 3)
                pe.wait_ge(zero, 4)

                def transposes(xn, made_, ready, free, s):
                    for q, tiles in enumerate(GROUPS):
                        wait(made_, s, tiles[-1] + 1)
                        free(q)
                        if TILES[tiles[0]][1] < P:
                            pe.sem_inc(carrier, 1)
                        width = sum(TILES[i][1] for i in tiles)
                        for i in tiles:
                            r = TILES[i][1]
                            at = TILES[i][0] - TILES[tiles[0]][0]
                            for b in range(NB):
                                a = nc.tensor.transpose(ps_a[:, q % 2, b * width + at:b * width + at + r],
                                                        xn[0:r, i, b * P:(b + 1) * P], ident[0:r, 0:r])
                        a.then_inc(ready.sem, 1)

                def queries_keys(s, js, spread):
                    for j in js:
                        x, b, h = combos[j]
                        if j == 0:
                            wait(t1_out, s)
                        if j >= 1 + spread:
                            wait(rot_made, s, 2 * (j - spread))
                        for v in range(2):
                            for kb in range(NB):
                                a = nc.tensor.matmul(ps_a[:, (2 * (j % 2) if spread else 0) + v, 0:HALF],
                                                     Wqk[:, 2 * x + v, kb, b * P:(b + 1) * P],
                                                     h1n[:, kb, h * HALF:(h + 1) * HALF], start=(kb == 0), stop=(kb == NB - 1))
                        a.then_inc(qk_ready.sem, 1)

                def values_scores(s, p):
                    if p >= 1:
                        wait(v_out, s, 2 * p)
                    else:
                        wait(v_out, later(s, -1))
                    wait(hr_made, s, 2 * p + 2)
                    for i in range(2):
                        for kb in range(NB):
                            a = nc.tensor.matmul(ps_v[0:RK, i * D:(i + 1) * D], hr[:, p % 2, i, kb, :], Wv[:, kb, :],
                                                 start=(kb == 0), stop=(kb == NB - 1))
                    a.then_inc(v_ready.sem, 1)
                    wait(kbd_made, s, 2 * p + 2)
                    if p >= 1:
                        wait(mx_made, s, p)
                    else:
                        wait(mx_made, later(s, -1))
                        wait(rot_made, s)
                    for i in range(2):
                        first = (2 * p + i) * T
                        for b in range(NB):
                            dst = ps_a[SECOND * i:SECOND * i + T, 2 + b, 0:HB * T].rearrange("p (h k) -> p h k", k=T)
                            nc.tensor.matmul(dst, QK[:, 0, b, first:first + T], kbd[:, p % 2, i, b, :, :],
                                             start=True, stop=False)
                            a = nc.tensor.matmul(dst, identb[0:T, 0:T], negk[:, :].rearrange("p (h k) -> p h k", k=T),
                                                 start=False, stop=True)
                    a.then_inc(s_ready.sem, 1)

                def maxima(s, p):
                    wait(mx_made, s, p + 1)
                    if p >= 1:
                        wait(mT_out, s, p)
                    nc.tensor.transpose(ps_mT[0:HEADS, 0:BOTH], mx[0:BOTH, p % 2, :], identb[0:BOTH, 0:BOTH]
                                        ).then_inc(mT_ready.sem, 1)

                def scores_transposed(s, p):
                    wait(mT_out, s, p + 1)
                    wait(e_out, s, p) if p >= 1 else wait(e_out, later(s, -1))
                    for i in range(2):
                        first = (2 * p + i) * T
                        for g, (b, h, m) in enumerate(HG):
                            dst = ps_st[0:m * T, (i * NG + g) * T:(i * NG + g + 1) * T]
                            nc.tensor.matmul(dst, kbd[:, p % 2, i, b, h:h + m, :].rearrange("p h k -> p (h k)"), QK[:, 0, b, first:first + T],
                                             start=True, stop=False)
                            a = nc.tensor.matmul(dst, sel[:, g, 0:m * T], aug[:, p % 2, i * T:(i + 1) * T], start=False, stop=True)
                    a.then_inc(st_ready.sem, 1)

                def outputs(s, p):
                    wait(e_out, s, p + 1)
                    wait(v_out, s, 2 * p + 2)
                    wait(o_made, s, p) if p >= 1 else wait(o_made, later(s, -1))
                    for i in range(2):
                        for g, (b, h, m) in enumerate(HG):
                            h0 = b * HB + h
                            a = nc.tensor.matmul(ps_o[SECOND * i:SECOND * i + T, h0 * VC:(h0 + m) * VC],
                                                 PT[0:m * T, p % 2, i, g * T:(g + 1) * T],
                                                 vbd[0:m * T, p % 2, i, h0:h0 + m, :].rearrange("p h v -> p (h v)"),
                                                 start=True, stop=True)
                    a.then_inc(o_ready.sem, 1)

                def outputs_transposed(s, p):
                    wait(o_made, s, p + 1)
                    wait(oT_out, s, p) if p >= 1 else wait(oT_out, later(s, -1))
                    for b in range(NB):
                        a = nc.tensor.transpose(ps_oT[:, b * BOTH:(b + 1) * BOTH], O[0:BOTH, p % 2, b * P:(b + 1) * P],
                                                ident[0:BOTH, 0:BOTH])
                    a.then_inc(oT_ready.sem, 1)

                def t1(s, free_banks):
                    transposes(xn1, xn1_made, t1_ready, lambda q: free_banks() if q < 2 else wait(t1_out, s, 2), s)

                def front(s):
                    t1(s, lambda: None)
                    queries_keys(s, range(8), True)

                def first_pair(s):
                    values_scores(s, 0)

                def body(prev, s, nxt):
                    def free():
                        wait(lg_out, later(s, -1))
                        wait(rot_made, s)
                        if prev:
                            wait(routed, prev, PLACED)

                    for k in range(PAIRS + 2):
                        if k >= 2:
                            outputs(s, k - 2)
                        if prev and k == 2:
                            count(prev)
                        if nxt and k == 3:
                            t1(nxt, free)
                        if 1 <= k <= PAIRS:
                            maxima(s, k - 1)
                        if 1 <= k < PAIRS:
                            values_scores(s, k)
                        if k >= 2:
                            outputs_transposed(s, k - 2)
                        if 1 <= k <= PAIRS:
                            scores_transposed(s, k - 1)
                        if nxt:
                            queries_keys(nxt, SLOTS.get(k, ()), False)
                    if nxt:
                        queries_keys(nxt, SLOTS[PAIRS + 2], False)
                    wait(oT_out, s)
                    if nxt:
                        wait(rot_made, nxt)
                    for i, (first, r) in enumerate(TILES):
                        if i >= 2:
                            wait(x_made, s, i - 1)
                        for b in range(NB):
                            a = nc.tensor.matmul(ps_a[0:r, i % 2, 0:D], aT[:, b, first:first + r], Wp[:, b, :], start=(b == 0),
                                                 stop=(b == NB - 1))
                        a.then_inc(p_ready.sem, 1)
                    if nxt:
                        first_pair(nxt)
                    transposes(xn2, xn2_made, t2_ready,
                               lambda q: wait(x_made, s) if q < 2 else wait(t2_out, s, 2), s)
                    wait(t2_out, s)
                    for i, (first, r) in enumerate(TILES):
                        for b in range(NB):
                            a = nc.tensor.matmul(ps_a[0:r, 1, 8 * i:8 * i + 8], h2[:, b, first:first + r], Wg[:, b, :],
                                                 start=(b == 0), stop=(b == NB - 1))
                        a.then_inc(lg_ready.sem, 1)

                def count(s):
                    wait(routed, s, MASKED)
                    wait(lg_out, s)
                    nc.tensor.matmul(ps_pos, upto[:], maskb[:].rearrange("p e n -> p (e n)"), start=True, stop=False)
                    nc.tensor.matmul(ps_pos, ones[:], before[:].rearrange("p e n -> p (e n)"), start=False, stop=True
                                     ).then_inc(counted.sem, 1)

                chunks(nc.tensor, front, first_pair, body)
                count((CHUNKS - 1, 0))

            @block.scalar
            def _(act):
                wait = lambda m, s, j=None: act.wait_ge(m.sem, m.at(s, j))
                credit(act, t1_out, h1_copied, hr_made, mT_out, e_out, oT_out, t2_out, lg_out, logits_exp)
                act.wait_ge(w_in, LOADS)
                act.wait_ge(const, 3)
                act.wait_ge(zero, 4)

                def evict(ready, h, k, out_, s):
                    for q, tiles in enumerate(GROUPS):
                        width = sum(TILES[i][1] for i in tiles)
                        first = TILES[tiles[0]][0]
                        wait(ready, s, q + 1)
                        for b in range(NB):
                            nc.scalar.activation(h[:, b, first:first + width], ps_a[:, q % 2, b * width:(b + 1) * width],
                                                 ACT.Identity, bias=vec[:, k + 1, b:b + 1], scale=vec[:, k, b:b + 1]
                                                 ).then_inc(out_.sem, 1)

                def front(s):
                    wait(h1_copied, later(s, -1))
                    wait(qk_ready, later(s, -1))
                    evict(t1_ready, h1n, 0, t1_out, s)

                def repeated(s, p):
                    if p == 0:
                        wait(h1_copied, s)
                    wait(v_ready, s, p - 1) if p >= 2 else wait(v_ready, later(s, -1))
                    for i in range(2):
                        first = (2 * p + i) * T
                        src = h1[:, :, first:first + T].rearrange("p b (a t) -> p b a t", a=1)
                        nc.scalar.activation(hr[:, p % 2, i, :, :].rearrange("p b (a t) -> p b a t", t=T),
                                             src.to_broadcast([P, NB, REP, T]), ACT.Copy).then_inc(hr_made.sem, 1)

                def maxima(s, p):
                    wait(mT_ready, s, p + 1)
                    wait(st_ready, s, p - 1) if p >= 2 else wait(st_ready, later(s, -1))
                    nc.scalar.activation(aug[0:HEADS, p % 2, :].rearrange("p (i q) -> p i q", i=2),
                                         ps_mT[0:HEADS, 0:2 * SECOND].rearrange("p (i q) -> p i q", i=2)[:, :, 0:T],
                                         ACT.Copy).then_inc(mT_out.sem, 1)

                def exponentials(s, p):
                    wait(st_ready, s, p + 1)
                    wait(o_ready, s, p - 1) if p >= 2 else wait(o_ready, later(s, -1))
                    nc.scalar.activation(PT[:, p % 2, :, :], ps_st[0:RK, 0:2 * NG * T].rearrange("p (i x) -> p i x", i=2),
                                         ACT.Exp, scale=float(HD) ** -0.5).then_inc(e_out.sem, 1)

                def transposed(s, p):
                    wait(oT_ready, s, p + 1)
                    if p == 0:
                        wait(p_ready, later(s, -1))
                    for b in range(NB):
                        src = ps_oT[:, b * BOTH:b * BOTH + BOTH]
                        for i in range(2):
                            a = nc.scalar.activation(aT[:, b, (2 * p + i) * T:(2 * p + i + 1) * T],
                                                     src[:, SECOND * i:SECOND * i + T], ACT.Copy)
                    a.then_inc(oT_out.sem, 1)

                def first_pair(s):
                    wait(hr_made, later(s, -1))
                    wait(t1_out, s)
                    nc.scalar.activation(h1[:], h1n[:], ACT.Copy).then_inc(h1_copied.sem, 1)
                    repeated(s, 0)

                def body(prev, s, nxt):
                    for k in range(PAIRS + 2):
                        if nxt and k == 3:
                            front(nxt)
                        if k + 1 < PAIRS:
                            repeated(s, k + 1)
                        if prev and k == 1:
                            exponentiate(prev)
                        if 1 <= k <= PAIRS:
                            maxima(s, k - 1)
                        if k >= 2:
                            transposed(s, k - 2)
                        if 1 <= k <= PAIRS:
                            exponentials(s, k - 1)
                    if nxt:
                        first_pair(nxt)
                    wait(lg_ready, later(s, -1))
                    evict(t2_ready, h2, 2, t2_out, s)
                    wait(lg_ready, s)
                    for first, tiles, r in ((0, NT - 1, P), (NT - 1, 1, TILES[-1][1])):
                        nc.scalar.activation(LG[0:r, first:first + tiles, :],
                                             ps_a[0:r, 1, 8 * first:8 * (first + tiles)].rearrange("p (i e) -> p i e", e=8),
                                             ACT.Copy).then_inc(lg_out.sem, 1)

                def exponentiate(s):
                    wait(routed, s, 2)
                    nc.scalar.activation(ex[:], ex[:], ACT.Exp).then_inc(logits_exp.sem, 1)

                chunks(nc.scalar, front, first_pair, body)
                exponentiate((CHUNKS - 1, 0))

            @block.vector
            def _(dve):
                wait = lambda m, s, j=None: dve.wait_ge(m.sem, m.at(s, j))
                credit(dve, routed, summed, *st_made, *mv_made, h0_made, xn1_made, rot_made, qk_copied, h2_scaled, v_out,
                       mx_made, inv_made, o_made, x_made, xn2_made)
                credit(dve, summed, st_made[0], mv_made[0], h0_made)
                dve.wait_ge(const, 3)

                def stats(s, k, src, ready):
                    for i, (_, r) in enumerate(TILES):
                        wait(ready, s, i + 1)
                        dve.sem_inc(carrier, 1)
                        a = nc.vector.bn_stats(st[0:r, k, i, :], src(i, r))
                    a.then_inc(st_made[k].sem, 1)
                    wait(st_made[k], s)
                    dve.sem_inc(carrier, 1)
                    for i, (_, r) in enumerate(TILES):
                        a = nc.vector.bn_aggr(mv[0:r, k, i, :], st[0:r, k, i, :])
                    a.then_inc(mv_made[k].sem, 1)

                def normed(s, k, src, dst, done):
                    wait(mv_made[k], s)
                    wait(rs_made[k], s)
                    for i, (_, r) in enumerate(TILES):
                        nc.vector.tensor_scalar(dst(i, r), src(i, r), mv[0:r, k, i, 0:1], rs[0:r, k, i:i + 1],
                                                ALU.subtract, ALU.mult).then_inc(done.sem, 1)

                def front_norms(s, k):
                    h0 = lambda i, r: H0[0:r, tile(s, i), :]
                    if k == 0:
                        for i, (_, r) in enumerate(TILES):
                            nc.vector.tensor_tensor(S[0:r, i:i + 1, :], X[0:r, tile(s, i), :], h0(i, r), ALU.add
                                                    ).then_inc(summed.sem, 1)
                        stats(s, 0, lambda i, r: S[0:r, i, :], summed)
                    if k == 1:
                        normed(s, 0, lambda i, r: S[0:r, i:i + 1, :], h0, h0_made)
                        stats(s, 1, h0, h0_made)
                    if k == 2:
                        wait(t1_ready, later(s, -1))
                        normed(s, 1, h0, lambda i, r: xn1[0:r, i:i + 1, :], xn1_made)

                def rotate(s, js, spread):
                    for j in js:
                        wait(qk_ready, s, j + 1)
                        wait(rope, s, j - 1) if j >= 2 else wait(rope, later(s, -1))
                        for v in range(2):
                            nc.vector.tensor_tensor(rot[:, j % 2, v, :].rearrange("p (n t) -> p n t", t=T),
                                                    ps_a[:, (2 * (j % 2) if spread else 0) + v, 0:HALF]
                                                    .rearrange("p (n t) -> p n t", t=T),
                                                    cs[:, v:v + 1, :].to_broadcast([P, CI // 2, T]), ALU.mult
                                                    ).then_inc(rot_made.sem, 1)

                def values(s, p):
                    wait(v_ready, s, p + 1)
                    wait(o_ready, s, p - 1) if p >= 2 else wait(o_ready, later(s, -1))
                    m = vmask[:, :].rearrange("p (h a) -> p h a", a=1).to_broadcast([RK, HEADS, HD])
                    for i in range(2):
                        nc.vector.tensor_tensor(vbd[:, p % 2, i, :, 0:HD],
                                                ps_v[0:RK, i * D:(i + 1) * D].rearrange("p (h v) -> p h v", v=HD), m, ALU.mult
                                                ).then_inc(v_out.sem, 1)

                def maxima(s, p):
                    wait(s_ready, s, p + 1)
                    wait(mT_ready, s, p - 1) if p >= 2 else wait(mT_ready, later(s, -1))
                    nc.vector.tensor_reduce(mx[0:BOTH, p % 2, :].rearrange("p (b h) -> p b h", b=NB),
                                            ps_a[0:BOTH, 2:4, 0:HB * T].rearrange("p b (h k) -> p b h k", k=T), AX.X, ALU.max
                                            ).then_inc(mx_made.sem, 1)

                def normalise(s, p):
                    wait(o_ready, s, p + 1)
                    o = ps_o[0:BOTH, 0:HEADS * VC].rearrange("p (h v) -> p h v", v=VC)
                    nc.vector.reciprocal(inv[0:BOTH, p % 2, :].rearrange("p (h a) -> p h a", a=1), o[:, :, HD:VC]
                                         ).then_inc(inv_made.sem, 1)
                    wait(inv_made, s, p + 1)
                    wait(oT_ready, s, p - 1) if p >= 2 else wait(oT_ready, later(s, -1))
                    nc.vector.tensor_tensor(O[0:BOTH, p % 2, :].rearrange("p (h v) -> p h v", v=HD), o[:, :, 0:HD],
                                            inv[0:BOTH, p % 2, :].rearrange("p (h a) -> p h a", a=1
                                                                            ).to_broadcast([BOTH, HEADS, HD]), ALU.mult
                                            ).then_inc(o_made.sem, 1)

                def route(s, part):
                    V = nc.vector
                    done = [{0: 0, 1: 2, 2: MASKED}[part]]

                    def then(*instructions):
                        for a in instructions:
                            a.then_inc(routed.sem, 1)
                            done[0] += 1
                        wait(routed, s, done[0])

                    by_e = lambda x: x.rearrange("p (n a) -> p n a", a=1).to_broadcast([P, NT, E])
                    flat = lambda x: x.rearrange("p e n -> p (e n)")
                    if part == 0:
                        wait(lg_out, s)
                        then(V.tensor_reduce(top[:], LG[:], AX.X, ALU.max))
                        then(V.tensor_tensor(ex[:], LG[:], by_e(top[:]), ALU.subtract))
                        assert done[0] == 2
                    if part == 1:
                        wait(logits_exp, s)
                        then(V.tensor_reduce(total[:], ex[:], AX.X, ALU.add))
                        then(V.reciprocal(inv_total[:], total[:]))
                        then(V.tensor_tensor(gates[:], ex[:], by_e(inv_total[:]), ALU.mult))
                        dve.sem_inc(carrier, 1)
                        for i in range(NT):
                            a = V.max(best[:, i, :], gates[:, i, :])
                        then(a)
                        dve.sem_inc(carrier, 1)
                        for i in range(NT):
                            a = V.max_index(which[:, i, :], best[:, i, :], gates[:, i, :])
                        then(a)
                        then(V.tensor_copy(who[:], which[:, :, 0:2]))
                        then(V.tensor_tensor(who[:], who[:], absent[:], ALU.add))
                        then(*(V.tensor_tensor(chosen[:, k], iota8[:].rearrange("p (e a) -> p e a", a=1).to_broadcast([P, E, NT]),
                                               who[:, :, k:k + 1].rearrange("p n a -> p a n").to_broadcast([P, E, NT]), ALU.is_equal)
                               for k in range(2)))
                        then(V.tensor_tensor(mask[:], chosen[:, 0], chosen[:, 1], ALU.add))
                        then(V.tensor_copy(maskb[:], mask[:]),
                             V.tensor_tensor_scan(flat(upto_tile[:]), flat(carry[:]), flat(mask[:]), 0.0, ALU.mult, ALU.add))
                        then(V.tensor_tensor(before_tile[:], upto_tile[:], mask[:], ALU.subtract))
                        by_n = counts[:].rearrange("p (e a) -> p e a", a=1)
                        then(V.tensor_tensor(before[:], before_tile[:], by_n.to_broadcast([P, E, NT]), ALU.add))
                        assert done[0] == MASKED, done[0]
                        V.tensor_tensor(by_n, by_n, upto_tile[:, :, NT - 1:NT], ALU.add).then_inc(kept, 1)
                    if part == 2:
                        wait(counted, s)
                        then(*(V.tensor_tensor(place[:, k], ps_pos.rearrange("p (e n) -> p e n", e=E), chosen[:, k], ALU.mult)
                               for k in range(2)))
                        assert done[0] == PLACED
                        then(*(V.tensor_reduce(pos[:, k, :], place[:, k].rearrange("p e n -> p n e"), AX.X, ALU.add)
                               for k in range(2)))
                        then(V.tensor_scalar(keep[:], pos[:], float(CAPACITY), None, ALU.is_le),
                             V.scalar_tensor_tensor(out=slot[:], in0=who[:].rearrange("p n k -> p k n"), scalar=float(CAPACITY),
                                                    in1=pos[:], op0=ALU.mult, op1=ALU.add))
                        then(V.tensor_scalar(slot[:], slot[:], -1.0, None, ALU.add))
                        here = slice(s[0] * NT, s[0] * NT + NT) if isinstance(s[0], int) else bass.ds(s[0] * NT + s[1] * NT, NT)
                        V.tensor_tensor(gate[:, :, here], best[:, :, 0:2].rearrange("p n k -> p k n"), keep[:], ALU.mult
                                        ).then_inc(kept, 1)
                        then(V.tensor_tensor(dst[:], slot[:], spare[:], ALU.subtract),
                             V.tensor_tensor(src[:], slot[:], keep[:], ALU.mult))
                        then(V.tensor_tensor(dst[:], dst[:], keep[:], ALU.mult))
                        then(V.tensor_tensor(dst[:], dst[:], spare[:], ALU.add))
                        dve.sem_inc(carrier, 1)
                        V.tensor_copy(src_i[:, :, here], src[:]).then_inc(kept, 1)
                        then(V.tensor_copy(dst_i[:], dst[:]))
                        V.tensor_scalar(spare[:], spare[:], float(NT * P), None, ALU.add).then_inc(kept, 1)
                        assert done[0] == ROUTE, done[0]

                def front(s):
                    stats(s, 1, lambda i, r: H0[0:r, tile(s, i), :], h0_made)
                    nc.vector.memset(ps_a[:], 0.0).then_inc(zero, 1)
                    nc.vector.memset(ps_st[:], 0.0).then_inc(zero, 1)
                    nc.vector.memset(ps_o[:], 1.0).then_inc(zero, 1)
                    nc.vector.memset(counts[:], 0.0).then_inc(zero, 1)
                    front_norms(s, 2)
                    dve.wait_ge(w_in, LOADS)
                    for p in range(2):
                        for i in range(2):
                            nc.vector.tensor_copy(vbd[:, p, i, :, HD:VC], vmask[:, :].rearrange("p (h a) -> p h a", a=1)
                                                  ).then_inc(zero, 1)
                    dve.wait_ge(zero, 8)
                    rotate(s, range(8), True)

                def copy_qk(s):
                    wait(rope, s)
                    wait(st_ready, later(s, -1))
                    wait(kbd_made, later(s, -1))
                    nc.vector.tensor_copy(QK[:], QKn[:]).then_inc(qk_copied.sem, 1)

                def first_pair(s):
                    copy_qk(s)
                    values(s, 0)
                    maxima(s, 0)

                def body(prev, s, nxt):
                    for k in range(PAIRS + 4):
                        if 2 <= k < PAIRS + 2:
                            normalise(s, k - 2)
                        if nxt:
                            rotate(nxt, SLOTS.get(k - 1, ()), False)
                        if 1 <= k < PAIRS:
                            values(s, k)
                            maxima(s, k)
                        if prev and k < 3:
                            route(prev, k)
                        if nxt and k < 3:
                            front_norms(nxt, k)
                    if nxt:
                        copy_qk(nxt)
                    for i, (_, r) in enumerate(TILES):
                        wait(p_ready, s, i + 1)
                        nc.vector.tensor_tensor(X[0:r, tile(s, i), :], ps_a[0:r, i % 2:i % 2 + 1, 0:D], H0[0:r, tile(s, i), :], ALU.add
                                                ).then_inc(x_made.sem, 1)
                    x = lambda i, r: X[0:r, tile(s, i), :]
                    stats(s, 2, x, x_made)
                    if nxt:
                        values(nxt, 0)
                    wait(t2_ready, later(s, -1))
                    normed(s, 2, x, lambda i, r: xn2[0:r, i:i + 1, :], xn2_made)
                    if nxt:
                        maxima(nxt, 0)
                    wait(xn2_made, s)
                    if prev:
                        dve.wait_ge(scattered, (prev[0] + (prev[1] + 1)) * (16 * 2 * NT))
                    for i, (_, r) in enumerate(TILES):
                        nc.vector.tensor_tensor(H2[0:r, i, :], xn2[0:r, i, :], row[0:r, 0, :], ALU.mult
                                                ).then_inc(h2_scaled.sem, 1)
                    for i, (_, r) in enumerate(TILES):
                        wait(h2_scaled, s, i + 1)
                        nc.vector.tensor_tensor(H2[0:r, i, :], H2[0:r, i, :], row[0:r, 1, :], ALU.add).then_inc(kept, 1)

                chunks(nc.vector, front, first_pair, body)
                for part in range(3):
                    route((CHUNKS - 1, 0), part)


def ffn_arrays(a, blocks):
    import numpy as np

    F = "L0_ffn_"
    hb, hd, rep = 8, 16, 3
    bf16 = mybir.dt.np(BF16)
    w = a[F + "Wqkv"].reshape(D, 16, 3, hd)
    q, k, v = (w[:, :, i] for i in range(3))
    swap = lambda m: np.concatenate([m[..., hd // 2:], m[..., :hd // 2]], -1)
    rows = lambda m: m.reshape(NB, P, -1).transpose(1, 0, 2)
    freq = (1.0 / 10000.0 ** (np.arange(0, hd, 2, dtype=np.float32) / np.float32(hd))).astype(np.float32)
    ang = np.arange(T, dtype=np.float32)[:, None] * freq
    cos, sin = np.cos(ang).astype(np.float32).T, np.sin(ang).astype(np.float32).T
    cs = np.stack([np.tile(np.concatenate([cos, cos]), (hb, 1)), np.tile(np.concatenate([-sin, sin]), (hb, 1))], 1)
    head = np.arange(P) // hd
    rep_of = (np.arange(16) % hb) % rep
    groups = [(b, h, min(rep, hb - h)) for b in range(NB) for h in range(0, hb, rep)]
    sel = np.zeros((32 + T, len(groups), rep * T), np.float32)
    for g, (b, h, m) in enumerate(groups):
        for r in range(m):
            sel[b * hb + h + r, g, r * T:(r + 1) * T] = -1
            sel[32 + np.arange(T), g, r * T + np.arange(T)] = 1
    later_key = np.where(np.arange(T)[None, :] > np.arange(T)[:, None], np.float32(-1e30), np.float32(0))
    return {
        "Wqk": np.stack([rows(np.ascontiguousarray(m).reshape(D, D)) for m in (q, swap(q), k, swap(k))], 1),
        "Wv": rows(v.reshape(D, D)),
        "Wproj": rows(a[F + "Wproj"]),
        "Wgate": rows(a[F + "Wgate"]),
        "ffn_vec": np.stack([blocks(a[F + n]) for n in ("ln1_g", "ln1_b", "ln2_g", "ln2_b")], 1),
        "ffn_rows": np.broadcast_to(np.stack([a[F + "ln2_g"], a[F + "ln2_b"]]), (P, 2, D)),
        "cos_sin": cs,
        "head_mask": np.tile((head[:, None] == np.arange(hb)[None, :]).astype(np.float32), (1, NB)),
        "value_mask": (np.arange(rep * T)[:, None] // T == rep_of[None, :]).astype(np.float32),
        "causal": np.tile(later_key, (1, hb)).astype(bf16),
        "causalT": later_key.T.astype(bf16),
        "identb": np.eye(P).astype(bf16),
        "select": sel.astype(bf16),
    }


def experts(nc, t, X, H0, gate, src_i, scatter, scattered, exp_in, exp_out, out, half_neg):
    EPS = 1e-05
    TT = CHUNKS * NT
    with ExitStack() as ctx:
        def sb(name, shape, dt=F32):
            return ctx.enter_context(nc.sbuf_tensor("ex_" + name, shape, dt))

        def sem(name):
            return ctx.enter_context(nc.semaphore("ex_" + name))

        expert_products(nc, t, scatter, scattered, exp_in, exp_out)

        got = sb("got", [P, TT, 2, D])
        S = sb("S", [P, TT, D])
        st = sb("st", [P, TT, 6])
        mv = sb("mv", [P, TT, 2])
        vr = sb("vr", [P, TT])
        rs = sb("rs", [P, TT])
        y = sb("y", [P, TT, D])
        gathered = [sem(f"gathered{c}") for c in range(CHUNKS)]
        added = sem("added")
        st_made = sem("st_made")
        mv_made = sem("mv_made")
        ve = sem("ve")
        rs_made = sem("rs_made")
        y_made = sem("y_made")
        stored = sem("stored")
        ones_in = sem("ones_in")
        with nc.Block() as block:
            @block.gpsimd
            def _(pool):
                nc.gpsimd.memset(mv[:], 1.0).then_inc(ones_in, 1)

                def gather(c):
                    for i in range(c * NT, (c + 1) * NT):
                        for k in range(2):
                            nc.gpsimd.indirect_dma_start(out=got[0:TILES[i % NT][1], i, k, :], out_offset=None, in_=exp_out,
                                                         in_offset=bass.IndirectOffsetOnAxis(
                                                             ap=src_i[0:TILES[i % NT][1], k, i:i + 1], axis=0)
                                                         ).then_inc(gathered[c], 16)

                def root(c):
                    part = slice(c * NT, (c + 1) * NT)
                    pool.wait_ge(mv_made, c + 1)
                    nc.gpsimd.tensor_scalar(vr[:, part], mv[:, part, 1], 1.0, EPS, ALU.mult, ALU.add).then_inc(ve, 1)
                    pool.wait_ge(ve, c + 1)
                    nc.gpsimd.tensor_tensor(rs[:, part], vr[:, part], half_neg[:, 0:NT], ALU.pow).then_inc(rs_made, 1)

                gather(0)
                pool.wait_ge(ones_in, 1)
                for c in range(1, CHUNKS):
                    gather(c)
                    root(c - 1)
                root(CHUNKS - 1)

            @block.vector
            def _(dve):
                V = nc.vector
                dve.wait_ge(ones_in, 1)
                tiles = lambda c: [(c * NT + i, r) for i, (_, r) in enumerate(TILES)]
                for c in range(CHUNKS):
                    for i, r in tiles(c):
                        V.tensor_tensor(S[0:r, i, :], X[0:r, i, :], H0[0:r, i, :], ALU.add).then_inc(added, 1)
                for c in range(CHUNKS):
                    dve.wait_ge(gathered[c], 16 * 2 * NT)
                    for k in range(2):
                        for i, r in tiles(c):
                            dve.wait_ge(added, TT + (2 * c + k - 1) * NT + i % NT + 1 if k else i + 1)
                            V.scalar_tensor_tensor(out=S[0:r, i, :], in0=got[0:r, i, k, :], scalar=gate[0:r, k, i:i + 1],
                                                   in1=S[0:r, i, :], op0=ALU.mult, op1=ALU.add).then_inc(added, 1)
                    for i, r in tiles(c):
                        dve.wait_ge(added, TT + (2 * c + 1) * NT + i % NT + 1)
                        a = V.bn_stats(st[0:r, i, :], S[0:r, i, :])
                    a.then_inc(st_made, 1)
                    dve.wait_ge(st_made, c + 1)
                    for i, r in tiles(c):
                        a = V.bn_aggr(mv[0:r, i, :], st[0:r, i, :])
                    a.then_inc(mv_made, 1)
                    dve.wait_ge(mv_made, c + 1)
                    dve.wait_ge(rs_made, c + 1)
                    for i, r in tiles(c):
                        a = V.tensor_scalar(y[0:r, i, :], S[0:r, i, :], mv[0:r, i, 0:1], rs[0:r, i:i + 1], ALU.subtract, ALU.mult)
                    a.then_inc(y_made, 1)

            @block.sync
            def _(sp):
                for c in range(CHUNKS):
                    sp.wait_ge(y_made, c + 1)
                    rows = out[c * CT:(c + 1) * CT, :]
                    nc.sync.dma_start(rows[0:4 * P, :].rearrange("(i p) d -> p i d", p=P), y[:, c * NT:c * NT + 4, :]
                                      ).then_inc(stored, 16)
                    nc.sync.dma_start(rows[4 * P:CT, :], y[0:CT - 4 * P, c * NT + 4, :]).then_inc(stored, 16)
                sp.wait_ge(stored, 32 * CHUNKS)


def expert_products(nc, t, scatter, scattered, exp_in, exp_out):
    E = 8
    TURN = 2
    with ExitStack() as ctx:
        def sb(name, shape, dt=F32):
            return ctx.enter_context(nc.sbuf_tensor("ep_" + name, shape, dt))

        def psum(name, shape, dt=F32):
            return ctx.enter_context(nc.psum_tensor("ep_" + name, shape, dt))

        def made(name, per):
            return Made(ctx.enter_context(nc.semaphore("ep_" + name)), per, TURN, TURN)

        ident = sb("ident", [P, P])
        W1 = sb("W1", [P, TURN, NB, FF])
        W2 = sb("W2", [P, TURN, FB, D])
        b1 = sb("b1", [P, TURN, FB])
        b2 = sb("b2", [P, TURN, D])
        xr = sb("xr", [P, TURN, NT, D])
        W1s = sb("W1s", [P, TURN, 2, NB, FF], F16)
        W2s = sb("W2s", [P, TURN, 2, FB, D], F16)
        xT = sb("xT", [P, TURN, 2, NB, CT], F16)
        hid = sb("hid", [P, 2, CT])
        hids = sb("hids", [P, 2, FB, CT], F16)
        y = sb("y", [P, TURN, NT, D])
        ps_h = psum("ps_h", [P, 4, 512])
        ps_t = psum("ps_t", [P, 2, 512])
        ps_y = psum("ps_y", [P, 2, 512])

        diag = ctx.enter_context(nc.semaphore("ep_diag"))
        carrier = ctx.enter_context(nc.semaphore("ep_carrier"))
        w1_in = [ctx.enter_context(nc.semaphore(f"ep_w1_in{c}")) for c in range(TURN)]
        w2_in = [ctx.enter_context(nc.semaphore(f"ep_w2_in{c}")) for c in range(TURN)]
        x_in = [ctx.enter_context(nc.semaphore(f"ep_x_in{c}")) for c in range(TURN)]
        t_ready = made("t_ready", len(GROUPS))
        h_ready = made("h_ready", FB)
        y_ready = made("y_ready", NT)
        t_high = made("t_high", 2 * len(GROUPS))
        t_out = made("t_out", 2 * len(GROUPS))
        w1_high, w1_out, w2_high, w2_out = (made(x, 1) for x in ("w1_high", "w1_out", "w2_high", "w2_out"))
        h_gelu = made("h_gelu", FB)
        h_high = made("h_high", FB)
        h_out = made("h_out", FB)
        PASSES = ((0, 0), (0, 1), (1, 0))
        y_out = made("y_out", NT)
        y_stored = [ctx.enter_context(nc.semaphore(f"ep_y_stored{c}")) for c in range(TURN)]

        def credit(eng, *sems):
            for s in sems:
                eng.sem_inc(s.sem, s.ahead * s.per)

        with nc.Block() as block:
            @block.sync
            def _(sp):
                wait = lambda m, s, j=None: sp.wait_ge(m.sem, m.at(s, j))

                one = lambda v, e: v[e:e + 1] if isinstance(e, int) else v[bass.ds(e, 1)]

                def load_rows(c, e):
                    rows = one(exp_in[0:E * CT, :].rearrange("(e r) d -> e r d", e=E), e)
                    nc.sync.dma_start(xr[:, c, 0:4, :], rows[:, 0:4 * P, :].rearrange("e (i p) d -> p (e i) d", p=P)
                                      ).then_inc(x_in[c], 16)
                    nc.sync.dma_start(xr[0:64, c, 4, :], rows[:, 4 * P:CT, :].rearrange("e r d -> (e r) d")).then_inc(x_in[c], 16)

                def load_weights(c, e):
                    for dst, name, into in ((W1[:, c].rearrange("p k f -> p (k f)"), "W1", w1_in), (b1[:, c, :], "b1", w1_in),
                                            (W2[:, c].rearrange("p k f -> p (k f)"), "W2", w2_in), (b2[:, c, :], "b2", w2_in)):
                        nc.sync.dma_start(dst, one(t[name], e).rearrange("e p n -> p (e n)")).then_inc(into[c], 16)

                def store(c, s, e):
                    wait(y_out, s)
                    rows = exp_out[:, :].rearrange("(e r) d -> e r d", e=E)
                    rows = rows[e:e + 1] if isinstance(e, int) else rows[bass.ds(e, 1)]
                    nc.sync.dma_start(rows[:, 0:4 * P, :].rearrange("e (i p) d -> p (e i) d", p=P), y[:, c, 0:4, :]
                                      ).then_inc(y_stored[c], 16)
                    nc.sync.dma_start(rows[:, 4 * P:CT, :].rearrange("e r d -> (e r) d"), y[0:64, c, 4, :]
                                      ).then_inc(y_stored[c], 16)

                for c in range(TURN):
                    sp.sem_inc(y_stored[c], 32)
                    load_weights(c, c)
                    if c == 0:
                        sp.wait_ge(scattered, 16 * 2 * NT * CHUNKS)
                    load_rows(c, c)
                with nc.sync.Fori(0, E // TURN - 1) as n:
                    for c in range(TURN):
                        store(c, (n, c), n * TURN + c)
                        load_rows(c, n * TURN + (TURN + c))
                        load_weights(c, n * TURN + (TURN + c))
                for c in range(TURN):
                    store(c, (E // TURN - 1, c), E - TURN + c)
                for c in range(TURN):
                    sp.wait_ge(y_stored[c], 32 + 32 * E // TURN)

            @block.gpsimd
            def _(pool):
                for i in range(NT):
                    scatter(i)
                nc.gpsimd.memset(ident[:], 0.0).then_inc(diag, 1)
                pool.wait_ge(diag, 1)
                nc.gpsimd.affine_select(out=ident[:], in_=ident[:], compare_op=ALU.not_equal, fill=1.0, base=0,
                                        pattern=[[-1, P]], channel_multiplier=1).then_inc(diag, 1)

            def turns(eng, step):
                with eng.Fori(0, E // TURN - 1) as n:
                    for c in range(TURN):
                        step((n, c), (n, c + 1))
                for c in range(TURN):
                    step((E // TURN - 1, c), (E // TURN - 1, c + 1) if c < TURN - 1 else None)

            def loads(s):
                return s[0] * 32 + 32 * (1 + s[1] // TURN)

            @block.tensor
            def _(pe):
                wait = lambda m, s, j=None: pe.wait_ge(m.sem, m.at(s, j))
                credit(pe, t_ready, h_ready, y_ready)
                pe.wait_ge(diag, 2)

                def transposes(s, qs):
                    c = s[1] % TURN
                    pe.wait_ge(x_in[c], loads(s))
                    for q in qs:
                        tiles = GROUPS[q]
                        wait(t_out, s, 2 * q - 2) if q == 2 else wait(t_out, later(s, -1))
                        if TILES[tiles[0]][1] < P:
                            pe.sem_inc(carrier, 1)
                        width = sum(TILES[i][1] for i in tiles)
                        for i in tiles:
                            r = TILES[i][1]
                            at = TILES[i][0] - TILES[tiles[0]][0]
                            for b in range(NB):
                                a = nc.tensor.transpose(ps_t[:, q % 2, b * width + at:b * width + at + r],
                                                        xr[0:r, c, i, b * P:(b + 1) * P], ident[0:r, 0:r])
                        a.then_inc(t_ready.sem, 1)

                def step(s, nxt):
                    c = s[1]
                    wait(t_out, s)
                    wait(w1_out, s)
                    for m in range(FB):
                        wait(h_high, s, m - 1) if m >= 2 else wait(h_high, later(s, -1))
                        for h in range(2):
                            for k, (w, x) in enumerate(PASSES):
                                for b in range(NB):
                                    a = nc.tensor.matmul(ps_h[:, 2 * (m % 2) + h, 0:HALF], W1s[:, c, w, b, m * P:(m + 1) * P],
                                                         xT[:, c, x, b, h * HALF:(h + 1) * HALF],
                                                         start=(k == b == 0), stop=(k == 2 and b == NB - 1))
                        a.then_inc(h_ready.sem, 1)
                    if nxt:
                        transposes(nxt, (0, 1))
                    wait(w2_out, s)
                    wait(h_high, s)
                    for i, (first, r) in enumerate(TILES):
                        if nxt and i == 1:
                            transposes(nxt, (2,))
                        wait(y_out, s, i - 1) if i >= 2 else wait(y_out, later(s, -1))
                        for k, (x, w) in enumerate(PASSES):
                            if i == 0 and k == 2:
                                wait(h_out, s)
                            for m in range(FB):
                                a = nc.tensor.matmul(ps_y[0:r, i % 2, 0:D], hids[:, x, m, first:first + r], W2s[:, c, w, m, :],
                                                     start=(k == m == 0), stop=(k == 2 and m == FB - 1))
                        a.then_inc(y_ready.sem, 1)

                transposes((0, 0), range(len(GROUPS)))
                turns(nc.tensor, step)

            @block.scalar
            def _(act):
                wait = lambda m, s, j=None: act.wait_ge(m.sem, m.at(s, j))
                credit(act, t_high, w1_high, w2_high, h_gelu, h_high)

                def high_rows(s):
                    c = s[1] % TURN
                    for q, tiles in enumerate(GROUPS):
                        width = sum(TILES[i][1] for i in tiles)
                        first = TILES[tiles[0]][0]
                        wait(t_ready, s, q + 1)
                        for b in range(NB):
                            nc.scalar.activation(xT[:, c, 0, b, first:first + width], ps_t[:, q % 2, b * width:(b + 1) * width],
                                                 ACT.Copy).then_inc(t_high.sem, 1)

                def high_weights(s):
                    c = s[1] % TURN
                    act.wait_ge(w1_in[c], loads(s))
                    nc.scalar.activation(W1s[:, c, 0], W1[:, c], ACT.Copy).then_inc(w1_high.sem, 1)
                    act.wait_ge(w2_in[c], loads(s))
                    wait(y_ready, later(s, -TURN))
                    nc.scalar.activation(W2s[:, c, 0], W2[:, c], ACT.Copy).then_inc(w2_high.sem, 1)

                def step(s, nxt):
                    for m in range(FB):
                        wait(h_ready, s, m + 1)
                        wait(h_out, s, m - 1) if m >= 2 else wait(h_out, later(s, -1))
                        nc.scalar.activation(hid[:, m % 2, :].rearrange("p (h n) -> p h n", h=2),
                                             ps_h[:, 2 * (m % 2):2 * (m % 2) + 2, 0:HALF], ACT.Gelu,
                                             bias=b1[:, s[1], m:m + 1]).then_inc(h_gelu.sem, 1)
                        wait(h_gelu, s, m + 1)
                        if m == 0:
                            wait(y_ready, later(s, -1))
                        nc.scalar.activation(hids[:, 0, m, :], hid[:, m % 2, :], ACT.Copy).then_inc(h_high.sem, 1)
                    if nxt:
                        wait(h_ready, later(nxt, -TURN))
                        high_rows(nxt)
                        high_weights(nxt)

                high_weights((0, 0))
                high_rows((0, 0))
                turns(nc.scalar, step)

            @block.vector
            def _(dve):
                wait = lambda m, s, j=None: dve.wait_ge(m.sem, m.at(s, j))
                credit(dve, t_out, w1_out, w2_out, h_out, y_out)

                def low_rows(s, qs):
                    c = s[1] % TURN
                    for q in qs:
                        tiles = GROUPS[q]
                        width = sum(TILES[i][1] for i in tiles)
                        first = TILES[tiles[0]][0]
                        wait(t_high, s, 2 * q + 2)
                        for b in range(NB):
                            of = slice(first, first + width)
                            nc.vector.tensor_tensor(xT[:, c, 1, b, of], ps_t[:, q % 2, b * width:(b + 1) * width],
                                                    xT[:, c, 0, b, of], ALU.subtract).then_inc(t_out.sem, 1)

                def low_weights(s, W, Ws, high, out_):
                    c = s[1] % TURN
                    wait(high, s)
                    nc.vector.tensor_tensor(Ws[:, c, 1], W[:, c], Ws[:, c, 0], ALU.subtract).then_inc(out_.sem, 1)

                def result(s, i):
                    c, r = s[1], TILES[i][1]
                    wait(y_ready, s, i + 1)
                    nc.vector.tensor_tensor(y[0:r, c, i, :], ps_y[0:r, i % 2, 0:D], b2[0:r, c, :], ALU.add).then_inc(y_out.sem, 1)

                def step(s, nxt):
                    for m in range(FB):
                        wait(h_high, s, m + 1)
                        nc.vector.tensor_tensor(hids[:, 1, m, :], hid[:, m % 2, :], hids[:, 0, m, :], ALU.subtract
                                                ).then_inc(h_out.sem, 1)
                    if nxt:
                        low_rows(nxt, (0, 1))
                    dve.wait_ge(y_stored[s[1]], s[0] * 32 + 32)
                    result(s, 0)
                    if nxt:
                        low_rows(nxt, (2,))
                        low_weights(nxt, W1, W1s, w1_high, w1_out)
                    result(s, 1)
                    result(s, 2)
                    if nxt:
                        low_weights(nxt, W2, W2s, w2_high, w2_out)
                    result(s, 3)
                    result(s, 4)

                low_weights((0, 0), W1, W1s, w1_high, w1_out)
                low_weights((0, 0), W2, W2s, w2_high, w2_out)
                low_rows((0, 0), range(len(GROUPS)))
                turns(nc.vector, step)


def expert_arrays(a):
    import numpy as np

    F = "L0_ffn_"
    E, TT = 8, CHUNKS * NT
    valid = np.array([[p < r for _, r in TILES] for p in range(P)])
    carry = np.ones((P, E, NT), np.float32)
    carry[:, :, 0] = 0
    return {
        "iota8": np.broadcast_to(np.arange(E, dtype=np.float32), (P, E)),
        "absent": np.broadcast_to(np.where(valid, 0, 99).astype(np.float32)[:, :, None], (P, NT, 2)),
        "carry": carry,
        "spare": (2 * N + np.arange(2)[None, :, None] * TT * P + np.arange(NT)[None, None, :] * P
                  + np.arange(P)[:, None, None]).astype(np.float32),
        "upto": np.triu(np.ones((P, P))).astype(mybir.dt.np(BF16)),
        "onesb": np.ones((P, P)).astype(mybir.dt.np(BF16)),
        "W1": a[F + "W1"].reshape(E, NB, P, FF).transpose(0, 2, 1, 3).reshape(E, P, -1),
        "W2": a[F + "W2"].reshape(E, FB, P, D).transpose(0, 2, 1, 3).reshape(E, P, -1),
        "b1": a[F + "b1"].reshape(E, FB, P).transpose(0, 2, 1),
        "b2": np.broadcast_to(a[F + "b2"][:, None, :], (E, P, D)),
    }




def kernel(**inputs):
    import numpy as np
    import concourse.bacc as bacc
    from concourse.bass_utils import run_bass_kernel_spmd

    a = {k: np.asarray(v) for k, v in inputs.items()}

    def blocks(v):
        v = v.reshape(*v.shape[:-1], v.shape[-1] // P, P)
        return np.moveaxis(v, -1, 0)

    def rows_first(w):
        L, k, m = w.shape
        return w.reshape(L, k // P, P, m).transpose(0, 2, 1, 3).reshape(L, P, -1)

    x = a["x"].reshape(IMAGES, 3, 6, 16, 6, 16).transpose(0, 2, 4, 3, 5, 1).reshape(CHUNKS, CT, PATCH)
    tr = lambda w: w.transpose(0, 2, 1)
    A = "L0_attn_"
    laid = {
        "patches": x,
        "patchesT": x.reshape(CHUNKS, CT, KP, P).transpose(0, 3, 2, 1),
        "W_mlp": a["L0_tok_W_mlp"].reshape(KP, P, D).transpose(1, 0, 2),
        "g1b1": np.stack([blocks(a["L0_tok_g1"]), blocks(a["L0_tok_b1"])], axis=1),
        "rows": np.broadcast_to(np.stack([a["L0_tok_b_mlp"], a["L0_tok_g2"], a["L0_tok_b2"], a[A + "ln0_w"],
                                          a[A + "ln0_b"]]), (P, 5, D)),
        "rwkv_vec": np.stack([blocks(a[A + n]) for n in ("ln1_w", "ln1_b", "tmk", "tmv", "tmr", "time_decay",
                                                         "time_first", "ln2_w", "ln2_b", "cmk", "cmr")], axis=2),
        "Wkvr": np.stack([rows_first(tr(a[A + n])) for n in ("Wk", "Wv", "Wr")], axis=2).reshape(LAYERS, P, -1),
        "Wo": rows_first(tr(a[A + "Wo"])),
        "Wck": rows_first(tr(a[A + "Wck"])),
        "Wcr": rows_first(tr(a[A + "Wcr"])),
        "Wcv": rows_first(tr(a[A + "Wcv"])),
    }
    laid.update(ffn_arrays(a, blocks))
    laid.update(expert_arrays(a))
    nc = bacc.Bacc("TRN2", target_bir_lowering=False, num_devices=1)
    arrays, t = {}, {}
    for name, v in laid.items():
        v = np.ascontiguousarray(v)
        arrays["in_" + name] = v
        t[name] = nc.dram_tensor("in_" + name, v.shape, mybir.dt.from_np(v.dtype), kind="ExternalInput").ap()
    out = nc.dram_tensor("out", (N, D), F32, kind="ExternalOutput").ap()
    bass_vit_tower(nc, t, out)
    r = run_bass_kernel_spmd(nc, [arrays], core_ids=[0])
    return r.results[0]["out"].reshape(IMAGES, T, D)
```
